# Optimizing a Trainium2 kernel written in Bass

```python
import numpy as np
import jax
import jax.numpy as jnp

def _softmax(x, axis=-1):
    return jax.nn.softmax(x, axis=axis)

def _gelu(x):
    return jax.nn.gelu(x, approximate=True)

def _silu(x):
    return jax.nn.silu(x)

def _sigmoid(x):
    return jax.nn.sigmoid(x)

def _layernorm(x, axis=-1, eps=1e-05):
    m = jnp.mean(x, axis=axis, keepdims=True)
    v = jnp.var(x, axis=axis, keepdims=True)
    return (x - m) / jnp.sqrt(v + eps)

def _scatter_add(tgt, idx, src, axis=0):
    return tgt.at[idx].add(src)

def _segment_sum(src, seg, n):
    return jax.ops.segment_sum(src, seg, n)
kernel_name = 'mk_decoder_postln_d1_seqx_r2_098e56'

def setup_inputs(seed: int=0):
    np.random.seed(seed)
    _w = jnp.asarray

    def _rec_inputs():
        import jax
        import jax.numpy as jnp
        _rk = jax.random.key(seed)
        x = 7.22e-05 + 1 * jax.random.normal(jax.random.fold_in(_rk, 1), (4, 1024, 512), jnp.float32)
        _lenS = 1024 - jax.random.randint(jax.random.fold_in(_rk, 7), (4,), 0, max(1, 1024 // 4) + 1, jnp.int32)
        _lenS2 = 1024 - jax.random.randint(jax.random.fold_in(_rk, 8), (4,), 0, max(1, 1024 // 4) + 1, jnp.int32)
        _ctx_1024P = jax.random.normal(jax.random.fold_in(_rk, 11), (4, 16, 512), jnp.float32)
        _ctx_1024c = jax.random.dirichlet(jax.random.fold_in(_rk, 511), 0.3 * jnp.ones((16,), jnp.float32), (4, 1024))
        _ctx_1024t = jnp.einsum('bsk,bkd->bsd', _ctx_1024c, _ctx_1024P)
        _ctx_1024t = _ctx_1024t * jax.lax.rsqrt(jnp.mean(jnp.square(_ctx_1024t)) + 1e-12) * 0.953939
        ctx_1024 = 4.13588e-05 + 0.999923 * (_ctx_1024t + 0.3 * jax.random.normal(jax.random.fold_in(_rk, 611), (4, 1024, 512), jnp.float32))
        _validS = jnp.arange(1024)[None, :] < _lenS[:, None]
        _validS2 = jnp.arange(1024)[None, :] < _lenS2[:, None]
        _causal = jnp.tril(jnp.ones((1024, 1024), dtype=bool))
        mask_BxSxS2_ik1 = jnp.where(jnp.broadcast_to(_validS2[:, None, :], (4, 1024, 1024)), 1, 0).astype(jnp.int32)
        return (x, ctx_1024, mask_BxSxS2_ik1)
    x, ctx_1024, mask_BxSxS2_ik1 = _rec_inputs()

    def _L0_attn_setup():
        import math
        import jax, jax.numpy as jnp
        import numpy as np
        PI = math.pi
        PHI = (1 + math.sqrt(5)) / 2
        B, T, D, H = (4, 512, 512, 16)
        DH = D // H

        def _chamber_beta_init(n_heads, layer_depth=0.5):
            lo = layer_depth * 0.5
            hi = 0.5 + layer_depth * 0.5
            frac = np.arange(n_heads) / max(n_heads - 1, 1)
            depth = lo + frac * (hi - lo)
            return (0.5 + 0.2 * (1.0 - 2.0 * depth)).astype(np.float32)
        key = jax.random.key(seed)
        ks = jax.random.split(key, 10)
        s = 0.02
        x = jax.random.normal(ks[0], (B, T, D), dtype=jnp.float32)
        Wa = jax.random.normal(ks[1], (D, H), jnp.float32) * s
        ba = jnp.zeros((H,), jnp.float32)
        We = jax.random.normal(ks[2], (D, H), jnp.float32) * s
        be = jnp.zeros((H,), jnp.float32)
        Wi = jax.random.normal(ks[3], (D, D), jnp.float32) * s
        Wo = jax.random.normal(ks[4], (D, D), jnp.float32) * s
        Wv = jax.random.normal(ks[5], (D, D), jnp.float32) * s
        Wout = jax.random.normal(ks[6], (D, D), jnp.float32) * s
        chi = jnp.ones((H,), jnp.float32)
        beta_p = jnp.asarray(_chamber_beta_init(H))
        iv_p = jnp.full((H,), 0.5, jnp.float32)
        ov_p = jnp.full((H,), 0.5, jnp.float32)
        return {'x': x, 'Wa': Wa, 'ba': ba, 'We': We, 'be': be, 'Wi': Wi, 'Wo': Wo, 'Wv': Wv, 'Wout': Wout, 'chi': chi, 'beta_p': beta_p, 'iv_p': iv_p, 'ov_p': ov_p}
    _L0_attn_all = _L0_attn_setup()
    _L0_attn_in = {k: v for k, v in _L0_attn_all.items() if k in ('Wa', 'ba', 'We', 'be', 'Wi', 'Wo', 'Wv', 'Wout', 'chi', 'beta_p', 'iv_p', 'ov_p')}
    del _L0_attn_all

    def _L0_xattn_setup():
        import jax, jax.numpy as jnp
        import numpy as np
        INPUT_DIM = 512
        HEADS = 16
        D_K = INPUT_DIM // HEADS
        B, S = (4, 1024)
        key = jax.random.key(seed)
        ks = jax.random.split(key, 12)
        scale = 1.0 / np.sqrt(INPUT_DIM)
        inp = {'q': jax.random.normal(ks[0], (B, S, INPUT_DIM), jnp.float32), 'k': jax.random.normal(ks[1], (B, S, INPUT_DIM), jnp.float32), 'v': jax.random.normal(ks[2], (B, S, INPUT_DIM), jnp.float32), 'mask': jax.random.randint(ks[3], (B, S, S), 0, 2, jnp.int32), 'Wq': jax.random.normal(ks[4], (INPUT_DIM, INPUT_DIM), jnp.float32) * scale, 'bq': jnp.zeros((INPUT_DIM,), jnp.float32), 'Wk': jax.random.normal(ks[5], (INPUT_DIM, INPUT_DIM), jnp.float32) * scale, 'bk': jnp.zeros((INPUT_DIM,), jnp.float32), 'Wv': jax.random.normal(ks[6], (INPUT_DIM, INPUT_DIM), jnp.float32) * scale, 'bv': jnp.zeros((INPUT_DIM,), jnp.float32), 'Wo': jax.random.normal(ks[7], (INPUT_DIM, INPUT_DIM), jnp.float32) * scale, 'bo': jnp.zeros((INPUT_DIM,), jnp.float32)}
        return inp
    _L0_xattn_all = _L0_xattn_setup()
    _L0_xattn_in = {k: v for k, v in _L0_xattn_all.items() if k in ('Wq', 'bq', 'Wk', 'bk', 'Wv', 'bv', 'Wo', 'bo')}
    del _L0_xattn_all

    def _L0_ffn_setup():
        import jax, jax.numpy as jnp
        import numpy as np
        HIDDEN = 512
        HEAD_DIM = 64
        N_EXPERTS = 16
        MIN_EXPERTS = 2
        B, T = (4, 1024)

        def _normalize(x, axis):
            n = jnp.sqrt(jnp.sum(x * x, axis=axis, keepdims=True))
            return x / jnp.maximum(n, 1e-12)

        def _ste(x):
            hard = jax.lax.stop_gradient((x > 0).astype(x.dtype))
            return hard + x - jax.lax.stop_gradient(x)

        def _gating(hidden_states, sim_matrix, gates):
            b, t, c = hidden_states.shape
            flat = hidden_states.reshape(b * t, c)
            logits = _normalize(flat, -1) @ _normalize(sim_matrix, 0) - jax.nn.sigmoid(gates)
            gated = jax.nn.relu(logits)
            mask = _ste(gated)
            inactive = jnp.sum(mask, axis=1) == 0
            _, fb_idx = jax.lax.top_k(logits, MIN_EXPERTS)
            fb = jnp.zeros_like(mask).at[jnp.arange(b * t)[:, None], fb_idx].set(1.0)
            fb_applied = inactive[:, None] & (fb > 0)
            mask = jnp.where(fb_applied, 1.0, mask)
            masked_logits = jnp.where(mask > 0, gated, -jnp.inf)
            return jax.nn.softmax(masked_logits, axis=-1).reshape(b, t, -1)
        key = jax.random.key(seed)
        ks = jax.random.split(key, 6)
        xav_qkv = float(np.sqrt(6.0 / (HIDDEN + HEAD_DIM)))
        return {'hidden_states': jax.random.normal(ks[0], (B, T, HIDDEN), dtype=jnp.float32), 'sim_matrix': jax.random.normal(ks[1], (HIDDEN, N_EXPERTS), dtype=jnp.float32), 'gates': jnp.zeros((N_EXPERTS,), dtype=jnp.float32), 'q_proj': jax.random.uniform(ks[2], (N_EXPERTS, HIDDEN, HEAD_DIM), jnp.float32, -xav_qkv, xav_qkv), 'k_proj': jax.random.uniform(ks[3], (N_EXPERTS, HIDDEN, HEAD_DIM), jnp.float32, -xav_qkv, xav_qkv), 'v_proj': jax.random.uniform(ks[4], (N_EXPERTS, HIDDEN, HEAD_DIM), jnp.float32, -xav_qkv, xav_qkv), 'o_proj': jax.random.uniform(ks[5], (N_EXPERTS, HEAD_DIM, HIDDEN), jnp.float32, -xav_qkv, xav_qkv)}
    _L0_ffn_all = _L0_ffn_setup()
    _L0_ffn_in = {k: v for k, v in _L0_ffn_all.items() if k in ('sim_matrix', 'gates', 'q_proj', 'k_proj', 'v_proj', 'o_proj')}
    del _L0_ffn_all
    return {'x': x, 'ctx_1024': ctx_1024, 'mask_BxSxS2_ik1': mask_BxSxS2_ik1, 'L0_attn_Wa': _L0_attn_in['Wa'], 'L0_attn_ba': _L0_attn_in['ba'], 'L0_attn_We': _L0_attn_in['We'], 'L0_attn_be': _L0_attn_in['be'], 'L0_attn_Wi': _L0_attn_in['Wi'], 'L0_attn_Wo': _L0_attn_in['Wo'], 'L0_attn_Wv': _L0_attn_in['Wv'], 'L0_attn_Wout': _L0_attn_in['Wout'], 'L0_attn_chi': _L0_attn_in['chi'], 'L0_attn_beta_p': _L0_attn_in['beta_p'], 'L0_attn_iv_p': _L0_attn_in['iv_p'], 'L0_attn_ov_p': _L0_attn_in['ov_p'], 'L0_xattn_Wq': _L0_xattn_in['Wq'], 'L0_xattn_bq': _L0_xattn_in['bq'], 'L0_xattn_Wk': _L0_xattn_in['Wk'], 'L0_xattn_bk': _L0_xattn_in['bk'], 'L0_xattn_Wv': _L0_xattn_in['Wv'], 'L0_xattn_bv': _L0_xattn_in['bv'], 'L0_xattn_Wo': _L0_xattn_in['Wo'], 'L0_xattn_bo': _L0_xattn_in['bo'], 'L0_ffn_sim_matrix': _L0_ffn_in['sim_matrix'], 'L0_ffn_gates': _L0_ffn_in['gates'], 'L0_ffn_q_proj': _L0_ffn_in['q_proj'], 'L0_ffn_k_proj': _L0_ffn_in['k_proj'], 'L0_ffn_v_proj': _L0_ffn_in['v_proj'], 'L0_ffn_o_proj': _L0_ffn_in['o_proj']}

def reference(x, ctx_1024, mask_BxSxS2_ik1, L0_attn_Wa, L0_attn_ba, L0_attn_We, L0_attn_be, L0_attn_Wi, L0_attn_Wo, L0_attn_Wv, L0_attn_Wout, L0_attn_chi, L0_attn_beta_p, L0_attn_iv_p, L0_attn_ov_p, L0_xattn_Wq, L0_xattn_bq, L0_xattn_Wk, L0_xattn_bk, L0_xattn_Wv, L0_xattn_bv, L0_xattn_Wo, L0_xattn_bo, L0_ffn_sim_matrix, L0_ffn_gates, L0_ffn_q_proj, L0_ffn_k_proj, L0_ffn_v_proj, L0_ffn_o_proj):
    import jax
    import jax.numpy as jnp

    def _L0_attn_ref(x, Wa, ba, We, be, Wi, Wo, Wv, Wout, chi, beta_p, iv_p, ov_p):
        import math
        import jax, jax.numpy as jnp
        import numpy as np
        PI = math.pi
        PHI = (1 + math.sqrt(5)) / 2
        B, T, D, H = (4, 512, 512, 16)
        DH = D // H

        def _chamber_beta_init(n_heads, layer_depth=0.5):
            lo = layer_depth * 0.5
            hi = 0.5 + layer_depth * 0.5
            frac = np.arange(n_heads) / max(n_heads - 1, 1)
            depth = lo + frac * (hi - lo)
            return (0.5 + 0.2 * (1.0 - 2.0 * depth)).astype(np.float32)
        Bb, Tt, Dd = x.shape
        Hh = Wa.shape[1]
        dh = Dd // Hh
        scale = math.sqrt(dh)
        aperture = jax.nn.sigmoid(x @ Wa + ba)
        expression = jax.nn.sigmoid(x @ We + be)
        inner = (x @ Wi).reshape(Bb, Tt, Hh, dh).transpose(0, 2, 1, 3)
        outer = (x @ Wo).reshape(Bb, Tt, Hh, dh).transpose(0, 2, 1, 3)
        alignment = jnp.einsum('bhqd,bhkd->bhqk', inner, outer) / scale
        attn_align = jax.nn.softmax(alignment, axis=-1)
        attn = attn_align * aperture.transpose(0, 2, 1)[..., :, None] * expression.transpose(0, 2, 1)[..., None, :]
        attn = attn / (attn.sum(axis=-1, keepdims=True) + 1e-08)
        v = (x @ Wv).reshape(Bb, Tt, Hh, dh).transpose(0, 2, 1, 3)
        converged = jnp.einsum('bhqk,bhkd->bhqd', attn, v)
        beta = jax.nn.sigmoid(beta_p)[None, :, None, None]
        iv = jax.nn.sigmoid(iv_p)[None, :, None, None]
        ov = jax.nn.sigmoid(ov_p)[None, :, None, None]
        angle = PI * beta
        ca, sa = (jnp.cos(angle), jnp.sin(angle))
        x_in = converged * iv
        half = dh // 2
        xr, xi = (x_in[..., :half], x_in[..., half:])
        chambered = jnp.concatenate([xr * ca - xi * sa, xr * sa + xi * ca], axis=-1) * ov
        rotated = chambered * jnp.tanh(chi)[None, :, None, None]
        combined = rotated.transpose(0, 2, 1, 3).reshape(Bb, Tt, Dd)
        return combined @ Wout

    def _L0_xattn_ref(q, k, v, mask, Wq, bq, Wk, bk, Wv, bv, Wo, bo):
        import jax, jax.numpy as jnp
        import numpy as np
        INPUT_DIM = 512
        HEADS = 16
        D_K = INPUT_DIM // HEADS
        B, S = (4, 1024)
        bs = q.shape[0]

        def proj(x, W, b):
            return (x @ W.T + b).reshape(bs, -1, HEADS, D_K).transpose(0, 2, 1, 3)
        qh, kh, vh = (proj(q, Wq, bq), proj(k, Wk, bk), proj(v, Wv, bv))
        scores = jnp.einsum('bhqd,bhkd->bhqk', qh, kh) / jnp.sqrt(jnp.float32(D_K))
        scores = jnp.where(mask[:, None] == 0, jnp.float32(-1000000000.0), scores)
        attn = jax.nn.softmax(scores, axis=-1)
        ctx = jnp.einsum('bhqk,bhkd->bhqd', attn, vh)
        concat = ctx.transpose(0, 2, 1, 3).reshape(bs, -1, INPUT_DIM)
        return concat @ Wo.T + bo

    def _L0_ffn_ref(hidden_states, sim_matrix, gates, q_proj, k_proj, v_proj, o_proj):
        import jax, jax.numpy as jnp
        import numpy as np
        HIDDEN = 512
        HEAD_DIM = 64
        N_EXPERTS = 16
        MIN_EXPERTS = 2
        B, T = (4, 1024)

        def _normalize(x, axis):
            n = jnp.sqrt(jnp.sum(x * x, axis=axis, keepdims=True))
            return x / jnp.maximum(n, 1e-12)

        def _ste(x):
            hard = jax.lax.stop_gradient((x > 0).astype(x.dtype))
            return hard + x - jax.lax.stop_gradient(x)

        def _gating(hidden_states, sim_matrix, gates):
            b, t, c = hidden_states.shape
            flat = hidden_states.reshape(b * t, c)
            logits = _normalize(flat, -1) @ _normalize(sim_matrix, 0) - jax.nn.sigmoid(gates)
            gated = jax.nn.relu(logits)
            mask = _ste(gated)
            inactive = jnp.sum(mask, axis=1) == 0
            _, fb_idx = jax.lax.top_k(logits, MIN_EXPERTS)
            fb = jnp.zeros_like(mask).at[jnp.arange(b * t)[:, None], fb_idx].set(1.0)
            fb_applied = inactive[:, None] & (fb > 0)
            mask = jnp.where(fb_applied, 1.0, mask)
            masked_logits = jnp.where(mask > 0, gated, -jnp.inf)
            return jax.nn.softmax(masked_logits, axis=-1).reshape(b, t, -1)
        b, t, c = hidden_states.shape
        rw = _gating(hidden_states, sim_matrix, gates)
        q = jnp.einsum('bte,bted->btd', rw, jnp.einsum('btc,ecd->bted', hidden_states, q_proj))
        k = jnp.einsum('bte,bted->btd', rw, jnp.einsum('btc,ecd->bted', hidden_states, k_proj))
        v = jnp.einsum('bte,bted->btd', rw, jnp.einsum('btc,ecd->bted', hidden_states, v_proj))
        scale = 1.0 / jnp.sqrt(jnp.asarray(HEAD_DIM, dtype=q.dtype))
        scores = jnp.einsum('bqd,bkd->bqk', q, k) * scale
        causal = jnp.tril(jnp.ones((t, t), dtype=bool))
        scores = jnp.where(causal, scores, -jnp.inf)
        attn = jnp.einsum('bqk,bkd->bqd', jax.nn.softmax(scores, axis=-1), v)
        mixed = attn[:, :, None, :] * rw[..., None]
        return jnp.einsum('bted,edc->btc', mixed, o_proj)
    x = _layernorm(x + _L0_attn_ref(x, L0_attn_Wa, L0_attn_ba, L0_attn_We, L0_attn_be, L0_attn_Wi, L0_attn_Wo, L0_attn_Wv, L0_attn_Wout, L0_attn_chi, L0_attn_beta_p, L0_attn_iv_p, L0_attn_ov_p), axis=-1)
    x = _layernorm(x + _L0_xattn_ref(x, ctx_1024, ctx_1024, mask_BxSxS2_ik1, L0_xattn_Wq, L0_xattn_bq, L0_xattn_Wk, L0_xattn_bk, L0_xattn_Wv, L0_xattn_bv, L0_xattn_Wo, L0_xattn_bo), axis=-1)
    x = _layernorm(x + _L0_ffn_ref(x, L0_ffn_sim_matrix, L0_ffn_gates, L0_ffn_q_proj, L0_ffn_k_proj, L0_ffn_v_proj, L0_ffn_o_proj), axis=-1)
    return x

_drawn_inputs = setup_inputs


def setup_inputs(seed=0):
    import zlib

    import numpy as np

    out = dict(_drawn_inputs(seed))
    spreads = {'L0_attn_ba': (0.0, 2.0),
     'L0_attn_be': (0.0, 0.8),
     'L0_attn_chi': (1.0, 0.6),
     'L0_attn_iv_p': (0.5, 0.6),
     'L0_attn_ov_p': (0.5, 0.6),
     'L0_xattn_bq': (0.0, 0.335),
     'L0_xattn_bk': (0.0, 2.0),
     'L0_xattn_bv': (0.0, 0.1),
     'L0_xattn_bo': (0.0, 0.1),
     'L0_ffn_gates': (0.0, 0.1)}
    factors = {'L0_attn_Wa': 64.0,
     'L0_attn_We': 8.0,
     'L0_attn_Wi': 8.0,
     'L0_attn_Wo': 8.0,
     'L0_attn_Wv': 7.736,
     'L0_attn_Wout': 8.0,
     'L0_attn_beta_p': 8.0}
    for name, (base, spread) in spreads.items():
        noise = np.random.default_rng([zlib.crc32(name.encode()), seed]).standard_normal(out[name].shape)
        drawn = base * np.exp(spread * noise) if base else spread * noise
        out[name] = jnp.asarray(drawn.astype(out[name].dtype))
    for name, factor in factors.items():
        out[name] = (out[name] * factor).astype(out[name].dtype)
    return out
```

```python
import math
from contextlib import ExitStack

import concourse.bass as bass
from concourse import mybir

P = 128
B, S, D, H = 4, 1024, 512, 16
DH = D // H
KT = D // P
TT = S // P
CH = 512
NC_ = S // CH
PAIRS = H // 2
VW = DH + 2
EPS = 1e-5
SCALE = DH ** -0.5
MASKED = -57344.0 * 16384.0
ABSENT = -1e8
SLOTS = 3
PRING = 4

ALU = mybir.AluOpType
ACT = mybir.ActivationFunctionType
AX = mybir.AxisListType
F32 = mybir.dt.float32
F32R = mybir.dt.float32r
BF16 = mybir.dt.bfloat16
FP8 = mybir.dt.float8e5
I32 = mybir.dt.int32


def attention_steps(masked):
    smax = lambda p: [("smax", p, h, t, c) for h in range(2) for t in range(TT) for c in range(NC_)]
    steps = [("Q", g, c) for g in range(KT) for c in range(NC_)]
    steps += [("K", 0, c) for c in range(NC_)]
    rest = [] if masked else [("EX",)] + [("AP", c) for c in range(NC_)]
    rest += [("K", g, c) for g in range(1, KT) for c in range(NC_)] + [("V", t) for t in range(TT)]
    first = smax(0)
    lead = 6
    every = -(-len(first) // (len(rest) - lead))
    for n, step in enumerate(rest):
        steps.append(step)
        if n >= lead:
            steps += first[:every]
            first = first[every:]
    steps += first
    if masked:
        steps.append(("CS",))
    steps.append(("mneg", 0))
    for p in range(PAIRS):
        extra = [[] for _ in range(TT)]
        if p == 0:
            ahead = smax(1) + smax(2)
            for kt in range(TT):
                extra[kt] += ahead[8 * kt:8 * kt + 8]
            extra[5].append(("mneg", 1))
        else:
            extra[1] += [("den", p - 1, c) for c in range(NC_)]
            if 2 <= p + 1 < PAIRS:
                extra[2].append(("mneg", p + 1))
            if p + 2 < PAIRS:
                ahead = smax(p + 2)
                for kt in range(1, TT):
                    extra[kt] += ahead[5 * (kt - 1):5 * kt]
        if masked:
            if p == 2:
                extra[3].append(("RZ",))
        else:
            extra[6] += [("apx", p, c) for c in range(NC_)]
        for kt in range(TT):
            steps.append(("st", p, kt))
            steps += extra[kt]
        steps.append(("tail", p))
    steps += [("den", PAIRS - 1, c) for c in range(NC_)]
    steps += [("out", t) for t in range(TT)]
    steps += [("xt", t) for t in range(TT)]
    if sum(s[0] not in ("st", "tail") for s in steps) % 2:
        steps.append(("pad",))
    return steps


def attention(nc, masked, io):
    steps = attention_steps(masked)
    uses = [s for s in steps if s[0] not in ("st", "tail")]
    PER = len(uses) // 2
    use_no = {s: n for n, s in enumerate(uses)}
    pair_slots = [[p for p in range(PAIRS) if p % SLOTS == s] for s in range(SLOTS)]

    ctx = ExitStack()
    with ctx:
        used = [0]
        base = nc.sbuf_base
        size = nc.sbuf_bytes_remaining // 64 * 64
        ctx.enter_context(nc.sbuf_tensor(f"arena{int(masked)}", [P, size], mybir.dt.uint8))
        start = -(-base // 64) * 64
        wide = {F32: 4, F32R: 4, BF16: 2, FP8: 1, I32: 4}

        def sb(name, shape, dt=F32, at=None):
            n = wide[dt]
            for k in shape[1:]:
                n *= k
            if at is None:
                at = start + used[0]
                used[0] += -(-n // 64) * 64
                assert used[0] + 64 <= size, (name, used[0], size)
            t = nc.alloc_sbuf_tensor_at(f"{name}_{int(masked)}", shape, dt, offset=at)
            place[name] = at
            return t

        place = {}
        sem = lambda n: ctx.enter_context(nc.semaphore(f"{n}_{int(masked)}"))

        stack = sb("stack", [P, SLOTS, 4, S], F32R)
        x_hi = stack[:, 1, :, :]
        x_lo = stack[:, 2, :, :]
        q_raw = sb("q_raw", [P, KT, S])
        k_raw = sb("k_raw", [P, KT, S])
        y = k_raw[:, :, :].rearrange("p g (a d) -> p (g a) d", d=D)
        qk = sb("qk", [P, 4, S], F32R)
        v_ext = sb("v_ext", [P, TT, H, VW])
        w0 = sb("w0", [P, 2, KT, D], F32R)
        probs = sb("probs", [P, PRING, S])
        w1 = sb("w1", [P, 2, KT, D], F32R, at=place["probs"])
        stage = sb("stage", [P, 2, S])
        u = sb("u", [P, NC_, CH])
        r = sb("r", [P, CH])
        eye = sb("eye", [P, P])
        neg_eye = sb("neg_eye", [P, P])
        sel_den = sb("sel_den", [P, P])
        mx = sb("mx", [P, 2, 2 * TT * NC_])
        mm = sb("mm", [P, 2 * TT])
        mrow = sb("mrow", [2 * TT, P], F32R)
        stats = sb("stats", [P, 6])
        mv = sb("mv", [P, TT, 2])
        sd = sb("sd", [P, TT])
        rstd = sb("rstd", [P, TT])
        tmp = sb("tmp", [P, TT])
        xts = sb("xts", [P, 2, KT, P], at=place["u"])
        if masked:
            mask_q = sb("mask_q", [P, TT, S], BF16)
            mask_k = sb("mask_k", [P, TT, S], FP8)
            mstage = sb("mstage", [P, 2, CH], I32)
            eye8 = sb("eye8", [P, P], FP8)
            bq = sb("bq", [P, KT])
            bk = sb("bk", [P, KT])
            bv = sb("bv", [P, D])
            bo = sb("bo", [P, D])
            ones = sb("ones", [P, 1])
            none = sb("none", [P, TT])
            vmean = sb("vmean", [P, KT])
            vm = sb("vm", [P, 2, KT, P], F32R)
            rz = sb("rz", [P, D])
        else:
            apx = sb("apx", [P, NC_, CH])
            wsm_raw = sb("wsm_raw", [P, KT, 2 * H])
            wsm = sb("wsm", [P, 2, KT, 2 * H], F32R)
            bsm = sb("bsm", [P, 2 * H])
            gate = sb("gate", [P, TT, 2 * H])
            ap_t = sb("ap_t", [H + 1, S])
            sel_ap = sb("sel_ap", [H + 1, PAIRS, P])
            turn_in = sb("turn_in", [P, 4, KT])
            turn = sb("turn", [P, 8, KT])
            sign = sb("sign", [P, 1])
            half_pi = sb("half_pi", [P, 1])

        psum = lambda n, shape: ctx.enter_context(nc.psum_tensor(f"{n}_{int(masked)}", shape, F32))
        work = [psum(f"work{b}", [P, CH]) for b in range(2)]
        scores = [psum(f"scores{b}", [P, S]) for b in range(2)]
        acc = psum("acc", [P, NC_, CH])

        const_in = sem("const_in")
        turn_sem = sem("turn_sem")
        setup = sem("setup")
        apart = sem("apart")
        work_full = [sem(f"work_full{b}") for b in range(2)]
        work_free = [sem(f"work_free{b}") for b in range(2)]
        stage_full = [sem(f"stage_full{b}") for b in range(2)]
        stage_free = sem("stage_free")
        chunk_ready = sem("chunk_ready")
        proj_done = sem("proj_done")
        group_split = sem("group_split")
        ones_set = sem("ones_set")
        stacked = [sem(f"stacked{s}") for s in range(SLOTS)]
        mrow_ready = sem("mrow_ready")
        mrow_in = [sem(f"mrow_in{s}") for s in range(SLOTS)]
        st_full = sem("st_full")
        p_full = sem("p_full")
        pv_done = sem("pv_done")
        u_ready = sem("u_ready")
        ctx_done = sem("ctx_done")
        mm_ready = sem("mm_ready")
        res_in = sem("res_in")
        res_ready = sem("res_ready")
        ct_split = sem("ct_split")
        out_done = sem("out_done")
        y_done = sem("y_done")
        var_ready = sem("var_ready")
        sd_ready = sem("sd_ready")
        x_ready = sem("x_ready")
        stored = sem("stored")
        xt_ready = sem("xt_ready")
        xt_stored = [sem(f"xt_stored{b}") for b in range(2)]
        if masked:
            mstage_full = [sem(f"mstage_full{b}") for b in range(2)]
            mstage_free = sem("mstage_free")
            maskq_ready = sem("maskq_ready")
            maskk_ready = sem("maskk_ready")
            vm_ready = sem("vm_ready")
            rz_ready = sem("rz_ready")
            bo_added = sem("bo_added")
        else:
            gate_sum = sem("gate_sum")
            gate_exp = sem("gate_exp")
            gate_ready = sem("gate_ready")
            ap_ready = sem("ap_ready")
            apx_ready = sem("apx_ready")

        chunks = [("wq", 0), ("wq", 1)] + [("x", k) for k in range(KT)] + [("wk", 0), ("wk", 1)]
        if masked:
            chunks += [("x2", k) for k in range(KT)]
        before_group0 = len(chunks)
        chunks += [("wv", 0), ("wv", 1), ("wo", 0), ("wo", 1)]
        NCH = len(chunks)
        chunk_no = {c: n for n, c in enumerate(chunks)}
        upto = lambda what: max(n for n, c in enumerate(chunks) if c[0] == what) + 1
        projections = ("wq", "wk", "wv", "wo")

        def chunk_parts(what, k):
            if what in ("x", "x2"):
                return x_hi[:, k, :], x_lo[:, k, :]
            w = w1 if what == "wk" else w0
            half = lambda part: w[:, part, 2 * k:2 * k + 2, :].rearrange("p k n -> p (k n)")
            return half(0), half(1)

        def wait_full(eng, i, step):
            n = use_no[step]
            eng.wait_ge(work_full[n % 2], i * PER + n // 2 + 1)
            return work[n % 2], work_free[n % 2]

        def alone(eng):
            eng.sem_inc(apart, 1)

        block = ctx.enter_context(nc.Block(f"layer{int(masked)}"))

        @block.sync
        def _(sp):
            consts = [(eye, io["eye"]), (neg_eye, io["neg_eye"]), (sel_den, io["sel_den"])]
            for t, src in consts:
                sp.dma_start(t[:, :], src).then_inc(const_in, 16)
            if masked:
                sp.dma_start(bq[:, :], io["bq"].rearrange("(g p) -> p g", p=P),
                             allow_slow_non_contiguous=True).then_inc(const_in, 16)
                sp.dma_start(bk[:, :], io["bk"].rearrange("(g p) -> p g", p=P),
                             allow_slow_non_contiguous=True).then_inc(const_in, 16)
                sp.dma_start(bv[:, :], io["bv"].partition_broadcast(P)).then_inc(const_in, 16)
                sp.dma_start(bo[:, :], io["bo"].partition_broadcast(P)).then_inc(const_in, 16)
            else:
                sp.dma_start(sel_ap[:, :, :], io["sel_ap"]).then_inc(const_in, 16)
                sp.dma_start(wsm_raw[:, :, 0:H], io["wa"].rearrange("(k p) h -> p k h", p=P)).then_inc(const_in, 16)
                sp.dma_start(wsm_raw[:, :, H:2 * H], io["we"].rearrange("(k p) h -> p k h", p=P)).then_inc(const_in, 16)
                sp.dma_start(bsm[:, 0:H], io["ba"].partition_broadcast(P)).then_inc(const_in, 16)
                sp.dma_start(bsm[:, H:2 * H], io["be"].partition_broadcast(P)).then_inc(const_in, 16)
                for n, src in enumerate((io["wo"], io["wo_swapped"])):
                    sp.dma_start(q_raw[:, 2 * n:2 * n + 2, :].rearrange("p g (a d) -> p (g a) d", d=D),
                                 src.rearrange("(k p) d -> p k d", p=P)).then_inc(const_in, 16)
                for n, name in enumerate(("beta", "iv", "ov", "chi")):
                    for q in range(4):
                        sp.dma_start(turn_in[DH * q:DH * (q + 1), n, :],
                                     io[name].rearrange("(k q) -> q k", q=4)[q, :].partition_broadcast(DH),
                                     allow_slow_non_contiguous=True).then_inc(const_in, 16)
                sp.dma_start(sign[:, :], io["sign"]).then_inc(const_in, 16)
                sp.wait_ge(turn_sem, 5)
                sp.dma_start(io["wo_turned"].rearrange("(k p) d -> p k d", p=P), y[:, 0:KT, :])\
                  .then_inc(turn_sem, 16)
                sp.wait_ge(turn_sem, 21)
            sp.wait_ge(setup, 3)
            with sp.Fori(0, B) as i:
                def load_chunk(n):
                    what, k = chunks[n]
                    sp.wait_ge(stage_free, 1 + i * NCH + max(n - 1, 0))
                    alone(sp)
                    if what in ("x", "x2"):
                        src = io["q_src"] if what == "x" else io["kv_src"]
                        src = src[bass.ds(i, 1), k * P:(k + 1) * P, :].rearrange("b p s -> (b p) s")
                        dst = stage[:, n % 2, :]
                    else:
                        name = "wo_turned" if what == "wo" and not masked else what
                        src = io[name][2 * k * P:(2 * k + 2) * P, :].rearrange("(k p) n -> p k n", p=P)
                        dst = stage[:, n % 2, :].rearrange("p (k n) -> p k n", k=2)
                    sp.dma_start(dst, src).then_inc(stage_full[n % 2], 16)

                def load_masks(src, n0):
                    for t in range(TT):
                        for c in range(NC_):
                            n = n0 + NC_ * t + c
                            sp.wait_ge(mstage_free, 1 + i * 2 * NC_ * TT + max(n - 1, 0))
                            alone(sp)
                            sp.dma_start(mstage[:, n % 2, :],
                                         src[bass.ds(i, 1), t * P:(t + 1) * P, c * CH:(c + 1) * CH]
                                         .rearrange("b p s -> (b p) s")).then_inc(mstage_full[n % 2], 16)

                def stack_pair(p):
                    s = p % SLOTS
                    sp.wait_ge(group_split, i * KT + p // 2 + 1)
                    alone(sp)
                    if p >= SLOTS:
                        sp.wait_ge(st_full, 1 + i * H * TT + 2 * TT * (p - SLOTS + 1))
                    elif p > 0:
                        sp.wait_ge(proj_done, 1 + i * 4 + 3)
                    alone(sp)
                    for h in range(2):
                        a = DH * ((2 * p + h) % 4)
                        for j, part in enumerate((0, 1, 0)):
                            sp.dma_start(stack[DH * j:DH * (j + 1), s, h, :].bitcast(F32),
                                         qk[a:a + DH, part, :].bitcast(F32)).then_inc(stacked[s], 16)
                        for j, part in enumerate((2, 2, 3)):
                            sp.dma_start(stack[DH * j:DH * (j + 1), s, 2 + h, :].bitcast(F32),
                                         qk[a:a + DH, part, :].bitcast(F32)).then_inc(stacked[s], 16)

                def max_row(p):
                    sp.wait_ge(mrow_ready, i * PAIRS + p + 1)
                    alone(sp)
                    sp.dma_start(stack[3 * DH:3 * DH + 1, p % SLOTS, 0:2, :].bitcast(F32),
                                 mrow[:, :].bitcast(F32)).then_inc(mrow_in[p % SLOTS], 16)

                for n in range(chunk_no[("wk", 0)]):
                    load_chunk(n)
                if masked:
                    load_masks(io["mask_q"], 0)
                for n in range(chunk_no[("wk", 0)], before_group0):
                    load_chunk(n)
                stack_pair(0)
                for n in range(before_group0, NCH - 2):
                    load_chunk(n)
                if masked:
                    load_masks(io["mask_k"], NC_ * TT)
                stack_pair(1)
                for n in range(NCH - 2, NCH):
                    load_chunk(n)
                stack_pair(2)
                max_row(0)
                max_row(1)
                for p in range(1, PAIRS):
                    if p + 2 < PAIRS and p > 0:
                        stack_pair(p + 2)
                    if p + 1 < PAIRS and p > 0:
                        max_row(p + 1)
                    if p == 5:
                        sp.wait_ge(group_split, i * KT + KT)
                        alone(sp)
                        sp.dma_start(y, io["res"][bass.ds(i, 1), :, :].rearrange("b (t p) d -> p (b t) d", p=P))\
                          .then_inc(res_in, 16)

        @block.gpsimd
        def _(pool):
            def split(raw, hi, lo):
                pool.tensor_scalar(hi, raw, 1.0, 0.0, ALU.mult, ALU.add)
                pool.drain()
                return pool.tensor_tensor(lo, raw, hi.bitcast(F32), ALU.subtract)

            pool.memset(stack[3 * DH:3 * DH + 1, 0, 2:4, :].bitcast(F32), 1.0)
            pool.drain()
            if not masked:
                pool.wait_ge(const_in, 16 * 27)
                split(wsm_raw[:, :, :], wsm[:, 0, :, :], wsm[:, 1, :, :])
                pool.drain()
            for count in (*work_free, stage_free, ct_split, stored, proj_done, pv_done, st_full, out_done, u_ready,
                          *xt_stored, *([mstage_free] if masked else [])):
                pool.sem_inc(count, 1)
            pool.drain().then_inc(setup, 1)
            with pool.Fori(0, B) as i:
                def split_chunk(n):
                    what, k = chunks[n]
                    hi, lo = chunk_parts(what, k)
                    if what == "x" and k == 0:
                        pool.wait_ge(st_full, 1 + i * H * TT)
                    if what == "x2" and k == 0:
                        pool.wait_ge(proj_done, 1 + i * 4 + 1)
                    if what == "wq" and k == 0:
                        pool.wait_ge(proj_done, 1 + i * 4)
                    if what == "wk" and k == 0:
                        pool.wait_ge(pv_done, 1 + i * PAIRS * TT)
                    if what == "wv" and k == 0:
                        pool.wait_ge(proj_done, 1 + i * 4 + 1)
                    if what == "wo" and k == 0:
                        pool.wait_ge(proj_done, 1 + i * 4 + 3)
                    nth = [m for m in range(NCH) if m % 2 == n % 2].index(n) + 1
                    pool.wait_ge(stage_full[n % 2], (i * (NCH // 2) + nth) * 16)
                    alone(pool)
                    split(stage[:, n % 2, :], hi, lo).then_inc(stage_free, 1)
                    pool.drain()
                    pool.engine_nop().then_inc(chunk_ready, 1)

                def split_group(g):
                    if g > 0:
                        for p in (2 * g - 2, 2 * g - 1):
                            s = p % SLOTS
                            pool.wait_ge(stacked[s], (i * len(pair_slots[s]) + pair_slots[s].index(p) + 1) * 12 * 16)
                    else:
                        for step in [("Q", 0, c) for c in range(NC_)] + [("K", 0, c) for c in range(NC_)]:
                            n = use_no[step]
                            pool.wait_ge(work_free[n % 2], 1 + i * PER + n // 2 + 1)
                    if g == 1:
                        for c in range(NC_):
                            n = use_no[("K", KT - 1, c)]
                            pool.wait_ge(work_free[n % 2], 1 + i * PER + n // 2 + 1)
                    if g == 0:
                        pool.wait_ge(out_done, 1 + i * TT)
                    alone(pool)
                    split(q_raw[:, g, :], qk[:, 0, :], qk[:, 1, :])
                    pool.drain()
                    split(k_raw[:, g, :], qk[:, 2, :], qk[:, 3, :])
                    pool.drain()
                    pool.engine_nop().then_inc(group_split, 1)

                for n in range(before_group0):
                    split_chunk(n)
                split_group(0)
                for n in range(before_group0, NCH - 2):
                    split_chunk(n)
                pool.wait_ge(proj_done, 1 + i * 4 + 3)
                alone(pool)
                for s in range(1, SLOTS):
                    pool.memset(stack[3 * DH:3 * DH + 1, s, 2:4, :].bitcast(F32), 1.0)
                    pool.drain()
                pool.engine_nop().then_inc(ones_set, 1)
                split_group(1)
                for n in range(NCH - 2, NCH):
                    split_chunk(n)
                for g in range(2, KT):
                    split_group(g)
                if masked:
                    pool.wait_ge(const_in, 16 * 7)
                    pool.wait_ge(res_in, i * 16 + 16)
                    for t in range(TT):
                        pool.tensor_tensor(y[:, t, :], y[:, t, :], bo[:, :], ALU.add)
                        pool.drain()
                    pool.engine_nop().then_inc(bo_added, 1)
                for t in range(TT):
                    if t == 0:
                        for s in range(SLOTS):
                            pool.wait_ge(stacked[s], (i + 1) * len(pair_slots[s]) * 12 * 16)
                    if t % (TT // NC_) == 0:
                        pool.wait_ge(ctx_done, i * PAIRS * NC_ + (PAIRS - 1) * NC_ + t // (TT // NC_) + 1)
                    if t >= 4:
                        pool.wait_ge(out_done, 1 + i * TT + t - 3)
                    alone(pool)
                    part = lambda k: qk[:, t % 4, k * D:(k + 1) * D].rearrange("p (g n) -> p g n", g=KT)
                    split(q_raw[:, :, t * P:(t + 1) * P], part(0), part(1)).then_inc(ct_split, 1)
                    pool.drain()

        @block.tensor
        def _(pe):
            pe.wait_ge(setup, 3)
            pe.wait_ge(const_in, 16 * (7 if masked else 27))
            with pe.Fori(0, B) as i:
                def parts(out, hi_l, lo_l, hi_r, lo_r):
                    for k in range(KT):
                        for n, (a, b) in enumerate(((hi_l, hi_r), (hi_l, lo_r), (lo_l, hi_r))):
                            last = pe.matmul(out, a(k), b(k), start=(k == 0 and n == 0),
                                             stop=(k == KT - 1 and n == 2))
                    return last

                def smax_ready(p):
                    s = p % SLOTS
                    pe.wait_ge(stacked[s], (i * len(pair_slots[s]) + pair_slots[s].index(p) + 1) * 12 * 16)

                def pv(p, kt):
                    for h in range(2):
                        pe.wait_ge(p_full, i * H * TT + 2 * (p * TT + kt) + h + 1)
                    if kt == 0:
                        pe.wait_ge(u_ready, 1 + (i * PAIRS + p) * NC_)
                    for c in range(NC_):
                        for h in range(2):
                            n = 2 * (p * TT + kt) + h
                            last = pe.matmul(acc[64 * h:64 * h + VW, c, :], v_ext[:, kt, 2 * p + h, :],
                                             probs[:, n % PRING, c * CH:(c + 1) * CH],
                                             start=(kt == 0), stop=(kt == TT - 1), skip_group_check=True)
                    last.then_inc(pv_done, 1)

                for step in steps:
                    kind = step[0]
                    if kind == "st":
                        _, p, kt = step
                        s = p % SLOTS
                        if kt == 0:
                            pe.wait_ge(mrow_in[s], (i * len(pair_slots[s]) + pair_slots[s].index(p) + 1) * 16)
                            if p == 1:
                                pe.wait_ge(ones_set, i + 1)
                            if p == 0 and masked:
                                pe.wait_ge(maskk_ready, i + 1)
                        for h in range(2):
                            n = 2 * (p * TT + kt) + h
                            if n >= 2:
                                pe.wait_ge(p_full, i * H * TT + n - 1)
                            for c in range(NC_):
                                last = pe.matmul(scores[n % 2][:, c * CH:(c + 1) * CH],
                                                 stack[0:3 * DH + 1, s, 2 + h, kt * P:(kt + 1) * P],
                                                 stack[0:3 * DH + 1, s, h, c * CH:(c + 1) * CH],
                                                 start=True, stop=not masked)
                                if masked:
                                    last = pe.matmul(scores[n % 2][:, c * CH:(c + 1) * CH], eye8[:, :],
                                                     mask_k[:, kt, c * CH:(c + 1) * CH], start=False, stop=True)
                            last.then_inc(st_full, 1)
                        if kt > 0:
                            pv(p, kt - 1)
                        continue
                    if kind == "tail":
                        pv(step[1], TT - 1)
                        continue
                    n = use_no[step]
                    bank = work[n % 2]
                    pe.wait_ge(work_free[n % 2], 1 + i * PER + n // 2)
                    if kind in ("Q", "K"):
                        _, g, c = step
                        w = w0 if kind == "Q" else w1
                        if g == 0 and c == 0:
                            pe.wait_ge(chunk_ready, i * NCH + (upto("x") if kind == "Q" else
                                                               before_group0))
                        last = parts(bank[:, :], lambda k: w[:, 0, k, g * P:(g + 1) * P],
                                     lambda k: w[:, 1, k, g * P:(g + 1) * P],
                                     lambda k: x_hi[:, k, c * CH:(c + 1) * CH],
                                     lambda k: x_lo[:, k, c * CH:(c + 1) * CH])
                    elif kind == "V":
                        t = step[1]
                        if t == 0:
                            pe.wait_ge(chunk_ready, i * NCH + upto("wv"))
                        last = parts(bank[:, :], lambda k: x_hi[:, k, t * P:(t + 1) * P],
                                     lambda k: x_lo[:, k, t * P:(t + 1) * P],
                                     lambda k: w0[:, 0, k, :], lambda k: w0[:, 1, k, :])
                    elif kind == "EX":
                        for t in range(TT):
                            last = parts(bank[:, t * 2 * H:(t + 1) * 2 * H], lambda k: x_hi[:, k, t * P:(t + 1) * P],
                                         lambda k: x_lo[:, k, t * P:(t + 1) * P],
                                         lambda k: wsm[:, 0, k, :], lambda k: wsm[:, 1, k, :])
                    elif kind == "AP":
                        pe.wait_ge(gate_ready, i + 1)
                        for t in range(TT // NC_):
                            last = pe.matmul(bank[0:H, t * P:(t + 1) * P],
                                             gate[:, step[1] * (TT // NC_) + t, 0:H], eye[:, :],
                                             start=True, stop=True)
                    elif kind == "smax":
                        _, p, h, t, c = step
                        if h == 0 and t == 0 and c == 0:
                            smax_ready(p)
                        s = p % SLOTS
                        last = pe.matmul(bank[:, :], stack[0:3 * DH, s, h, t * P:(t + 1) * P],
                                         stack[0:3 * DH, s, 2 + h, c * CH:(c + 1) * CH], start=True, stop=True)
                    elif kind == "mneg":
                        pe.wait_ge(mm_ready, i * PAIRS + step[1] + 1)
                        last = pe.matmul(bank[0:2 * TT, 0:P], mm[:, :], neg_eye[:, :], start=True, stop=True)
                    elif kind == "apx":
                        _, p, c = step
                        pe.wait_ge(ap_ready, (i + 1) * NC_)
                        last = pe.matmul(bank[:, :], sel_ap[:, p, :], ap_t[:, c * CH:(c + 1) * CH],
                                         start=True, stop=True)
                    elif kind == "den":
                        _, p, c = step
                        pe.wait_ge(u_ready, 1 + (i * PAIRS + p) * NC_ + c + 1)
                        last = pe.matmul(bank[:, :], sel_den[:, :], u[:, c, :], start=True, stop=True)
                    elif kind == "CS":
                        for h in range(H):
                            a = DH * (h % 4)
                            for t in range(TT):
                                last = pe.matmul(bank[a:a + DH, h // 4:h // 4 + 1], v_ext[:, t, h, 0:DH],
                                                 ones[:, :], start=(t == 0), stop=(t == TT - 1))
                    elif kind == "RZ":
                        pe.wait_ge(vm_ready, i + 1)
                        pe.wait_ge(chunk_ready, i * NCH + upto("wo"))
                        last = parts(bank[:, :], lambda k: vm[:, 0, k, :], lambda k: vm[:, 1, k, :],
                                     lambda k: w0[:, 0, k, :], lambda k: w0[:, 1, k, :])
                    elif kind == "out":
                        t = step[1]
                        if t == 0:
                            pe.wait_ge(chunk_ready, i * NCH + upto("wo"))
                        pe.wait_ge(ct_split, 1 + i * TT + t + 1)
                        last = parts(bank[:, :], lambda k: qk[:, t % 4, k * P:(k + 1) * P],
                                     lambda k: qk[:, t % 4, D + k * P:D + (k + 1) * P],
                                     lambda k: w0[:, 0, k, :], lambda k: w0[:, 1, k, :])
                    elif kind == "xt":
                        t = step[1]
                        if t == 0:
                            pe.wait_ge(x_ready, i * TT + TT)
                        for k in range(KT):
                            last = pe.transpose(bank[:, k * P:(k + 1) * P], y[:, t, k * P:(k + 1) * P], eye[:, :])
                    elif kind == "pad":
                        last = pe.matmul(bank[0:2 * TT, 0:P], mm[:, :], neg_eye[:, :], start=True, stop=True)
                    last.then_inc(work_full[n % 2], 1)
                    if step in (("Q", KT - 1, NC_ - 1), ("K", KT - 1, NC_ - 1), ("V", TT - 1), ("out", TT - 1)):
                        pe.drain().then_inc(proj_done, 1)
                    if kind == "out":
                        pe.drain().then_inc(out_done, 1)

        @block.scalar
        def _(act):
            act.wait_ge(const_in, 16 * (7 if masked else 27))
            if not masked:
                act.wait_ge(turn_sem, 1)
                act.activation(turn[:, 0:3, :], turn_in[:, 0:3, :], ACT.Exp, scale=-1.0)
                act.activation(turn[:, 3, :], turn_in[:, 3, :], ACT.Tanh)
                act.drain().then_inc(turn_sem, 1)
                act.wait_ge(turn_sem, 3)
                act.activation(turn[:, 4, :], turn[:, 0, :], ACT.Sin, scale=math.pi)
                act.activation(turn[:, 5, :], turn[:, 0, :], ACT.Sin, scale=-math.pi, bias=half_pi[:, 0:1])
                act.drain().then_inc(turn_sem, 1)
            with act.Fori(0, B) as i:
                for step in steps:
                    kind = step[0]
                    if kind in ("Q", "K"):
                        _, g, c = step
                        bank, free = wait_full(act, i, step)
                        if g == 0 and c == 0:
                            if kind == "Q":
                                act.wait_ge(ct_split, 1 + i * TT)
                            else:
                                act.wait_ge(stored, 1 + i * 16)
                        dst = (q_raw if kind == "Q" else k_raw)[:, g, c * CH:(c + 1) * CH]
                        if masked:
                            bias = (bq if kind == "Q" else bk)[:, g:g + 1]
                            act.activation(dst, bank[:, :], ACT.Identity, bias=bias).then_inc(free, 1)
                        else:
                            act.activation(dst, bank[:, :], ACT.Copy).then_inc(free, 1)
                    elif kind == "EX":
                        act.wait_ge(gate_sum, i + 1)
                        act.activation(gate[:, :, :], gate[:, :, :], ACT.Exp, scale=-1.0).then_inc(gate_exp, 1)
                    elif kind == "AP":
                        bank, free = wait_full(act, i, step)
                        c = step[1]
                        act.activation(ap_t[0:H, c * CH:(c + 1) * CH], bank[0:H, :], ACT.Copy).then_inc(free, 1)
                        act.drain().then_inc(ap_ready, 1)
                    elif kind == "mneg":
                        bank, free = wait_full(act, i, step)
                        p = step[1]
                        if p > 0:
                            s = (p - 1) % SLOTS
                            act.wait_ge(mrow_in[s], (i * len(pair_slots[s]) + pair_slots[s].index(p - 1) + 1) * 16)
                        act.activation(mrow[:, :], bank[0:2 * TT, 0:P], ACT.Copy).then_inc(free, 1)
                        act.drain().then_inc(mrow_ready, 1)
                    elif kind == "apx":
                        bank, free = wait_full(act, i, step)
                        _, p, c = step
                        act.wait_ge(u_ready, 1 + (i * PAIRS + p) * NC_)
                        act.activation(apx[:, c, :], bank[:, :], ACT.Copy).then_inc(free, 1)
                        act.drain().then_inc(apx_ready, 1)
                    elif kind == "RZ":
                        bank, free = wait_full(act, i, step)
                        act.activation(rz[:, :], bank[:, :], ACT.Copy).then_inc(free, 1)
                        act.drain().then_inc(rz_ready, 1)
                    elif kind == "pad":
                        bank, free = wait_full(act, i, step)
                        alone(act)
                        act.drain().then_inc(free, 1)
                    elif kind == "st":
                        _, p, kt = step
                        for h in range(2):
                            n = 2 * (p * TT + kt) + h
                            act.wait_ge(st_full, 1 + i * H * TT + n + 1)
                            if n >= PRING:
                                act.wait_ge(pv_done, 1 + i * PAIRS * TT + p * TT + kt - PRING // 2 + 1)
                            act.activation(probs[:, n % PRING, :], scores[n % 2][:, :], ACT.Exp,
                                           scale=SCALE).then_inc(p_full, 1)
                    elif kind == "xt":
                        t = step[1]
                        if t == 0:
                            act.wait_ge(var_ready, i + 1)
                            act.activation(sd[:, :], tmp[:, :], ACT.Sqrt).then_inc(sd_ready, 1)
                            act.wait_ge(x_ready, i * TT + TT)
                            act.dma_start(io["out"][bass.ds(i, 1), :, :].rearrange("b (t p) d -> p (b t) d", p=P), y)\
                               .then_inc(stored, 16)
                        bank, free = wait_full(act, i, step)
                        if t >= 2:
                            act.wait_ge(xt_stored[t % 2], 1 + (i * (TT // 2) + t // 2) * 16)
                        act.activation(xts[:, t % 2, :, :].rearrange("p k n -> p (k n)"), bank[:, :],
                                       ACT.Copy).then_inc(free, 1)
                        act.drain().then_inc(xt_ready, 1)
                        act.wait_ge(xt_ready, i * TT + t + 1)
                        act.dma_start(io["out_t"][bass.ds(i, 1), :, t * P:(t + 1) * P]
                                      .rearrange("b (k p) s -> p (b k) s", p=P), xts[:, t % 2, :, :])\
                           .then_inc(xt_stored[t % 2], 16)
            act.wait_ge(stored, 1 + B * 16)
            for b in range(2):
                act.wait_ge(xt_stored[b], 1 + B * (TT // 2) * 16)

        @block.vector
        def _(dve):
            dve.memset(acc[:, :, :], 0.0).then_inc(setup, 1)
            dve.wait_ge(const_in, 16 * (7 if masked else 27))
            if masked:
                dve.memset(ones[:, :], 1.0)
                dve.memset(v_ext[:, :, :, DH:VW], 1.0)
                dve.tensor_scalar(eye8[:, :], eye[:, :], 16384.0, None, ALU.mult, saturate=False)
            else:
                dve.memset(v_ext[:, :, :, DH + 1:VW], 1.0)
                dve.memset(ap_t[:, :], 1e-8)
                dve.memset(half_pi[:, :], math.pi / 2)
                dve.tensor_scalar(turn_in[:, 0:3, :], turn_in[:, 0:3, :], -87.0, None, ALU.max)
                dve.drain().then_inc(turn_sem, 1)
                dve.wait_ge(turn_sem, 2)
                dve.tensor_scalar(turn[:, 0:3, :], turn[:, 0:3, :], 1.0, None, ALU.add)
                dve.drain()
                dve.reciprocal(turn[:, 0:3, :], turn[:, 0:3, :])
                dve.drain().then_inc(turn_sem, 1)
                dve.wait_ge(turn_sem, 4)
                dve.tensor_tensor(turn[:, 6, :], turn[:, 1, :], turn[:, 2, :], ALU.mult)
                dve.drain()
                dve.tensor_tensor(turn[:, 6, :], turn[:, 6, :], turn[:, 3, :], ALU.mult)
                dve.drain()
                dve.tensor_tensor(turn[:, 5, :], turn[:, 5, :], turn[:, 6, :], ALU.mult)
                dve.tensor_tensor(turn[:, 7, :], turn[:, 4, :], turn[:, 6, :], ALU.mult)
                dve.drain()
                dve.tensor_scalar(turn[:, 7, :], turn[:, 7, :], sign[:, 0:1], None, ALU.mult)
                dve.drain()
                wo_as_is = q_raw[:, 0:2, :].rearrange("p g (a d) -> p (g a) d", d=D)
                wo_swapped = q_raw[:, 2:4, :].rearrange("p g (a d) -> p (g a) d", d=D)
                for k in range(KT):
                    dve.tensor_scalar(y[:, k, :], wo_as_is[:, k, :], turn[:, 5, k:k + 1], None, ALU.mult)
                dve.drain()
                for k in range(KT):
                    dve.scalar_tensor_tensor(out=y[:, k, :], in0=wo_swapped[:, k, :], scalar=turn[:, 7, k:k + 1],
                                             in1=y[:, k, :], op0=ALU.mult, op1=ALU.add)
                dve.drain().then_inc(turn_sem, 1)
            dve.drain().then_inc(setup, 1)
            with dve.Fori(0, B) as i:
                def take_sums(p):
                    dve.wait_ge(pv_done, 1 + i * PAIRS * TT + (p + 1) * TT)
                    if p == 0:
                        for b in range(2):
                            dve.wait_ge(xt_stored[b], 1 + i * (TT // 2) * 16)
                    for c in range(NC_):
                        if masked:
                            dve.tensor_copy(u[:, c, :], acc[:, c, :]).then_inc(u_ready, 1)
                        else:
                            dve.wait_ge(apx_ready, (i * PAIRS + p) * NC_ + c + 1)
                            dve.tensor_tensor(u[:, c, :], acc[:, c, :], apx[:, c, :], ALU.mult).then_inc(u_ready, 1)

                def maxima(p):
                    if p > 0:
                        n = use_no[("mneg", p - 1)]
                        dve.wait_ge(work_full[n % 2], i * PER + n // 2 + 1)
                    alone(dve)
                    dve.drain()
                    m = mx[:, p % 2, :].rearrange("p (n c) -> p n c", c=NC_)
                    if masked:
                        dve.tensor_tensor(mm[:, :], m[:, :, 0], m[:, :, 1], ALU.max)
                        dve.drain()
                        dve.tensor_scalar(mm[:, :], mm[:, :], ABSENT, None, ALU.max).then_inc(mm_ready, 1)
                    else:
                        dve.tensor_tensor(mm[:, :], m[:, :, 0], m[:, :, 1], ALU.max).then_inc(mm_ready, 1)

                for step in steps:
                    kind = step[0]
                    if step == ("Q", 0, 0) and masked:
                        for t in range(TT):
                            for c in range(NC_):
                                n = NC_ * t + c
                                dve.wait_ge(mstage_full[n % 2], (i * NC_ * TT + n // 2 + 1) * 16)
                                dve.tensor_scalar(mask_q[:, t, c * CH:(c + 1) * CH], mstage[:, n % 2, :], 0,
                                                  MASKED, ALU.is_equal, ALU.mult).then_inc(mstage_free, 1)
                        dve.drain()
                        dve.tensor_reduce(none[:, :], mask_q[:, :, :], AX.X, ALU.max)
                        dve.drain()
                        dve.tensor_scalar(none[:, :], none[:, :], -1.0, None, ALU.is_lt)
                    if step == ("st", 0, 0) and masked:
                        for t in range(TT):
                            for c in range(NC_):
                                n = NC_ * (TT + t) + c
                                dve.wait_ge(mstage_full[n % 2], (i * NC_ * TT + n // 2 + 1) * 16)
                                alone(dve)
                                dve.tensor_scalar(mask_k[:, t, c * CH:(c + 1) * CH], mstage[:, n % 2, :], 0,
                                                  MASKED / 16384.0, ALU.is_equal, ALU.mult, saturate=False).then_inc(mstage_free, 1)
                        dve.drain().then_inc(maskk_ready, 1)
                    if kind == "V":
                        t = step[1]
                        bank, free = wait_full(dve, i, step)
                        val = bank[:, :].rearrange("p (h d) -> p h d", h=H)
                        if masked:
                            dve.tensor_tensor(v_ext[:, t, :, 0:DH], val,
                                              bv[:, :].rearrange("p (h d) -> p h d", h=H), ALU.add).then_inc(free, 1)
                        else:
                            dve.tensor_tensor(v_ext[:, t, :, 0:DH], val,
                                              gate[:, t, H:2 * H].unsqueeze(2).to_broadcast([P, H, DH]),
                                              ALU.mult).then_inc(free, 1)
                    elif kind == "EX":
                        bank, free = wait_full(dve, i, step)
                        dve.tensor_tensor(gate[:, :, :], bank[:, 0:TT * 2 * H].rearrange("p (t h) -> p t h", t=TT),
                                          bsm[:, :].unsqueeze(1).to_broadcast([P, TT, 2 * H]), ALU.add)\
                           .then_inc(free, 1)
                        dve.drain()
                        dve.tensor_scalar(gate[:, :, :], gate[:, :, :], -87.0, None, ALU.max)
                        dve.drain().then_inc(gate_sum, 1)
                        dve.wait_ge(gate_exp, i + 1)
                        dve.tensor_scalar(gate[:, :, :], gate[:, :, :], 1.0, None, ALU.add)
                        dve.drain()
                        dve.reciprocal(gate[:, :, :], gate[:, :, :])
                        dve.drain().then_inc(gate_ready, 1)
                        dve.tensor_copy(v_ext[:, :, :, DH:DH + 1], gate[:, :, H:2 * H].unsqueeze(3))
                    elif kind == "smax":
                        _, p, h, t, c = step
                        bank, free = wait_full(dve, i, step)
                        j = (h * TT + t) * NC_ + c
                        if masked:
                            alone(dve)
                            dve.tensor_tensor_reduce(bank[:, :], bank[:, :], mask_q[:, t, c * CH:(c + 1) * CH],
                                                     1.0, -3e38, ALU.add, ALU.max,
                                                     mx[:, p % 2, j:j + 1]).then_inc(free, 1)
                        else:
                            dve.tensor_reduce(mx[:, p % 2, j:j + 1], bank[:, :], AX.X, ALU.max).then_inc(free, 1)
                        if (h, t, c) == (1, TT - 1, NC_ - 1) and p < 2:
                            maxima(p)
                    elif kind == "CS":
                        bank, free = wait_full(dve, i, step)
                        dve.tensor_scalar(vmean[:, :], bank[:, 0:KT], 1.0 / S, None, ALU.mult).then_inc(free, 1)
                        dve.drain()
                        wide_mean = vmean[:, :].unsqueeze(2).to_broadcast([P, KT, P])
                        dve.tensor_copy(vm[:, 0, :, :], wide_mean)
                        dve.drain()
                        dve.tensor_tensor(vm[:, 1, :, :], wide_mean, vm[:, 0, :, :].bitcast(F32), ALU.subtract)
                        dve.drain().then_inc(vm_ready, 1)
                    elif kind == "st":
                        _, p, kt = step
                        if kt == 0 and p > 0:
                            take_sums(p - 1)
                            if 2 <= p + 1 < PAIRS:
                                maxima(p + 1)
                        if kt == 4 and p == PAIRS - 1 and masked:
                            dve.wait_ge(bo_added, i + 1)
                            dve.wait_ge(rz_ready, i + 1)
                            for t in range(TT):
                                dve.scalar_tensor_tensor(out=y[:, t, :], in0=rz[:, :], scalar=none[:, t:t + 1],
                                                         in1=y[:, t, :], op0=ALU.mult, op1=ALU.add)
                    elif kind == "tail" and step[1] == PAIRS - 1:
                        take_sums(PAIRS - 1)
                    elif kind == "den":
                        _, p, c = step
                        bank, free = wait_full(dve, i, step)
                        alone(dve)
                        dve.drain()
                        if masked:
                            dve.tensor_scalar(r[:, :], bank[:, :], 1e-30, None, ALU.max).then_inc(free, 1)
                            dve.drain()
                            dve.reciprocal(r[:, :], r[:, :])
                        else:
                            dve.reciprocal(r[:, :], bank[:, :]).then_inc(free, 1)
                        dve.drain()
                        for h in range(2):
                            a = DH * ((2 * p + h) % 4)
                            last = dve.tensor_tensor(q_raw[a:a + DH, p // 2, c * CH:(c + 1) * CH],
                                                     u[64 * h:64 * h + DH, c, :], r[64 * h:64 * h + DH, :], ALU.mult)
                        dve.drain().then_inc(ctx_done, 1)
                    elif kind == "out":
                        t = step[1]
                        bank, free = wait_full(dve, i, step)
                        if t == 0:
                            dve.wait_ge(res_in, i * 16 + 16)
                        dve.tensor_tensor(y[:, t, :], bank[:, :], y[:, t, :], ALU.add).then_inc(free, 1)
                        dve.drain()
                        dve.bn_stats(stats[:, :], y[:, t, :])
                        dve.drain()
                        dve.bn_aggr(mv[:, t, :], stats[:, :])
                        if t == TT - 1:
                            dve.drain()
                            dve.tensor_scalar(tmp[:, :], mv[:, :, 1], EPS, None, ALU.add).then_inc(var_ready, 1)
                            dve.wait_ge(sd_ready, i + 1)
                            dve.reciprocal(rstd[:, :], sd[:, :])
                            dve.drain()
                            dve.tensor_tensor(sd[:, :], rstd[:, :], rstd[:, :], ALU.mult)
                            dve.drain()
                            dve.tensor_tensor(sd[:, :], sd[:, :], tmp[:, :], ALU.mult)
                            dve.drain()
                            dve.tensor_scalar(sd[:, :], sd[:, :], -0.5, 1.5, ALU.mult, ALU.add)
                            dve.drain()
                            dve.tensor_tensor(rstd[:, :], rstd[:, :], sd[:, :], ALU.mult)
                            dve.drain()
                            for q in range(TT):
                                dve.tensor_scalar(y[:, q, :], y[:, q, :], mv[:, q, 0:1], rstd[:, q:q + 1],
                                                  ALU.subtract, ALU.mult).then_inc(x_ready, 1)


E = 16
HD = 64
WIDE = E * HD
FK = WIDE // P
RING = 4
INV = HD ** -0.5
XC = 256


def ffn_steps():
    steps = [("LG",)] + [("proj", w, t) for w in range(6) for t in range(TT)]
    steps += [("turn", n) for n in range(TT // 2)]
    halves = lambda qt: range(1 if qt < TT // 2 else 2)
    for n in range(TT + 2):
        if 2 <= n:
            steps += [("mixed_t", n - 2, g) for g in range(2)]
        if n < TT:
            steps += [("score", n, c) for c in halves(n)]
        if 1 <= n <= TT:
            steps += [("prob_t", n - 1, c) for c in halves(n - 1)]
        if 2 <= n:
            steps.append(("out", n - 2))
        if 1 <= n <= TT:
            steps.append(("pv", n - 1))
    while len(steps) % RING:
        steps.append(("pad", len(steps) % RING))
    return steps


def expert_layer(nc, io):
    steps = ffn_steps()
    PER = len(steps) // RING
    use_no = {s: n for n, s in enumerate(steps)}
    ctx = ExitStack()
    with ctx:
        used = [0]
        size = nc.sbuf_bytes_remaining // 64 * 64
        start = -(-nc.sbuf_base // 64) * 64
        ctx.enter_context(nc.sbuf_tensor("arena_e", [P, size], mybir.dt.uint8))

        def sb(name, shape, dt=F32, at=None):
            n = 4
            for k in shape[1:]:
                n *= k
            if at is None:
                at = start + used[0]
                used[0] += -(-n // 64) * 64
                assert used[0] + 64 <= size, (name, used[0], size)
            place[name] = at
            return nc.alloc_sbuf_tensor_at(f"{name}_e", shape, dt, offset=at)

        place = {}
        sem = lambda n: ctx.enter_context(nc.semaphore(f"{n}_e"))

        w_in = sb("w_in", [P, 6, 2, KT, CH], F32R)
        w_out = sb("w_out", [P, 2, FK, D], F32R)
        x = sb("x", [P, 2, KT, S], F32R)
        prob = sb("prob", [P, 2, S], at=place["x"])
        prob_t = sb("prob_t", [P, TT, P], at=place["x"] + 8 * S)
        mixed = sb("mixed", [P, E, HD], at=place["x"] + 12 * S)
        mixed_t = sb("mixed_t", [P, 2, FK, P], F32R, at=place["x"] + 16 * S)
        y = sb("y", [P, TT, D])
        weighted = sb("weighted", [P, 2, CH])
        part = sb("part", [P, HD])
        qkv = sb("qkv", [P, 3, TT, HD])
        q_t = sb("q_t", [HD, S])
        k_t = sb("k_t", [HD, S])
        stage = sb("stage", [P, 2, XC])
        w_stage = sb("w_stage", [P, 2, CH])
        eye = sb("eye", [P, P])
        causal = sb("causal", [P, P])
        lower = sb("lower", [P, E, E])
        square = sb("square", [P, CH], at=place["weighted"])
        sim_raw = sb("sim_raw", [P, KT, E])
        sim_sq = sb("sim_sq", [P, KT, E])
        sim = sb("sim", [P, 2, KT, E], F32R)
        ones = sb("ones", [P, P])
        norm = sb("norm", [P, 4, E])
        gates = sb("gates", [P, E])
        lg = sb("lg", [P, TT, E])
        rw = sb("rw", [P, TT, E])
        pick = sb("pick", [P, TT, E])
        beats = sb("beats", [P, TT, E, E], at=place["q_t"])
        small = sb("small", [P, 10, TT])
        nmax = sb("nmax", [P, TT, 2])
        total = sb("total", [P, TT, 2])
        rtot = sb("rtot", [P, TT])
        attn = sb("attn", [P, HD])
        stats = sb("stats", [P, 6])
        mv = sb("mv", [P, TT, 2])
        sd = sb("sd", [P, TT])
        rstd = sb("rstd", [P, TT])
        tmp = sb("tmp", [P, TT])

        bank_of = [ctx.enter_context(nc.psum_tensor(f"work{b}_e", [P, CH], F32)) for b in range(RING)]

        const_in = sem("const_in")
        setup = sem("setup")
        apart = sem("apart")
        norm_sem = sem("norm_sem")
        work_full = [sem(f"work_full{b}") for b in range(RING)]
        work_free = [sem(f"work_free{b}") for b in range(RING)]
        stage_full = [sem(f"stage_full{b}") for b in range(2)]
        stage_free = sem("stage_free")
        w_hi = sem("w_hi")
        w_ready = sem("w_ready")
        x_over = sem("x_over")
        x_full = [sem(f"x_full{b}") for b in range(2)]
        x_free = sem("x_free")
        x_ready = sem("x_ready")
        proj_done = sem("proj_done")
        res_in = sem("res_in")
        squares = sem("squares")
        roots = sem("roots")
        lg_ready = sem("lg_ready")
        exp_ready = sem("exp_ready")
        qkv_ready = sem("qkv_ready")
        turned_in = sem("turned_in")
        masked_in = sem("masked_in")
        prob_ready = sem("prob_ready")
        prob_t_ready = sem("prob_t_ready")
        mixed_ready = sem("mixed_ready")
        hi_ready = sem("hi_ready")
        lo_ready = sem("lo_ready")
        var_ready = sem("var_ready")
        sd_ready = sem("sd_ready")
        y_ready = sem("y_ready")
        stored = sem("stored")

        w_chunks = [(w, k) for w in range(6) for k in range(KT)] + [(6, k) for k in range(FK)]
        NW = len(w_chunks)
        NX = KT * S // XC
        halves = lambda qt: range(1 if qt < TT // 2 else 2)
        keys = lambda qt, c: min(CH, (qt + 1) * P - c * CH)
        scored = lambda qt: sum(len(halves(q)) for q in range(qt + 1))
        SC = scored(TT - 1)

        def wait_full(eng, i, step):
            n = use_no[step]
            eng.wait_ge(work_full[n % RING], i * PER + n // RING + 1)
            return bank_of[n % RING], work_free[n % RING]

        def alone(eng):
            eng.sem_inc(apart, 1)

        block = ctx.enter_context(nc.Block("experts"))

        @block.sync
        def _(sp):
            for t, src in ((eye, io["eye"]), (causal, io["causal"])):
                sp.dma_start(t[:, :], src).then_inc(const_in, 16)
            sp.dma_start(lower[:, :, :], io["lower"].partition_broadcast(P)).then_inc(const_in, 16)
            sp.dma_start(gates[:, :], io["gates"].partition_broadcast(P)).then_inc(const_in, 16)
            sp.dma_start(sim_raw[:, :, :], io["sim"].rearrange("(k p) e -> p k e", p=P)).then_inc(const_in, 16)

            def load_x(i):
                for n in range(NX):
                    k, c = n // (S // XC), n % (S // XC)
                    sp.wait_ge(x_free, 1 + i * NX + max(n - 1, 0))
                    alone(sp)
                    sp.dma_start(stage[:, n % 2, :], io["src_t"][bass.ds(i, 1), k * P:(k + 1) * P, c * XC:(c + 1) * XC]
                                 .rearrange("b p s -> (b p) s")).then_inc(x_full[n % 2], 16)

            for n, (w, k) in enumerate(w_chunks):
                if n >= 2:
                    sp.wait_ge(stage_free, n - 1)
                if w < 6:
                    src = io[("wq", "wk", "wv")[w // 2]][k * P:(k + 1) * P, (w % 2) * CH:(w % 2 + 1) * CH]
                else:
                    src = io["wo"][k * P:(k + 1) * P, :]
                sp.dma_start(w_stage[:, n % 2, :], src).then_inc(stage_full[n % 2], 16)
            sp.wait_ge(setup, 3)
            with sp.Fori(0, B) as i:
                sp.wait_ge(stored, 1 + i * 16)
                alone(sp)
                sp.dma_start(y[:, :, :], io["res"][bass.ds(i, 1), :, :].rearrange("b (t p) d -> p (b t) d", p=P))\
                  .then_inc(res_in, 16)
                load_x(i)
                sp.wait_ge(y_ready, i * TT + TT)
                alone(sp)
                sp.dma_start(io["out"][bass.ds(i, 1), :, :].rearrange("b (t p) d -> p (b t) d", p=P), y[:, :, :])\
                  .then_inc(stored, 16)
            sp.wait_ge(stored, 1 + B * 16)

        @block.gpsimd
        def _(pool):
            for count in (*work_free, x_over, x_free, stored):
                pool.sem_inc(count, 1)
            pool.drain().then_inc(setup, 1)
            pool.wait_ge(setup, 3)
            with pool.Fori(0, B) as i:
                pool.wait_ge(x_over, 1 + i)
                alone(pool)
                for n in range(NX):
                    k, c = n // (S // XC), n % (S // XC)
                    pool.wait_ge(x_full[n % 2], (i * (NX // 2) + n // 2 + 1) * 16)
                    alone(pool)
                    hi, lo = (x[:, part, k, c * XC:(c + 1) * XC] for part in range(2))
                    pool.tensor_scalar(hi, stage[:, n % 2, :], 1.0, 0.0, ALU.mult, ALU.add)
                    pool.drain()
                    pool.tensor_tensor(lo, stage[:, n % 2, :], hi.bitcast(F32), ALU.subtract).then_inc(x_free, 1)
                pool.drain().then_inc(x_ready, 1)

        @block.tensor
        def _(pe):
            pe.wait_ge(setup, 3)
            pe.wait_ge(norm_sem, 1)
            for k in range(KT):
                last = pe.matmul(bank_of[0][:, 0:E], ones[:, :], sim_sq[:, k, :], start=(k == 0), stop=(k == KT - 1))
            last.then_inc(norm_sem, 1)
            pe.wait_ge(norm_sem, 5)
            with pe.Fori(0, B) as i:
                def parts(out, hi_l, lo_l, hi_r, lo_r, tiles=KT):
                    for k in range(tiles):
                        for n, (a, b) in enumerate(((hi_l, hi_r), (hi_l, lo_r), (lo_l, hi_r))):
                            last = pe.matmul(out, a(k), b(k), start=(k == 0 and n == 0),
                                             stop=(k == tiles - 1 and n == 2))
                    return last

                for n, step in enumerate(steps):
                    kind = step[0]
                    bank = bank_of[n % RING]
                    pe.wait_ge(work_free[n % RING], 1 + i * PER + n // RING)
                    if kind == "LG":
                        pe.wait_ge(x_ready, i + 1)
                        for t in range(TT):
                            last = parts(bank[:, t * E:(t + 1) * E], lambda k: x[:, 0, k, t * P:(t + 1) * P],
                                         lambda k: x[:, 1, k, t * P:(t + 1) * P],
                                         lambda k: sim[:, 0, k, :], lambda k: sim[:, 1, k, :])
                    elif kind == "proj":
                        _, w, t = step
                        if t == 0:
                            pe.wait_ge(w_ready, (w + 1) * KT)
                        last = parts(bank[:, :], lambda k: x[:, 0, k, t * P:(t + 1) * P],
                                     lambda k: x[:, 1, k, t * P:(t + 1) * P],
                                     lambda k: w_in[:, w, 0, k, :], lambda k: w_in[:, w, 1, k, :])
                    elif kind == "turn":
                        if step[1] == 0:
                            pe.wait_ge(qkv_ready, i + 1)
                        alone(pe)
                        for j in range(2):
                            for part_ in range(2):
                                at = (2 * part_ + j) * P
                                last = pe.transpose(bank[0:HD, at:at + P], qkv[:, part_, 2 * step[1] + j, :], eye[:, :])
                    elif kind == "score":
                        _, qt, c = step
                        if qt == 0:
                            pe.wait_ge(turned_in, i + 1)
                        last = pe.matmul(bank[:, 0:keys(qt, c)], q_t[:, qt * P:(qt + 1) * P],
                                         k_t[:, c * CH:c * CH + keys(qt, c)], start=True, stop=True)
                    elif kind == "prob_t":
                        _, qt, c = step
                        pe.wait_ge(prob_ready, i * SC + scored(qt) - len(halves(qt)) + c + 1)
                        for j in range(keys(qt, c) // P):
                            last = pe.transpose(bank[:, j * P:(j + 1) * P],
                                                prob[:, qt % 2, c * CH + j * P:c * CH + (j + 1) * P], eye[:, :])
                    elif kind == "pv":
                        qt = step[1]
                        pe.wait_ge(prob_t_ready, i * TT + qt + 1)
                        for kt in range(qt + 1):
                            last = pe.matmul(bank[:, 0:HD], prob_t[:, kt, :], qkv[:, 2, kt, :],
                                             start=(kt == 0), stop=(kt == qt))
                    elif kind == "mixed_t":
                        _, qt, g = step
                        pe.wait_ge(mixed_ready, i * TT + qt + 1)
                        for j in range(FK // 2):
                            at = (g * FK // 2 + j) * P
                            last = pe.transpose(bank[:, j * P:(j + 1) * P],
                                                mixed[:, :, :].rearrange("p e d -> p (e d)")[:, at:at + P], eye[:, :])
                    elif kind == "out":
                        qt = step[1]
                        pe.wait_ge(lo_ready, (i * TT + qt + 1) * 2)
                        if qt == 0:
                            pe.wait_ge(w_ready, NW)
                        last = parts(bank[:, :], lambda k: mixed_t[:, 0, k, :], lambda k: mixed_t[:, 1, k, :],
                                     lambda k: w_out[:, 0, k, :], lambda k: w_out[:, 1, k, :], FK)
                    elif kind == "pad":
                        last = pe.matmul(bank[:, 0:P], ones[:, :], eye[:, :], start=True, stop=True)
                    last.then_inc(work_full[n % RING], 1)
                    if step == ("out", TT - 1):
                        pe.drain().then_inc(x_over, 1)

        @block.scalar
        def _(act):
            act.wait_ge(norm_sem, 3)
            act.activation(norm[:, 1, :], norm[:, 0, :], ACT.Sqrt)
            act.drain()
            act.activation(norm[:, 2, :], gates[:, :], ACT.Exp, scale=-1.0)
            act.drain().then_inc(norm_sem, 1)
            act.wait_ge(setup, 3)
            for n, (w, k) in enumerate(w_chunks):
                act.wait_ge(stage_full[n % 2], 16 * (n // 2 + 1))
                hi = w_in[:, w, 0, k, :] if w < 6 else w_out[:, 0, k, :]
                act.activation(hi, w_stage[:, n % 2, :], ACT.Copy).then_inc(w_hi, 1)
            with act.Fori(0, B) as i:
                for step in steps:
                    kind = step[0]
                    if kind == "LG":
                        act.wait_ge(res_in, i * 16 + 16)
                        for t in range(TT):
                            act.activation(square[:, :], y[:, t, :], ACT.Square, accum_out=small[:, 0, t:t + 1])
                            act.drain()
                        act.activation(small[:, 1, :], small[:, 0, :], ACT.Sqrt)
                        act.drain().then_inc(roots, 1)
                        act.wait_ge(lg_ready, i + 1)
                        act.activation(pick[:, :, :], pick[:, :, :], ACT.Exp)
                        act.drain().then_inc(exp_ready, 1)
                    elif kind == "turn":
                        n = step[1]
                        bank, free = wait_full(act, i, step)
                        act.activation(q_t[:, 2 * n * P:(2 * n + 2) * P], bank[0:HD, 0:2 * P], ACT.Copy)
                        act.activation(k_t[:, 2 * n * P:(2 * n + 2) * P], bank[0:HD, 2 * P:4 * P], ACT.Copy)\
                           .then_inc(free, 1)
                        if n == TT // 2 - 1:
                            act.drain().then_inc(turned_in, 1)
                    elif kind == "score":
                        _, qt, c = step
                        act.wait_ge(masked_in, i * TT + qt + 1)
                        bank, free = wait_full(act, i, step)
                        act.activation(prob[:, qt % 2, c * CH:c * CH + keys(qt, c)], bank[:, 0:keys(qt, c)], ACT.Exp,
                                       scale=INV, bias=nmax[:, qt, 0:1], accum_out=total[:, qt, c:c + 1])\
                           .then_inc(free, 1)
                        act.drain().then_inc(prob_ready, 1)
                    elif kind == "prob_t":
                        _, qt, c = step
                        bank, free = wait_full(act, i, step)
                        act.activation(prob_t[:, c * 4:c * 4 + keys(qt, c) // P, :].rearrange("p k n -> p (k n)"),
                                       bank[:, 0:keys(qt, c)], ACT.Copy).then_inc(free, 1)
                        if c == halves(qt)[-1]:
                            act.drain().then_inc(prob_t_ready, 1)
                    elif kind == "mixed_t":
                        _, qt, g = step
                        n = use_no[step]
                        act.wait_ge(work_full[n % RING], i * PER + n // RING + 1)
                        act.activation(mixed_t[:, 0, g * 4:g * 4 + 4, :].rearrange("p k n -> p (k n)"),
                                       bank_of[n % RING][:, :], ACT.Copy)
                        act.drain().then_inc(hi_ready, 1)
                    elif kind == "pad":
                        bank, free = wait_full(act, i, step)
                        alone(act)
                        act.drain().then_inc(free, 1)
                    if step == ("out", TT - 1):
                        act.wait_ge(var_ready, i + 1)
                        act.activation(sd[:, :], tmp[:, :], ACT.Sqrt).then_inc(sd_ready, 1)

        @block.vector
        def _(dve):
            dve.memset(ones[:, :], 1.0)
            dve.wait_ge(const_in, 16 * 5)
            dve.tensor_tensor(sim_sq[:, :, :], sim_raw[:, :, :], sim_raw[:, :, :], ALU.mult)
            dve.drain().then_inc(setup, 1)
            dve.engine_nop().then_inc(setup, 1)
            dve.engine_nop().then_inc(norm_sem, 1)
            dve.wait_ge(norm_sem, 2)
            dve.tensor_copy(norm[:, 0, :], bank_of[0][:, 0:E])
            dve.tensor_scalar(gates[:, :], gates[:, :], -87.0, None, ALU.max)
            dve.drain().then_inc(norm_sem, 1)
            dve.wait_ge(norm_sem, 4)

            def better_root(out, sq, root, hold):
                dve.tensor_scalar(root, root, 1e-12, None, ALU.max)
                dve.drain()
                dve.reciprocal(hold, root)
                dve.drain()
                dve.tensor_tensor(hold, hold, sq, ALU.mult)
                dve.drain()
                dve.tensor_tensor(hold, hold, root, ALU.add)
                dve.drain()
                dve.tensor_scalar(out, hold, 0.5, 1e-12, ALU.mult, ALU.max)
                dve.drain()

            better_root(norm[:, 1, :], norm[:, 0, :], norm[:, 1, :], norm[:, 3, :])
            dve.reciprocal(norm[:, 1, :], norm[:, 1, :])
            dve.drain()
            dve.tensor_tensor(sim_sq[:, :, :], sim_raw[:, :, :], norm[:, 1, :].unsqueeze(1).to_broadcast([P, KT, E]),
                              ALU.mult)
            dve.tensor_scalar(norm[:, 2, :], norm[:, 2, :], 1.0, None, ALU.add)
            dve.drain()
            dve.reciprocal(gates[:, :], norm[:, 2, :])
            dve.tensor_copy(sim[:, 0, :, :], sim_sq[:, :, :])
            dve.drain()
            dve.tensor_tensor(sim[:, 1, :, :], sim_sq[:, :, :], sim[:, 0, :, :].bitcast(F32), ALU.subtract)
            dve.drain().then_inc(norm_sem, 1)
            for n, (w, k) in enumerate(w_chunks):
                dve.wait_ge(w_hi, n + 1)
                hi, lo = (w_in[:, w, part_, k, :] if w < 6 else w_out[:, part_, k, :] for part_ in range(2))
                dve.tensor_tensor(lo, w_stage[:, n % 2, :], hi.bitcast(F32), ALU.subtract).then_inc(stage_free, 1)
                dve.drain().then_inc(w_ready, 1)
            with dve.Fori(0, B) as i:
                for step in steps:
                    kind = step[0]
                    if kind == "LG":
                        bank, free = wait_full(dve, i, step)
                        dve.wait_ge(roots, i + 1)
                        alone(dve)
                        better_root(small[:, 1, :], small[:, 0, :], small[:, 1, :], small[:, 2, :])
                        dve.reciprocal(small[:, 1, :], small[:, 1, :])
                        dve.drain()
                        dve.tensor_tensor(lg[:, :, :], bank[:, 0:TT * E].rearrange("p (t e) -> p t e", t=TT),
                                          small[:, 1, :].unsqueeze(2).to_broadcast([P, TT, E]), ALU.mult)\
                           .then_inc(free, 1)
                        dve.drain()
                        dve.tensor_tensor(lg[:, :, :], lg[:, :, :], gates[:, :].unsqueeze(1).to_broadcast([P, TT, E]),
                                          ALU.subtract)
                        dve.drain()
                        for t in range(TT):
                            me = lg[:, t, :].unsqueeze(2).to_broadcast([P, E, E])
                            other = lg[:, t, :].unsqueeze(1).to_broadcast([P, E, E])
                            dve.tensor_tensor(beats[:, t, :, :], other, me, ALU.is_equal)
                        dve.drain()
                        for t in range(TT):
                            dve.tensor_tensor(beats[:, t, :, :], beats[:, t, :, :], lower[:, :, :], ALU.mult)
                        dve.drain()
                        dve.tensor_reduce(rw[:, :, :], beats[:, :, :, :], AX.X, ALU.add)
                        dve.drain()
                        for t in range(TT):
                            me = lg[:, t, :].unsqueeze(2).to_broadcast([P, E, E])
                            other = lg[:, t, :].unsqueeze(1).to_broadcast([P, E, E])
                            dve.tensor_tensor(beats[:, t, :, :], other, me, ALU.is_gt)
                        dve.drain()
                        dve.tensor_reduce(pick[:, :, :], beats[:, :, :, :], AX.X, ALU.add)
                        dve.drain()
                        dve.tensor_tensor(rw[:, :, :], rw[:, :, :], pick[:, :, :], ALU.add)
                        dve.drain()
                        dve.tensor_scalar(rw[:, :, :], rw[:, :, :], 2.0, None, ALU.is_lt)
                        dve.tensor_scalar(lg[:, :, :], lg[:, :, :], 0.0, None, ALU.max)
                        dve.drain()
                        dve.tensor_reduce(small[:, 3, :], lg[:, :, :], AX.X, ALU.max)
                        dve.drain()
                        dve.tensor_scalar(small[:, 4, :], small[:, 3, :], 0.0, None, ALU.is_le)
                        dve.drain()
                        top = small[:, 3, :].unsqueeze(2).to_broadcast([P, TT, E])
                        dve.tensor_tensor(rw[:, :, :], rw[:, :, :],
                                          small[:, 4, :].unsqueeze(2).to_broadcast([P, TT, E]), ALU.mult)
                        dve.tensor_tensor(pick[:, :, :], lg[:, :, :], top, ALU.subtract)
                        dve.drain().then_inc(lg_ready, 1)
                        dve.tensor_scalar(lg[:, :, :], lg[:, :, :], 0.0, None, ALU.is_gt)
                        dve.drain()
                        dve.tensor_tensor(rw[:, :, :], rw[:, :, :], lg[:, :, :], ALU.add)
                        dve.drain()
                        dve.wait_ge(exp_ready, i + 1)
                        dve.tensor_tensor(rw[:, :, :], rw[:, :, :], pick[:, :, :], ALU.mult)
                        dve.drain()
                        dve.tensor_reduce(small[:, 5, :], rw[:, :, :], AX.X, ALU.add)
                        dve.drain()
                        dve.reciprocal(small[:, 6, :], small[:, 5, :])
                        dve.drain()
                        dve.tensor_tensor(rw[:, :, :], rw[:, :, :],
                                          small[:, 6, :].unsqueeze(2).to_broadcast([P, TT, E]), ALU.mult)
                        dve.drain()
                    elif kind == "proj":
                        _, w, t = step
                        bank, free = wait_full(dve, i, step)
                        prod = weighted[:, t % 2, :]
                        dve.tensor_tensor(prod.rearrange("p (e d) -> p e d", d=HD),
                                          bank[:, :].rearrange("p (e d) -> p e d", d=HD),
                                          rw[:, t, (w % 2) * 8:(w % 2) * 8 + 8].unsqueeze(2)
                                          .to_broadcast([P, 8, HD]), ALU.mult).then_inc(free, 1)
                        dve.drain()
                        target = qkv[:, w // 2, t, :] if w % 2 == 0 else part[:, :]
                        dve.tensor_reduce(target, prod.rearrange("p (e d) -> p d e", d=HD), AX.X, ALU.add)
                        if w % 2:
                            dve.drain()
                            dve.tensor_tensor(qkv[:, w // 2, t, :], qkv[:, w // 2, t, :], part[:, :], ALU.add)
                            if (w, t) == (5, TT - 1):
                                dve.drain().then_inc(qkv_ready, 1)
                            else:
                                dve.drain()
                    elif kind == "score":
                        _, qt, c = step
                        bank, free = wait_full(dve, i, step)
                        last_half = c == halves(qt)[-1]
                        width = keys(qt, c)
                        if last_half:
                            dve.tensor_tensor(bank[:, width - P:width], bank[:, width - P:width], causal[:, :], ALU.add)
                            dve.drain()
                        dve.tensor_reduce(nmax[:, qt, c:c + 1], bank[:, 0:width], AX.X, ALU.max)
                        if last_half:
                            dve.drain()
                            if c:
                                dve.tensor_tensor(nmax[:, qt, 0:1], nmax[:, qt, 0:1], nmax[:, qt, 1:2], ALU.max)
                                dve.drain()
                            dve.tensor_scalar(nmax[:, qt, 0:1], nmax[:, qt, 0:1], -INV, None, ALU.mult)
                            dve.drain().then_inc(masked_in, 1)
                    elif kind == "pv":
                        qt = step[1]
                        bank, free = wait_full(dve, i, step)
                        dve.wait_ge(prob_ready, i * SC + scored(qt))
                        if len(halves(qt)) == 2:
                            alone(dve)
                            dve.tensor_tensor(rtot[:, qt:qt + 1], total[:, qt, 0:1], total[:, qt, 1:2], ALU.add)
                            dve.drain()
                            dve.reciprocal(rtot[:, qt:qt + 1], rtot[:, qt:qt + 1])
                        else:
                            dve.reciprocal(rtot[:, qt:qt + 1], total[:, qt, 0:1])
                        dve.drain()
                        dve.tensor_scalar(attn[:, :], bank[:, 0:HD], rtot[:, qt:qt + 1], None, ALU.mult)\
                           .then_inc(free, 1)
                        dve.drain()
                        dve.tensor_tensor(mixed[:, :, :], attn[:, :].unsqueeze(1).to_broadcast([P, E, HD]),
                                          rw[:, qt, :].unsqueeze(2).to_broadcast([P, E, HD]), ALU.mult)
                        dve.drain().then_inc(mixed_ready, 1)
                    elif kind == "mixed_t":
                        _, qt, g = step
                        n = use_no[step]
                        dve.wait_ge(hi_ready, (i * TT + qt) * 2 + g + 1)
                        dst = lambda part_: mixed_t[:, part_, g * 4:g * 4 + 4, :].rearrange("p k n -> p (k n)")
                        dve.tensor_tensor(dst(1), bank_of[n % RING][:, :], dst(0).bitcast(F32), ALU.subtract)\
                           .then_inc(work_free[n % RING], 1)
                        dve.drain().then_inc(lo_ready, 1)
                    elif kind == "out":
                        t = step[1]
                        bank, free = wait_full(dve, i, step)
                        dve.tensor_tensor(y[:, t, :], bank[:, :], y[:, t, :], ALU.add).then_inc(free, 1)
                        dve.drain()
                        dve.bn_stats(stats[:, :], y[:, t, :])
                        dve.drain()
                        dve.bn_aggr(mv[:, t, :], stats[:, :])
                        if t == TT - 1:
                            dve.drain()
                            dve.tensor_scalar(tmp[:, :], mv[:, :, 1], EPS, None, ALU.add).then_inc(var_ready, 1)
                            dve.wait_ge(sd_ready, i + 1)
                            dve.reciprocal(rstd[:, :], sd[:, :])
                            dve.drain()
                            dve.tensor_tensor(sd[:, :], rstd[:, :], rstd[:, :], ALU.mult)
                            dve.drain()
                            dve.tensor_tensor(sd[:, :], sd[:, :], tmp[:, :], ALU.mult)
                            dve.drain()
                            dve.tensor_scalar(sd[:, :], sd[:, :], -0.5, 1.5, ALU.mult, ALU.add)
                            dve.drain()
                            dve.tensor_tensor(rstd[:, :], rstd[:, :], sd[:, :], ALU.mult)
                            dve.drain()
                            for q in range(TT):
                                dve.tensor_scalar(y[:, q, :], y[:, q, :], mv[:, q, 0:1], rstd[:, q:q + 1],
                                                  ALU.subtract, ALU.mult).then_inc(y_ready, 1)


def constants():
    import numpy as np

    eye = np.eye(P, dtype=np.float32)
    sel = {}
    for masked in (False, True):
        m = np.zeros((P, P), np.float32)
        for h in range(2):
            m[64 * h + DH, 64 * h:64 * h + 64] = 1.0
            if not masked:
                m[64 * h + DH + 1, 64 * h:64 * h + 64] = 1.0
        sel[masked] = m
    sign = np.where(np.arange(P) % DH < DH // 2, 1.0, -1.0).astype(np.float32).reshape(P, 1)
    ap = np.zeros((H + 1, PAIRS, P), np.float32)
    for p in range(PAIRS):
        for h in range(2):
            ap[2 * p + h, p, 64 * h:64 * h + DH + 1] = 1.0
            ap[H, p, 64 * h + DH + 1] = 1.0
    return {"eye": eye, "neg_eye": -eye, "sel_den1": sel[False], "sel_den2": sel[True], "sel_ap": ap, "sign": sign,
            "causal": np.where(np.arange(P)[None, :] > np.arange(P)[:, None], np.float32(-1e30), np.float32(0)),
            "lower": np.tril(np.ones((E, E), np.float32), -1)}


def turned(a, axes):
    import numpy as np

    return np.ascontiguousarray(np.transpose(a, axes))



def program(nc, ins, out):
    scratch = lambda name, shape: nc.dram_tensor(name, shape, F32).ap()
    x1, x1_t = scratch("x1", [B, S, D]), scratch("x1_t", [B, D, S])
    x2, x2_t = scratch("x2", [B, S, D]), scratch("x2_t", [B, D, S])
    attention(nc, False, dict(
        q_src=ins["x_t"], kv_src=ins["x_t"], res=ins["x"], wq=ins["L0_attn_Wi"], wk=ins["L0_attn_Wo"],
        wv=ins["L0_attn_Wv"], wo=ins["L0_attn_Wout"], wo_swapped=ins["Wout_swapped"],
        wo_turned=scratch("wo_turned", [D, D]), wa=ins["L0_attn_Wa"], we=ins["L0_attn_We"], ba=ins["L0_attn_ba"],
        be=ins["L0_attn_be"], beta=ins["L0_attn_beta_p"], iv=ins["L0_attn_iv_p"], ov=ins["L0_attn_ov_p"],
        chi=ins["L0_attn_chi"], out=x1, out_t=x1_t, eye=ins["eye"], neg_eye=ins["neg_eye"],
        sel_den=ins["sel_den1"], sel_ap=ins["sel_ap"], sign=ins["sign"]))
    attention(nc, True, dict(
        q_src=x1_t, kv_src=ins["ctx_t"], res=x1, wq=ins["Wq_t"], wk=ins["Wk_t"], wv=ins["Wv_t"], wo=ins["Wo_t"],
        bq=ins["L0_xattn_bq"], bk=ins["L0_xattn_bk"], bv=ins["L0_xattn_bv"], bo=ins["L0_xattn_bo"],
        mask_q=ins["mask"], mask_k=ins["mask_t"], out=x2, out_t=x2_t, eye=ins["eye"], neg_eye=ins["neg_eye"],
        sel_den=ins["sel_den2"]))
    expert_layer(nc, dict(
        src_t=x2_t, res=x2, sim=ins["L0_ffn_sim_matrix"], gates=ins["L0_ffn_gates"], wq=ins["q_proj_t"],
        wk=ins["k_proj_t"], wv=ins["v_proj_t"], wo=ins["o_proj"], out=out, eye=ins["eye"],
        causal=ins["causal"], lower=ins["lower"]))


def kernel(**inputs):
    import numpy as np
    import concourse.bacc as bacc
    from concourse.bass_utils import run_bass_kernel_spmd

    arrays = {name: np.ascontiguousarray(inputs[name]) for name in (
        "x", "L0_attn_Wa", "L0_attn_ba", "L0_attn_We", "L0_attn_be", "L0_attn_Wi", "L0_attn_Wo", "L0_attn_Wv",
        "L0_attn_Wout", "L0_attn_chi", "L0_attn_beta_p", "L0_attn_iv_p", "L0_attn_ov_p", "L0_xattn_bq",
        "L0_xattn_bk", "L0_xattn_bv", "L0_xattn_bo", "L0_ffn_sim_matrix", "L0_ffn_gates")}
    arrays["x_t"] = turned(inputs["x"], (0, 2, 1))
    arrays["ctx_t"] = turned(inputs["ctx_1024"], (0, 2, 1))
    arrays["mask"] = np.ascontiguousarray(inputs["mask_BxSxS2_ik1"])
    arrays["mask_t"] = turned(inputs["mask_BxSxS2_ik1"], (0, 2, 1))
    for name in ("Wq", "Wk", "Wv", "Wo"):
        arrays[f"{name}_t"] = turned(inputs[f"L0_xattn_{name}"], (1, 0))
    arrays["Wout_swapped"] = np.ascontiguousarray(
        np.asarray(inputs["L0_attn_Wout"]).reshape(H, 2, DH // 2, D)[:, ::-1].reshape(D, D))
    for name in ("q_proj", "k_proj", "v_proj"):
        arrays[f"{name}_t"] = turned(inputs[f"L0_ffn_{name}"], (1, 0, 2)).reshape(D, WIDE)
    arrays["o_proj"] = np.ascontiguousarray(inputs["L0_ffn_o_proj"]).reshape(WIDE, D)
    arrays.update(constants())
    nc = bacc.Bacc("TRN2", target_bir_lowering=False, num_devices=1)
    ins = {name: nc.dram_tensor(name, a.shape, mybir.dt.from_np(a.dtype), kind="ExternalInput").ap()
           for name, a in arrays.items()}
    out = nc.dram_tensor("out", (B, S, D), F32, kind="ExternalOutput").ap()
    program(nc, ins, out)
    result = run_bass_kernel_spmd(nc, [arrays], core_ids=[0])
    return result.results[0]["out"]
```

```python
import math
from contextlib import ExitStack

import concourse.bass as bass
from concourse import mybir

P = 128
B, S, D, H = 4, 1024, 512, 16
DH = D // H
KT = D // P
TT = S // P
CH = 512
NC_ = S // CH
HALF = TT // NC_
PAIRS = H // 2
VW = DH + 2
EPS = 1e-5
SCALE = DH ** -0.5
MASKED = -57344.0 * 16384.0
ABSENT = -1e8
STACK_DMAS = 6
SLOTS = 3
PRING = 4

ALU = mybir.AluOpType
ACT = mybir.ActivationFunctionType
AX = mybir.AxisListType
F32 = mybir.dt.float32
F32R = mybir.dt.float32r
BF16 = mybir.dt.bfloat16
FP8 = mybir.dt.float8e5
I32 = mybir.dt.int32


def attention_steps(masked):
    smax = lambda p: [("smax", p, h, t, c) for h in range(2) for t in range(TT) for c in range(NC_)]
    steps = [("Q", g, c) for g in range(KT) for c in range(NC_)]
    steps += [("K", 0, c) for c in range(NC_)]
    rest = [] if masked else [("EX", c) for c in range(NC_)]
    rest += [("K", g, c) for g in range(1, KT) for c in range(NC_)]
    rest += [] if masked else [("AP",)]
    rest += [("V", t) for t in range(TT)]
    first = smax(0)
    lead = 6
    every = -(-len(first) // (len(rest) - lead - 1))
    for n, step in enumerate(rest):
        if n == len(rest) - 1:
            steps += first + [("mneg", 0)]
        steps.append(step)
        if n >= lead:
            steps += first[:every]
            first = first[every:]
    if masked:
        steps.append(("CS",))

    GAPS = 4
    ahead = [m for p in range(1, PAIRS) for m in smax(p)]
    left = 0
    due = []
    for p in range(PAIRS):
        extra = {}
        if p > 0:
            extra[7] = [("den", p - 1)]
            extra[11] = [("bc", p - 1, 0)]
            extra[13] = [("bc", p - 1, 1)]
        if masked and p == 2:
            extra[15] = [("RZ",)]
        if not masked:
            extra[20] = [("apx", p, 0)]
            extra[22] = [("apx", p, 1)]
        for kt in range(TT):
            before = (p, kt - 1) if kt else (p - 1, TT - 1)
            work = [("st", p, kt, h) for h in range(2)] + [("pv", *before, c) for c in range(NC_)]
            for g in range(GAPS):
                if work[g][1] >= 0:
                    steps.append(work[g])
                n = GAPS * kt + g
                steps += extra.get(n, [])
                if due:
                    left += 1
                    if left >= 3:
                        steps.append(due.pop(0))
                        left = 0
                rate = (0 if n < GAPS else 2 if n % 2 else 1) if p == 0 else 1
                for _ in range(rate):
                    if ahead:
                        m = ahead.pop(0)
                        steps.append(m)
                        if m[2:] == (1, TT - 1, NC_ - 1):
                            due.append(("mneg", m[1]))
                            left = 0
    assert not ahead and not due
    steps += [("pv", PAIRS - 1, TT - 1, c) for c in range(NC_)]
    steps += [("den", PAIRS - 1)] + [("bc", PAIRS - 1, c) for c in range(NC_)]
    steps += [("out", t) for t in range(TT)]
    steps += [("xt", t) for t in range(TT)]
    if sum(s[0] not in ("st", "pv") for s in steps) % 2:
        steps.append(("pad",))
    return steps


def attention(nc, masked, io):
    steps = attention_steps(masked)
    uses = [s for s in steps if s[0] not in ("st", "pv")]
    PER = len(uses) // 2
    use_no = {s: n for n, s in enumerate(uses)}
    pair_slots = [[p for p in range(PAIRS) if p % SLOTS == s] for s in range(SLOTS)]

    ctx = ExitStack()
    with ctx:
        used = [0]
        base = nc.sbuf_base
        size = nc.sbuf_bytes_remaining // 64 * 64
        ctx.enter_context(nc.sbuf_tensor(f"arena{int(masked)}", [P, size], mybir.dt.uint8))
        start = -(-base // 64) * 64
        wide = {F32: 4, F32R: 4, BF16: 2, FP8: 1, I32: 4}

        def sb(name, shape, dt=F32, at=None):
            n = wide[dt]
            for k in shape[1:]:
                n *= k
            if at is None:
                at = start + used[0]
                used[0] += -(-n // 64) * 64
                assert used[0] + 64 <= size, (name, used[0], size)
            t = nc.alloc_sbuf_tensor_at(f"{name}_{int(masked)}", shape, dt, offset=at)
            place[name] = at
            return t

        place = {}
        sem = lambda n: ctx.enter_context(nc.semaphore(f"{n}_{int(masked)}"))

        stack = sb("stack", [P, SLOTS, 4, S], F32R)
        x_hi = stack[:, 1, :, :]
        x_lo = stack[:, 2, :, :]
        q_raw = sb("q_raw", [P, KT, S])
        k_raw = sb("k_raw", [P, KT, S])
        y = k_raw[:, :, :].rearrange("p g (a d) -> p (g a) d", d=D)
        qk = sb("qk", [P, 4, S], F32R)
        v_ext = sb("v_ext", [P, TT, H, VW])
        w0 = sb("w0", [P, 2, KT, D], F32R)
        probs = sb("probs", [P, PRING, S])
        w1 = sb("w1", [P, 2, KT, D], F32R, at=place["probs"])
        stage = sb("stage", [P, 2, S])
        u = sb("u", [P, NC_, CH])
        r = sb("r", [P, TT, 2])
        eye = sb("eye", [P, P])
        neg_eye = sb("neg_eye", [P, P])
        sel_den = sb("sel_den", [P, 2])
        mx = sb("mx", [P, 2, 2 * TT * NC_])
        mm = sb("mm", [P, 2 * TT])
        mrow = sb("mrow", [2 * TT, P], F32R)
        stats = sb("stats", [P, 6])
        mv = sb("mv", [P, TT, 2])
        sd = sb("sd", [P, TT])
        rstd = sb("rstd", [P, TT])
        tmp = sb("tmp", [P, TT])
        xts = sb("xts", [P, KT, S], at=place["qk"])
        if masked:
            mask_q = sb("mask_q", [P, TT, S], BF16)
            mask_k = sb("mask_k", [P, TT, S], FP8)
            mstage = sb("mstage", [P, 2, CH], I32)
            eye8 = sb("eye8", [P, P], FP8)
            bq = sb("bq", [P, KT])
            bk = sb("bk", [P, KT])
            bv = sb("bv", [P, D])
            bo = sb("bo", [P, D])
            ones = sb("ones", [P, 1])
            none = sb("none", [P, TT])
            vmean = sb("vmean", [P, KT])
            vm = sb("vm", [P, 2, KT, P], F32R)
            rz = sb("rz", [P, D])
        else:
            apx = sb("apx", [P, NC_, CH])
            wsm_raw = sb("wsm_raw", [P, KT, 2 * H])
            wsm = sb("wsm", [P, 2, KT, 2 * H], F32R)
            bsm = sb("bsm", [2 * H, 1])
            gate = sb("gate", [P, TT, H])
            gate_t = sb("gate_t", [2 * H + 1, S])
            sel_ap = sb("sel_ap", [2 * H + 1, PAIRS, P])
            turn_in = sb("turn_in", [P, 4, KT])
            turn = sb("turn", [P, 8, KT])
            sign = sb("sign", [P, 1])
            half_pi = sb("half_pi", [P, 1])

        psum = lambda n, shape: ctx.enter_context(nc.psum_tensor(f"{n}_{int(masked)}", shape, F32))
        work = [psum(f"work{b}", [P, CH]) for b in range(2)]
        scores = [psum(f"scores{b}", [P, S]) for b in range(2)]
        acc = psum("acc", [P, NC_, CH])

        const_in = sem("const_in")
        turn_sem = sem("turn_sem")
        setup = sem("setup")
        apart = sem("apart")
        work_full = [sem(f"work_full{b}") for b in range(2)]
        work_free = [sem(f"work_free{b}") for b in range(2)]
        stage_full = [sem(f"stage_full{b}") for b in range(2)]
        stage_free = sem("stage_free")
        hi_split = sem("hi_split")
        chunk_ready = sem("chunk_ready")
        proj_done = sem("proj_done")
        group_split = sem("group_split")
        ones_set = sem("ones_set")
        stacked = [sem(f"stacked{s}") for s in range(SLOTS)]
        mrow_ready = sem("mrow_ready")
        mrow_in = [sem(f"mrow_in{s}") for s in range(SLOTS)]
        st_full = sem("st_full")
        p_full = sem("p_full")
        pv_done = sem("pv_done")
        u_ready = sem("u_ready")
        r_ready = sem("r_ready")
        ctx_done = sem("ctx_done")
        mm_ready = sem("mm_ready")
        res_in = sem("res_in")
        res_ready = sem("res_ready")
        ct_split = sem("ct_split")
        out_done = sem("out_done")
        y_done = sem("y_done")
        var_ready = sem("var_ready")
        sd_ready = sem("sd_ready")
        x_ready = sem("x_ready")
        stored = sem("stored")
        xt_ready = sem("xt_ready")
        xt_stored = sem("xt_stored")
        if masked:
            mstage_full = [sem(f"mstage_full{b}") for b in range(2)]
            mstage_free = sem("mstage_free")
            maskq_ready = sem("maskq_ready")
            maskk_ready = sem("maskk_ready")
            vm_ready = sem("vm_ready")
            rz_ready = sem("rz_ready")
            bo_added = sem("bo_added")
        else:
            gate_sum = sem("gate_sum")
            gate_exp = sem("gate_exp")
            gate_ready = sem("gate_ready")
            apx_ready = sem("apx_ready")

        chunks = [("x", k) for k in range(KT)] + [("wq", 0), ("wq", 1), ("wk", 0), ("wk", 1)]
        if masked:
            chunks += [("x2", k) for k in range(KT)]
        before_group0 = len(chunks)
        shared = ("wq", "x2")
        chunks += [("wv", 0), ("wv", 1), ("wo", 0), ("wo", 1)]
        NCH = len(chunks)
        upto = lambda what: max(n for n, c in enumerate(chunks) if c[0] == what) + 1

        def chunk_parts(what, k):
            if what in ("x", "x2"):
                return x_hi[:, k, :], x_lo[:, k, :]
            w = w1 if what in ("wq", "wv") else w0
            half = lambda part: w[:, part, 2 * k:2 * k + 2, :].rearrange("p k n -> p (k n)")
            return half(0), half(1)

        def wait_full(eng, i, step):
            n = use_no[step]
            eng.wait_ge(work_full[n % 2], i * PER + n // 2 + 1)
            return work[n % 2], work_free[n % 2]

        def alone(eng):
            eng.sem_inc(apart, 1)

        def chunks_of(what):
            return [n for n in range(NCH) if chunks[n][0] == what]

        SHARED = len([c for c in chunks if c[0] in shared])

        def nth_in_slot(n):
            return len([m for m in range(n + 1) if m % 2 == n % 2])

        def wait_place(eng, i, what):
            if what == "wq":
                eng.wait_ge(pv_done, 1 + i * PAIRS * TT)
            else:
                eng.wait_ge(proj_done, 1 + i * 4 + 1)
            eng.wait_ge(chunk_ready, i * NCH + chunks_of(what)[0])

        block = ctx.enter_context(nc.Block(f"layer{int(masked)}"))

        @block.sync
        def _(sp):
            consts = [(eye, io["eye"]), (neg_eye, io["neg_eye"]), (sel_den, io["sel_den"])]
            for t, src in consts:
                sp.dma_start(t[:, :], src).then_inc(const_in, 16)
            if masked:
                sp.dma_start(bq[:, :], io["bq"].rearrange("(g p) -> p g", p=P),
                             allow_slow_non_contiguous=True).then_inc(const_in, 16)
                sp.dma_start(bk[:, :], io["bk"].rearrange("(g p) -> p g", p=P),
                             allow_slow_non_contiguous=True).then_inc(const_in, 16)
                sp.dma_start(bv[:, :], io["bv"].partition_broadcast(P)).then_inc(const_in, 16)
                sp.dma_start(bo[:, :], io["bo"].partition_broadcast(P)).then_inc(const_in, 16)
            else:
                sp.dma_start(sel_ap[:, :, :], io["sel_ap"]).then_inc(const_in, 16)
                sp.dma_start(wsm_raw[:, :, 0:H], io["wa"].rearrange("(k p) h -> p k h", p=P)).then_inc(const_in, 16)
                sp.dma_start(wsm_raw[:, :, H:2 * H], io["we"].rearrange("(k p) h -> p k h", p=P)).then_inc(const_in, 16)
                for n, name in enumerate(("ba", "be")):
                    sp.dma_start(bsm[n * H:(n + 1) * H, :], io[name].rearrange("(h a) -> h a", a=1),
                                 allow_slow_non_contiguous=True).then_inc(const_in, 16)
                for n, src in enumerate((io["wo"], io["wo_swapped"])):
                    sp.dma_start(q_raw[:, 2 * n:2 * n + 2, :].rearrange("p g (a d) -> p (g a) d", d=D),
                                 src.rearrange("(k p) d -> p k d", p=P)).then_inc(const_in, 16)
                for n, name in enumerate(("beta", "iv", "ov", "chi")):
                    for q in range(4):
                        sp.dma_start(turn_in[DH * q:DH * (q + 1), n, :],
                                     io[name].rearrange("(k q) -> q k", q=4)[q, :].partition_broadcast(DH),
                                     allow_slow_non_contiguous=True).then_inc(const_in, 16)
                sp.dma_start(sign[:, :], io["sign"]).then_inc(const_in, 16)
                sp.wait_ge(turn_sem, 5)
                sp.dma_start(io["wo_turned"].rearrange("(k p) d -> p k d", p=P), y[:, 0:KT, :])\
                  .then_inc(turn_sem, 16)
                sp.wait_ge(turn_sem, 21)
            sp.wait_ge(setup, 3)
            with sp.Fori(0, B) as i:
                def load_chunk(n):
                    what, k = chunks[n]
                    sp.wait_ge(stage_free, 1 + i * NCH + max(n - 1, 0))
                    alone(sp)
                    if what in ("x", "x2"):
                        src = io["q_src"] if what == "x" else io["kv_src"]
                        src = src[bass.ds(i, 1), k * P:(k + 1) * P, :].rearrange("b p s -> (b p) s")
                        dst = stage[:, n % 2, :]
                    else:
                        name = "wo_turned" if what == "wo" and not masked else what
                        src = io[name][2 * k * P:(2 * k + 2) * P, :].rearrange("(k p) n -> p k n", p=P)
                        dst = stage[:, n % 2, :].rearrange("p (k n) -> p k n", k=2)
                    sp.dma_start(dst, src).then_inc(stage_full[n % 2], 16)

                def stack_pair(p):
                    s = p % SLOTS
                    sp.wait_ge(group_split, i * KT + p // 2 + 1)
                    alone(sp)
                    if p >= SLOTS:
                        sp.wait_ge(st_full, 1 + i * H * TT + 2 * TT * (p - SLOTS + 1))
                    elif p > 0:
                        sp.wait_ge(proj_done, 1 + i * 4 + 3)
                    alone(sp)
                    for h in range(2):
                        a = DH * ((2 * p + h) % 4)
                        for j, (first, step) in enumerate(((0, 2), (1, 1), (0, 3))):
                            sp.dma_start(stack[DH * j:DH * (j + 1), s, h:h + 3:2, :].bitcast(F32),
                                         qk[a:a + DH, first:first + step + 1:step, :].bitcast(F32))\
                              .then_inc(stacked[s], 16)

                def max_row(p):
                    sp.wait_ge(mrow_ready, i * PAIRS + p + 1)
                    alone(sp)
                    sp.dma_start(stack[3 * DH:3 * DH + 1, p % SLOTS, 0:2, :].bitcast(F32),
                                 mrow[:, :].bitcast(F32)).then_inc(mrow_in[p % SLOTS], 16)

                for n in range(NCH - 2):
                    load_chunk(n)
                stack_pair(0)
                stack_pair(1)
                max_row(0)
                for n in range(NCH - 2, NCH):
                    load_chunk(n)
                stack_pair(2)
                max_row(1)
                for p in range(1, PAIRS):
                    if p + 2 < PAIRS and p > 0:
                        stack_pair(p + 2)
                    if p + 1 < PAIRS and p > 0:
                        max_row(p + 1)
                    if p == 5:
                        sp.wait_ge(group_split, i * KT + KT)
                        alone(sp)
                        sp.dma_start(y, io["res"][bass.ds(i, 1), :, :].rearrange("b (t p) d -> p (b t) d", p=P))\
                          .then_inc(res_in, 16)

        @block.gpsimd
        def _(pool):
            def split(raw, hi, lo):
                pool.tensor_scalar(hi, raw, 1.0, 0.0, ALU.mult, ALU.add)
                pool.drain()
                return pool.tensor_tensor(lo, raw, hi.bitcast(F32), ALU.subtract)

            pool.memset(stack[3 * DH:3 * DH + 1, 0, 2:4, :].bitcast(F32), 1.0)
            pool.drain()
            if not masked:
                pool.wait_ge(const_in, 16 * 27)
                split(wsm_raw[:, :, :], wsm[:, 0, :, :], wsm[:, 1, :, :])
                pool.drain()
            for count in (*work_free, stage_free, ct_split, stored, proj_done, pv_done, st_full, out_done, u_ready,
                          xt_stored, *([mstage_free] if masked else [])):
                pool.sem_inc(count, 1)
            pool.drain().then_inc(setup, 1)
            with pool.Fori(0, B) as i:
                def split_chunk(n):
                    what, k = chunks[n]
                    if what in shared:
                        return
                    hi, lo = chunk_parts(what, k)
                    if what == "x" and k == 0:
                        pool.wait_ge(st_full, 1 + i * H * TT)
                    if what == "wk" and k == 0:
                        pool.wait_ge(proj_done, 1 + i * 4)
                        pool.wait_ge(chunk_ready, i * NCH + upto("wq"))
                    if what == "wv" and k == 0:
                        pool.wait_ge(proj_done, 1 + i * 4 + 1)
                    if what == "wo" and k == 0:
                        pool.wait_ge(proj_done, 1 + i * 4 + 2)
                    pool.wait_ge(stage_full[n % 2], (i * (NCH // 2) + nth_in_slot(n)) * 16)
                    alone(pool)
                    split(stage[:, n % 2, :], hi, lo).then_inc(stage_free, 1)
                    pool.drain()
                    pool.engine_nop().then_inc(chunk_ready, 1)

                def split_group(g):
                    if g > 0:
                        for p in (2 * g - 2, 2 * g - 1):
                            s = p % SLOTS
                            pool.wait_ge(stacked[s], (i * len(pair_slots[s]) + pair_slots[s].index(p) + 1) * STACK_DMAS * 16)
                    else:
                        for step in [("Q", 0, c) for c in range(NC_)] + [("K", 0, c) for c in range(NC_)]:
                            n = use_no[step]
                            pool.wait_ge(work_free[n % 2], 1 + i * PER + n // 2 + 1)
                    if g == 1:
                        for c in range(NC_):
                            n = use_no[("K", KT - 1, c)]
                            pool.wait_ge(work_free[n % 2], 1 + i * PER + n // 2 + 1)
                    if g == 0:
                        pool.wait_ge(out_done, 1 + i * TT)
                        pool.wait_ge(xt_stored, 1 + i * NC_ * 16)
                    alone(pool)
                    split(q_raw[:, g, :], qk[:, 0, :], qk[:, 1, :])
                    pool.drain()
                    split(k_raw[:, g, :], qk[:, 2, :], qk[:, 3, :])
                    pool.drain()
                    pool.engine_nop().then_inc(group_split, 1)

                for n in range(before_group0):
                    split_chunk(n)
                split_group(0)
                for n in range(before_group0, NCH - 2):
                    split_chunk(n)
                pool.wait_ge(proj_done, 1 + i * 4 + 3)
                alone(pool)
                for s in range(1, SLOTS):
                    pool.memset(stack[3 * DH:3 * DH + 1, s, 2:4, :].bitcast(F32), 1.0)
                    pool.drain()
                pool.engine_nop().then_inc(ones_set, 1)
                split_group(1)
                for n in range(NCH - 2, NCH):
                    split_chunk(n)
                for g in range(2, KT):
                    split_group(g)
                if masked:
                    pool.wait_ge(const_in, 16 * 7)
                    pool.wait_ge(res_in, i * 16 + 16)
                    for t in range(TT):
                        pool.tensor_tensor(y[:, t, :], y[:, t, :], bo[:, :], ALU.add)
                        pool.drain()
                    pool.engine_nop().then_inc(bo_added, 1)
                for t in range(TT):
                    if t == 0:
                        for s in range(SLOTS):
                            pool.wait_ge(stacked[s], (i + 1) * len(pair_slots[s]) * STACK_DMAS * 16)
                    if t % (TT // NC_) == 0:
                        pool.wait_ge(ctx_done, i * NC_ + t // (TT // NC_) + 1)
                    if t >= 4:
                        pool.wait_ge(out_done, 1 + i * TT + t - 3)
                    alone(pool)
                    part = lambda k: qk[:, t % 4, k * D:(k + 1) * D].rearrange("p (g n) -> p g n", g=KT)
                    split(q_raw[:, :, t * P:(t + 1) * P], part(0), part(1)).then_inc(ct_split, 1)
                    pool.drain()

        @block.tensor
        def _(pe):
            pe.wait_ge(setup, 3)
            pe.wait_ge(const_in, 16 * (7 if masked else 27))
            with pe.Fori(0, B) as i:
                def parts(out, hi_l, lo_l, hi_r, lo_r):
                    for k in range(KT):
                        for n, (a, b) in enumerate(((hi_l, hi_r), (hi_l, lo_r), (lo_l, hi_r))):
                            last = pe.matmul(out, a(k), b(k), start=(k == 0 and n == 0),
                                             stop=(k == KT - 1 and n == 2))
                    return last

                def smax_ready(p):
                    s = p % SLOTS
                    pe.wait_ge(stacked[s], (i * len(pair_slots[s]) + pair_slots[s].index(p) + 1) * STACK_DMAS * 16)

                for step in steps:
                    kind = step[0]
                    if kind == "st":
                        _, p, kt, h = step
                        s = p % SLOTS
                        if kt == 0 and h == 0:
                            pe.wait_ge(mrow_in[s], (i * len(pair_slots[s]) + pair_slots[s].index(p) + 1) * 16)
                            if p == 1:
                                pe.wait_ge(ones_set, i + 1)
                            if p == 0 and masked:
                                pe.wait_ge(maskk_ready, i + 1)
                        n = 2 * (p * TT + kt) + h
                        if n >= 2:
                            pe.wait_ge(p_full, i * H * TT + n - 1)
                        for c in range(NC_):
                            last = pe.matmul(scores[n % 2][:, c * CH:(c + 1) * CH],
                                             stack[0:3 * DH + 1, s, 2 + h, kt * P:(kt + 1) * P],
                                             stack[0:3 * DH + 1, s, h, c * CH:(c + 1) * CH],
                                             start=True, stop=not masked)
                            if masked:
                                last = pe.matmul(scores[n % 2][:, c * CH:(c + 1) * CH], eye8[:, :],
                                                 mask_k[:, kt, c * CH:(c + 1) * CH], start=False, stop=True)
                        last.then_inc(st_full, 1)
                        continue
                    if step in (("CS",), ("pv", 0, 0, 0)):
                        for t in (TT - 2, TT - 1):
                            n = use_no[("V", t)]
                            pe.wait_ge(work_free[n % 2], 1 + i * PER + n // 2 + 1)
                    if kind == "pv":
                        _, p, kt, c = step
                        if c == 0:
                            pe.wait_ge(p_full, i * H * TT + 2 * (p * TT + kt) + 2)
                            if kt == 0:
                                pe.wait_ge(u_ready, 1 + (i * PAIRS + p) * NC_)
                        for h in range(2):
                            n = 2 * (p * TT + kt) + h
                            last = pe.matmul(acc[64 * h:64 * h + VW, c, :], v_ext[:, kt, 2 * p + h, :],
                                             probs[:, n % PRING, c * CH:(c + 1) * CH],
                                             start=(kt == 0), stop=(kt == TT - 1), skip_group_check=True)
                        if c == NC_ - 1:
                            last.then_inc(pv_done, 1)
                        continue
                    n = use_no[step]
                    bank = work[n % 2]
                    pe.wait_ge(work_free[n % 2], 1 + i * PER + n // 2)
                    if kind in ("Q", "K"):
                        _, g, c = step
                        w = w1 if kind == "Q" else w0
                        if g == 0 and c == 0:
                            pe.wait_ge(chunk_ready, i * NCH + (upto("wq") if kind == "Q" else
                                                               before_group0))
                        last = parts(bank[:, :], lambda k: w[:, 0, k, g * P:(g + 1) * P],
                                     lambda k: w[:, 1, k, g * P:(g + 1) * P],
                                     lambda k: x_hi[:, k, c * CH:(c + 1) * CH],
                                     lambda k: x_lo[:, k, c * CH:(c + 1) * CH])
                    elif kind == "V":
                        t = step[1]
                        if t == 0:
                            pe.wait_ge(chunk_ready, i * NCH + upto("wv"))
                        last = parts(bank[:, :], lambda k: x_hi[:, k, t * P:(t + 1) * P],
                                     lambda k: x_lo[:, k, t * P:(t + 1) * P],
                                     lambda k: w1[:, 0, k, :], lambda k: w1[:, 1, k, :])
                    elif kind == "EX":
                        c = step[1]
                        last = parts(bank[0:2 * H, :], lambda k: wsm[:, 0, k, :], lambda k: wsm[:, 1, k, :],
                                     lambda k: x_hi[:, k, c * CH:(c + 1) * CH],
                                     lambda k: x_lo[:, k, c * CH:(c + 1) * CH])
                    elif kind == "AP":
                        pe.wait_ge(gate_ready, (i + 1) * NC_)
                        for t in range(TT):
                            last = pe.matmul(bank[:, t * H:(t + 1) * H], gate_t[0:2 * H, t * P:(t + 1) * P],
                                             eye[0:2 * H, H:2 * H], start=True, stop=True)
                    elif kind == "smax":
                        _, p, h, t, c = step
                        if h == 0 and t == 0 and c == 0:
                            smax_ready(p)
                        s = p % SLOTS
                        last = pe.matmul(bank[:, :], stack[0:3 * DH, s, h, t * P:(t + 1) * P],
                                         stack[0:3 * DH, s, 2 + h, c * CH:(c + 1) * CH], start=True, stop=True)
                    elif kind == "mneg":
                        pe.wait_ge(mm_ready, i * PAIRS + step[1] + 1)
                        last = pe.matmul(bank[0:2 * TT, 0:P], mm[:, :], neg_eye[:, :], start=True, stop=True)
                    elif kind == "apx":
                        _, p, c = step
                        last = pe.matmul(bank[:, :], sel_ap[:, p, :], gate_t[:, c * CH:(c + 1) * CH],
                                         start=True, stop=True)
                    elif kind == "den":
                        p = step[1]
                        pe.wait_ge(u_ready, 1 + (i * PAIRS + p + 1) * NC_)
                        for t in range(TT):
                            at = t * P % CH
                            last = pe.matmul(bank[:, 2 * t:2 * t + 2], u[:, t * P // CH, at:at + P], sel_den[:, :],
                                             start=True, stop=True)
                    elif kind == "bc":
                        _, p, c = step
                        pe.wait_ge(r_ready, i * PAIRS + p + 1)
                        for t in range(TT // NC_):
                            for h in range(2):
                                last = pe.matmul(bank[64 * h:64 * h + DH, t * P:(t + 1) * P],
                                                 r[:, c * (TT // NC_) + t, h:h + 1].to_broadcast([P, DH]),
                                                 eye[:, :], start=True, stop=True)
                    elif kind == "CS":
                        for h in range(H):
                            a = DH * (h % 4)
                            for t in range(TT):
                                last = pe.matmul(bank[a:a + DH, h // 4:h // 4 + 1], v_ext[:, t, h, 0:DH],
                                                 ones[:, :], start=(t == 0), stop=(t == TT - 1))
                    elif kind == "RZ":
                        pe.wait_ge(vm_ready, i + 1)
                        pe.wait_ge(chunk_ready, i * NCH + upto("wo"))
                        last = parts(bank[:, :], lambda k: vm[:, 0, k, :], lambda k: vm[:, 1, k, :],
                                     lambda k: w0[:, 0, k, :], lambda k: w0[:, 1, k, :])
                    elif kind == "out":
                        t = step[1]
                        if t == 0:
                            pe.wait_ge(chunk_ready, i * NCH + upto("wo"))
                        pe.wait_ge(ct_split, 1 + i * TT + t + 1)
                        last = parts(bank[:, :], lambda k: qk[:, t % 4, k * P:(k + 1) * P],
                                     lambda k: qk[:, t % 4, D + k * P:D + (k + 1) * P],
                                     lambda k: w0[:, 0, k, :], lambda k: w0[:, 1, k, :])
                    elif kind == "xt":
                        t = step[1]
                        if t % HALF == 0:
                            pe.wait_ge(x_ready, i * TT + t + HALF)
                        for k in range(KT):
                            last = pe.transpose(bank[:, k * P:(k + 1) * P], y[:, t, k * P:(k + 1) * P], eye[:, :])
                    elif kind == "pad":
                        last = pe.matmul(bank[0:2 * TT, 0:P], mm[:, :], neg_eye[:, :], start=True, stop=True)
                    last.then_inc(work_full[n % 2], 1)
                    if step in (("Q", KT - 1, NC_ - 1), ("K", KT - 1, NC_ - 1), ("V", TT - 1), ("out", TT - 1)):
                        pe.drain().then_inc(proj_done, 1)
                    if kind == "out":
                        pe.drain().then_inc(out_done, 1)

        @block.scalar
        def _(act):
            act.wait_ge(const_in, 16 * (7 if masked else 27))
            if not masked:
                act.wait_ge(turn_sem, 1)
                act.activation(turn[:, 0:3, :], turn_in[:, 0:3, :], ACT.Exp, scale=-1.0)
                act.activation(turn[:, 3, :], turn_in[:, 3, :], ACT.Tanh)
                act.drain().then_inc(turn_sem, 1)
                act.wait_ge(turn_sem, 3)
                act.activation(turn[:, 4, :], turn[:, 0, :], ACT.Sin, scale=math.pi)
                act.activation(turn[:, 5, :], turn[:, 0, :], ACT.Sin, scale=-math.pi, bias=half_pi[:, 0:1])
                act.drain().then_inc(turn_sem, 1)
            with act.Fori(0, B) as i:
                def split_hi(what):
                    wait_place(act, i, what)
                    alone(act)
                    for n in chunks_of(what):
                        act.wait_ge(stage_full[n % 2], (i * (NCH // 2) + nth_in_slot(n)) * 16)
                        act.activation(chunk_parts(*chunks[n])[0], stage[:, n % 2, :], ACT.Copy).then_inc(hi_split, 1)

                def load_mask_pieces(src, pieces):
                    for n in pieces:
                        t, c = n // NC_ % TT, n % NC_
                        act.wait_ge(mstage_free, 1 + i * 2 * NC_ * TT + max(n - 1, 0))
                        alone(act)
                        act.dma_start(mstage[:, n % 2, :],
                                      src[bass.ds(i, 1), t * P:(t + 1) * P, c * CH:(c + 1) * CH]
                                      .rearrange("b p s -> (b p) s")).then_inc(mstage_full[n % 2], 16)

                for step in steps:
                    kind = step[0]
                    if step == ("Q", 0, 0):
                        split_hi("wq")
                    if step == ("K", 0, 0) and masked:
                        split_hi("x2")
                    if kind in ("Q", "K"):
                        _, g, c = step
                        if masked:
                            piece = 2 * (NC_ * g + c) + (0 if kind == "Q" else NC_ * TT)
                            load_mask_pieces(io["mask_q"] if kind == "Q" else io["mask_k"], (piece, piece + 1))
                        bank, free = wait_full(act, i, step)
                        if g == 0 and c == 0:
                            if kind == "Q":
                                act.wait_ge(ct_split, 1 + i * TT)
                            else:
                                act.wait_ge(stored, 1 + i * 16)
                        dst = (q_raw if kind == "Q" else k_raw)[:, g, c * CH:(c + 1) * CH]
                        if masked:
                            bias = (bq if kind == "Q" else bk)[:, g:g + 1]
                            act.activation(dst, bank[:, :], ACT.Identity, bias=bias).then_inc(free, 1)
                        else:
                            act.activation(dst, bank[:, :], ACT.Copy).then_inc(free, 1)
                    elif kind == "EX":
                        c = step[1]
                        act.wait_ge(gate_sum, i * NC_ + c + 1)
                        z = gate_t[0:2 * H, c * CH:(c + 1) * CH]
                        act.activation(z, z, ACT.Exp, scale=-1.0).then_inc(gate_exp, 1)
                    elif kind == "mneg":
                        bank, free = wait_full(act, i, step)
                        p = step[1]
                        if p > 0:
                            s = (p - 1) % SLOTS
                            act.wait_ge(mrow_in[s], (i * len(pair_slots[s]) + pair_slots[s].index(p - 1) + 1) * 16)
                        act.activation(mrow[:, :], bank[0:2 * TT, 0:P], ACT.Copy).then_inc(free, 1)
                        act.drain().then_inc(mrow_ready, 1)
                    elif kind == "apx":
                        bank, free = wait_full(act, i, step)
                        _, p, c = step
                        act.wait_ge(u_ready, 1 + (i * PAIRS + p) * NC_)
                        act.activation(apx[:, c, :], bank[:, :], ACT.Copy).then_inc(free, 1)
                        act.drain().then_inc(apx_ready, 1)
                    elif kind == "RZ":
                        bank, free = wait_full(act, i, step)
                        act.activation(rz[:, :], bank[:, :], ACT.Copy).then_inc(free, 1)
                        act.drain().then_inc(rz_ready, 1)
                    elif kind == "pad":
                        bank, free = wait_full(act, i, step)
                        alone(act)
                        act.drain().then_inc(free, 1)
                    elif kind == "st":
                        _, p, kt, h = step
                        n = 2 * (p * TT + kt) + h
                        act.wait_ge(st_full, 1 + i * H * TT + n + 1)
                        if n >= PRING:
                            act.wait_ge(pv_done, 1 + i * PAIRS * TT + p * TT + kt - PRING // 2 + 1)
                        act.activation(probs[:, n % PRING, :], scores[n % 2][:, :], ACT.Exp,
                                       scale=SCALE).then_inc(p_full, 1)
                    elif kind == "xt":
                        t = step[1]
                        if t == 0:
                            for c in range(NC_):
                                half = slice(c * HALF, (c + 1) * HALF)
                                act.wait_ge(var_ready, i * NC_ + c + 1)
                                act.activation(sd[:, half], tmp[:, half], ACT.Sqrt).then_inc(sd_ready, 1)
                        if t == TT - 1:
                            act.wait_ge(x_ready, i * TT + TT)
                            alone(act)
                            act.dma_start(io["out"][bass.ds(i, 1), :, :].rearrange("b (t p) d -> p (b t) d", p=P), y)\
                               .then_inc(stored, 16)
                        bank, free = wait_full(act, i, step)
                        act.activation(xts[:, :, t * P:(t + 1) * P], bank[:, :].rearrange("p (k n) -> p k n", k=KT),
                                       ACT.Copy).then_inc(free, 1)
                        if t % HALF == HALF - 1:
                            c = t // HALF
                            act.drain().then_inc(xt_ready, 1)
                            act.wait_ge(xt_ready, i * NC_ + c + 1)
                            act.dma_start(io["out_t"][bass.ds(i, 1), :, c * CH:(c + 1) * CH]
                                          .rearrange("b (k p) s -> p (b k) s", p=P), xts[:, :, c * CH:(c + 1) * CH])\
                               .then_inc(xt_stored, 16)
            act.wait_ge(stored, 1 + B * 16)
            act.wait_ge(xt_stored, 1 + B * NC_ * 16)

        @block.vector
        def _(dve):
            dve.memset(acc[:, :, :], 1e-30 if masked else 0.0).then_inc(setup, 1)
            dve.wait_ge(const_in, 16 * (7 if masked else 27))
            if masked:
                dve.memset(ones[:, :], 1.0)
                dve.memset(v_ext[:, :, :, DH:VW], 1.0)
                dve.tensor_scalar(eye8[:, :], eye[:, :], 16384.0, None, ALU.mult, saturate=False)
            else:
                dve.memset(v_ext[:, :, :, DH + 1:VW], 1.0)
                dve.memset(gate_t[2 * H:2 * H + 1, :], 1e-8)
                dve.memset(half_pi[:, :], math.pi / 2)
                dve.tensor_scalar(turn_in[:, 0:3, :], turn_in[:, 0:3, :], -87.0, None, ALU.max)
                dve.drain().then_inc(turn_sem, 1)
                dve.wait_ge(turn_sem, 2)
                dve.tensor_scalar(turn[:, 0:3, :], turn[:, 0:3, :], 1.0, None, ALU.add)
                dve.drain()
                dve.reciprocal(turn[:, 0:3, :], turn[:, 0:3, :])
                dve.drain().then_inc(turn_sem, 1)
                dve.wait_ge(turn_sem, 4)
                dve.tensor_tensor(turn[:, 6, :], turn[:, 1, :], turn[:, 2, :], ALU.mult)
                dve.drain()
                dve.tensor_tensor(turn[:, 6, :], turn[:, 6, :], turn[:, 3, :], ALU.mult)
                dve.drain()
                dve.tensor_tensor(turn[:, 5, :], turn[:, 5, :], turn[:, 6, :], ALU.mult)
                dve.tensor_tensor(turn[:, 7, :], turn[:, 4, :], turn[:, 6, :], ALU.mult)
                dve.drain()
                dve.tensor_scalar(turn[:, 7, :], turn[:, 7, :], sign[:, 0:1], None, ALU.mult)
                dve.drain()
                wo_as_is = q_raw[:, 0:2, :].rearrange("p g (a d) -> p (g a) d", d=D)
                wo_swapped = q_raw[:, 2:4, :].rearrange("p g (a d) -> p (g a) d", d=D)
                for k in range(KT):
                    dve.tensor_scalar(y[:, k, :], wo_as_is[:, k, :], turn[:, 5, k:k + 1], None, ALU.mult)
                dve.drain()
                for k in range(KT):
                    dve.scalar_tensor_tensor(out=y[:, k, :], in0=wo_swapped[:, k, :], scalar=turn[:, 7, k:k + 1],
                                             in1=y[:, k, :], op0=ALU.mult, op1=ALU.add)
                dve.drain().then_inc(turn_sem, 1)
            dve.drain().then_inc(setup, 1)
            with dve.Fori(0, B) as i:
                def take_sums(p):
                    alone(dve)
                    dve.drain()
                    dve.wait_ge(pv_done, 1 + i * PAIRS * TT + (p + 1) * TT)
                    for c in range(NC_):
                        if masked:
                            dve.tensor_copy(u[:, c, :], acc[:, c, :]).then_inc(u_ready, 1)
                        else:
                            dve.wait_ge(apx_ready, (i * PAIRS + p) * NC_ + c + 1)
                            dve.tensor_tensor(u[:, c, :], acc[:, c, :], apx[:, c, :], ALU.mult).then_inc(u_ready, 1)

                def split_lo(what):
                    wait_place(dve, i, what)
                    alone(dve)
                    for j, n in enumerate(chunks_of(what)):
                        hi, lo = chunk_parts(*chunks[n])
                        dve.wait_ge(hi_split, i * SHARED + (len(chunks_of("wq")) if what == "x2" else 0) + j + 1)
                        alone(dve)
                        dve.tensor_tensor(lo, stage[:, n % 2, :], hi.bitcast(F32), ALU.subtract)\
                           .then_inc(stage_free, 1)
                        dve.drain().then_inc(chunk_ready, 1)

                def maxima(p):
                    if p > 0:
                        n = use_no[("mneg", p - 1)]
                        dve.wait_ge(work_full[n % 2], i * PER + n // 2 + 1)
                    alone(dve)
                    dve.drain()
                    m = mx[:, p % 2, :].rearrange("p (n c) -> p n c", c=NC_)
                    if masked:
                        dve.tensor_tensor(mm[:, :], m[:, :, 0], m[:, :, 1], ALU.max)
                        dve.drain()
                        if p == 0:
                            dve.tensor_scalar(none[:, :], mm[:, 0:TT], ABSENT, None, ALU.is_lt)
                            dve.drain()
                        dve.tensor_scalar(mm[:, :], mm[:, :], ABSENT, None, ALU.max).then_inc(mm_ready, 1)
                    else:
                        dve.tensor_tensor(mm[:, :], m[:, :, 0], m[:, :, 1], ALU.max).then_inc(mm_ready, 1)

                for step in steps:
                    kind = step[0]
                    if step == ("Q", 0, 0):
                        split_lo("wq")
                    if step == ("K", 0, 0) and masked:
                        split_lo("x2")
                        dve.wait_ge(st_full, 1 + i * H * TT)
                        alone(dve)
                    if kind in ("Q", "K") and masked:
                        _, g, c = step
                        piece = 2 * (NC_ * g + c) + (0 if kind == "Q" else NC_ * TT)
                        for n in (piece, piece + 1):
                            t, c = n // NC_ % TT, n % NC_
                            dve.wait_ge(mstage_full[n % 2], (i * NC_ * TT + n // 2 + 1) * 16)
                            alone(dve)
                            mask, fill = (mask_q, MASKED) if kind == "Q" else (mask_k, MASKED / 16384.0)
                            dve.tensor_scalar(mask[:, t, c * CH:(c + 1) * CH], mstage[:, n % 2, :], 0, fill,
                                              ALU.is_equal, ALU.mult, saturate=False).then_inc(mstage_free, 1)
                        if step == ("K", KT - 1, NC_ - 1):
                            dve.drain().then_inc(maskk_ready, 1)
                    if kind == "V":
                        t = step[1]
                        bank, free = wait_full(dve, i, step)
                        val = bank[:, :].rearrange("p (h d) -> p h d", h=H)
                        if masked:
                            dve.tensor_tensor(v_ext[:, t, :, 0:DH], val,
                                              bv[:, :].rearrange("p (h d) -> p h d", h=H), ALU.add).then_inc(free, 1)
                        else:
                            dve.tensor_tensor(v_ext[:, t, :, 0:DH], val,
                                              gate[:, t, :].unsqueeze(2).to_broadcast([P, H, DH]),
                                              ALU.mult).then_inc(free, 1)
                    elif kind == "EX":
                        bank, free = wait_full(dve, i, step)
                        c = step[1]
                        z = gate_t[0:2 * H, c * CH:(c + 1) * CH]
                        dve.tensor_scalar(z, bank[0:2 * H, :], bsm[:, 0:1], -87.0, ALU.add, ALU.max).then_inc(free, 1)
                        dve.drain().then_inc(gate_sum, 1)
                        dve.wait_ge(gate_exp, i * NC_ + c + 1)
                        alone(dve)
                        dve.tensor_scalar(z, z, 1.0, None, ALU.add)
                        dve.drain()
                        dve.reciprocal(z, z)
                        dve.drain().then_inc(gate_ready, 1)
                    elif kind == "AP":
                        bank, free = wait_full(dve, i, step)
                        dve.tensor_copy(gate[:, :, :], bank[:, 0:TT * H].rearrange("p (t h) -> p t h", t=TT))\
                           .then_inc(free, 1)
                        dve.drain()
                        dve.tensor_copy(v_ext[:, :, :, DH:DH + 1], gate[:, :, :].unsqueeze(3))
                    elif kind == "smax":
                        _, p, h, t, c = step
                        bank, free = wait_full(dve, i, step)
                        j = (h * TT + t) * NC_ + c
                        if masked:
                            alone(dve)
                            dve.tensor_tensor_reduce(bank[:, :], bank[:, :], mask_q[:, t, c * CH:(c + 1) * CH],
                                                     1.0, -3e38, ALU.add, ALU.max,
                                                     mx[:, p % 2, j:j + 1]).then_inc(free, 1)
                        else:
                            dve.tensor_reduce(mx[:, p % 2, j:j + 1], bank[:, :], AX.X, ALU.max).then_inc(free, 1)
                        if (h, t, c) == (1, TT - 1, NC_ - 1):
                            maxima(p)
                    elif kind == "CS":
                        bank, free = wait_full(dve, i, step)
                        dve.tensor_scalar(vmean[:, :], bank[:, 0:KT], 1.0 / S, None, ALU.mult).then_inc(free, 1)
                        dve.drain()
                        wide_mean = vmean[:, :].unsqueeze(2).to_broadcast([P, KT, P])
                        dve.tensor_copy(vm[:, 0, :, :], wide_mean)
                        dve.drain()
                        dve.tensor_tensor(vm[:, 1, :, :], wide_mean, vm[:, 0, :, :].bitcast(F32), ALU.subtract)
                        dve.drain().then_inc(vm_ready, 1)
                    elif kind == "st":
                        if step == ("st", PAIRS - 1, 4, 0) and masked:
                            dve.wait_ge(bo_added, i + 1)
                            dve.wait_ge(rz_ready, i + 1)
                            for t in range(TT):
                                dve.scalar_tensor_tensor(out=y[:, t, :], in0=rz[:, :], scalar=none[:, t:t + 1],
                                                         in1=y[:, t, :], op0=ALU.mult, op1=ALU.add)
                    elif kind == "pv":
                        if step[2:] == (TT - 1, NC_ - 1):
                            take_sums(step[1])
                    elif kind == "den":
                        bank, free = wait_full(dve, i, step)
                        dve.reciprocal(r[:, :, :].rearrange("p t h -> p (t h)"), bank[:, 0:2 * TT]).then_inc(free, 1)
                        dve.drain().then_inc(r_ready, 1)
                    elif kind == "bc":
                        _, p, c = step
                        bank, free = wait_full(dve, i, step)
                        for h in range(2):
                            a = DH * ((2 * p + h) % 4)
                            last = dve.tensor_tensor(q_raw[a:a + DH, p // 2, c * CH:(c + 1) * CH],
                                                     u[64 * h:64 * h + DH, c, :], bank[64 * h:64 * h + DH, :],
                                                     ALU.mult)
                        last.then_inc(free, 1)
                        if p == PAIRS - 1:
                            dve.drain().then_inc(ctx_done, 1)
                    elif kind == "out":
                        t = step[1]
                        bank, free = wait_full(dve, i, step)
                        if t == 0:
                            dve.wait_ge(res_in, i * 16 + 16)
                        dve.tensor_tensor(y[:, t, :], bank[:, :], y[:, t, :], ALU.add).then_inc(free, 1)
                        dve.drain()
                        dve.bn_stats(stats[:, :], y[:, t, :])
                        dve.drain()
                        dve.bn_aggr(mv[:, t, :], stats[:, :])
                        c = t // (TT - 1)
                        if t == HALF or t == TT - 1:
                            half = slice(c * HALF, (c + 1) * HALF)
                            dve.drain()
                            dve.tensor_scalar(tmp[:, half], mv[:, half, 1], EPS, None, ALU.add).then_inc(var_ready, 1)
                        if t in (HALF + 1, TT - 1):
                            dve.wait_ge(sd_ready, i * NC_ + c + 1)
                            half = slice(c * HALF, (c + 1) * HALF)
                            alone(dve)
                            dve.reciprocal(rstd[:, half], sd[:, half])
                            dve.drain()
                            dve.tensor_tensor(sd[:, half], rstd[:, half], rstd[:, half], ALU.mult)
                            dve.drain()
                            dve.tensor_tensor(sd[:, half], sd[:, half], tmp[:, half], ALU.mult)
                            dve.drain()
                            dve.tensor_scalar(sd[:, half], sd[:, half], -0.5, 1.5, ALU.mult, ALU.add)
                            dve.drain()
                            dve.tensor_tensor(rstd[:, half], rstd[:, half], sd[:, half], ALU.mult)
                            dve.drain()
                        if t > HALF:
                            ready = range((t - HALF - 1) * 2, (t - HALF) * 2) if t < TT - 1 else range(HALF, TT)
                            for q in ready:
                                dve.tensor_scalar(y[:, q, :], y[:, q, :], mv[:, q, 0:1], rstd[:, q:q + 1],
                                                  ALU.subtract, ALU.mult).then_inc(x_ready, 1)


E = 16
HD = 64
WIDE = E * HD
FK = WIDE // P
RING = 4
INV = HD ** -0.5
XC = 256


def ffn_steps():
    steps = [("LG",)] + [("proj", w, t) for w in range(6) for t in range(TT)]
    steps += [("turn", n) for n in range(TT // 2)]
    halves = lambda qt: range(1 if qt < TT // 2 else 2)
    for n in range(TT + 2):
        if 2 <= n:
            steps += [("mixed_t", n - 2, g) for g in range(2)]
        if n < TT:
            steps += [("score", n, c) for c in halves(n)]
        if 1 <= n <= TT:
            steps += [("prob_t", n - 1, c) for c in halves(n - 1)]
        if 2 <= n:
            steps.append(("out", n - 2))
        if 1 <= n <= TT:
            steps.append(("pv", n - 1))
    while len(steps) % RING:
        steps.append(("pad", len(steps) % RING))
    return steps


def expert_layer(nc, io):
    steps = ffn_steps()
    PER = len(steps) // RING
    use_no = {s: n for n, s in enumerate(steps)}
    ctx = ExitStack()
    with ctx:
        used = [0]
        size = nc.sbuf_bytes_remaining // 64 * 64
        start = -(-nc.sbuf_base // 64) * 64
        ctx.enter_context(nc.sbuf_tensor("arena_e", [P, size], mybir.dt.uint8))

        def sb(name, shape, dt=F32, at=None):
            n = 4
            for k in shape[1:]:
                n *= k
            if at is None:
                at = start + used[0]
                used[0] += -(-n // 64) * 64
                assert used[0] + 64 <= size, (name, used[0], size)
            place[name] = at
            return nc.alloc_sbuf_tensor_at(f"{name}_e", shape, dt, offset=at)

        place = {}
        sem = lambda n: ctx.enter_context(nc.semaphore(f"{n}_e"))

        w_in = sb("w_in", [P, 6, 2, KT, CH], F32R)
        w_out = sb("w_out", [P, 2, FK, D], F32R)
        x = sb("x", [P, 2, KT, S], F32R)
        prob = sb("prob", [P, 2, S], at=place["x"])
        prob_t = sb("prob_t", [P, TT, P], at=place["x"] + 8 * S)
        mixed = sb("mixed", [P, E, HD], at=place["x"] + 12 * S)
        mixed_t = sb("mixed_t", [P, 2, FK, P], F32R, at=place["x"] + 16 * S)
        y = sb("y", [P, TT, D])
        weighted = sb("weighted", [P, 2, CH])
        part = sb("part", [P, HD])
        qkv = sb("qkv", [P, 3, TT, HD])
        q_t = sb("q_t", [HD, S])
        k_t = sb("k_t", [HD, S])
        stage = sb("stage", [P, 2, XC])
        w_stage = sb("w_stage", [P, 2, CH])
        eye = sb("eye", [P, P])
        causal = sb("causal", [P, P])
        lower = sb("lower", [P, E, E])
        square = sb("square", [P, CH], at=place["weighted"])
        sim_raw = sb("sim_raw", [P, KT, E])
        sim_sq = sb("sim_sq", [P, KT, E])
        sim = sb("sim", [P, 2, KT, E], F32R)
        ones = sb("ones", [P, P])
        norm = sb("norm", [P, 4, E])
        gates = sb("gates", [P, E])
        lg = sb("lg", [P, TT, E])
        rw = sb("rw", [P, TT, E])
        pick = sb("pick", [P, TT, E])
        beats = sb("beats", [P, TT, E, E], at=place["q_t"])
        small = sb("small", [P, 10, TT])
        nmax = sb("nmax", [P, TT, 2])
        total = sb("total", [P, TT, 2])
        rtot = sb("rtot", [P, TT])
        attn = sb("attn", [P, HD])
        stats = sb("stats", [P, 6])
        mv = sb("mv", [P, TT, 2])
        sd = sb("sd", [P, TT])
        rstd = sb("rstd", [P, TT])
        tmp = sb("tmp", [P, TT])

        bank_of = [ctx.enter_context(nc.psum_tensor(f"work{b}_e", [P, CH], F32)) for b in range(RING)]

        const_in = sem("const_in")
        setup = sem("setup")
        apart = sem("apart")
        norm_sem = sem("norm_sem")
        work_full = [sem(f"work_full{b}") for b in range(RING)]
        work_free = [sem(f"work_free{b}") for b in range(RING)]
        stage_full = [sem(f"stage_full{b}") for b in range(2)]
        stage_free = sem("stage_free")
        w_hi = sem("w_hi")
        w_ready = sem("w_ready")
        x_over = sem("x_over")
        x_full = [sem(f"x_full{b}") for b in range(2)]
        x_free = sem("x_free")
        x_ready = sem("x_ready")
        proj_done = sem("proj_done")
        res_in = sem("res_in")
        squares = sem("squares")
        roots = sem("roots")
        lg_ready = sem("lg_ready")
        exp_ready = sem("exp_ready")
        qkv_ready = sem("qkv_ready")
        turned_in = sem("turned_in")
        masked_in = sem("masked_in")
        prob_ready = sem("prob_ready")
        prob_t_ready = sem("prob_t_ready")
        mixed_ready = sem("mixed_ready")
        hi_ready = sem("hi_ready")
        lo_ready = sem("lo_ready")
        var_ready = sem("var_ready")
        sd_ready = sem("sd_ready")
        y_ready = sem("y_ready")
        stored = sem("stored")

        w_chunks = [(w, k) for w in range(6) for k in range(KT)] + [(6, k) for k in range(FK)]
        NW = len(w_chunks)
        NX = KT * S // XC
        halves = lambda qt: range(1 if qt < TT // 2 else 2)
        keys = lambda qt, c: min(CH, (qt + 1) * P - c * CH)
        scored = lambda qt: sum(len(halves(q)) for q in range(qt + 1))
        SC = scored(TT - 1)

        def wait_full(eng, i, step):
            n = use_no[step]
            eng.wait_ge(work_full[n % RING], i * PER + n // RING + 1)
            return bank_of[n % RING], work_free[n % RING]

        def alone(eng):
            eng.sem_inc(apart, 1)

        block = ctx.enter_context(nc.Block("experts"))

        @block.sync
        def _(sp):
            for t, src in ((eye, io["eye"]), (causal, io["causal"])):
                sp.dma_start(t[:, :], src).then_inc(const_in, 16)
            sp.dma_start(lower[:, :, :], io["lower"].partition_broadcast(P)).then_inc(const_in, 16)
            sp.dma_start(gates[:, :], io["gates"].partition_broadcast(P)).then_inc(const_in, 16)
            sp.dma_start(sim_raw[:, :, :], io["sim"].rearrange("(k p) e -> p k e", p=P)).then_inc(const_in, 16)

            def load_x(i):
                for n in range(NX):
                    k, c = n // (S // XC), n % (S // XC)
                    sp.wait_ge(x_free, 1 + i * NX + max(n - 1, 0))
                    alone(sp)
                    sp.dma_start(stage[:, n % 2, :], io["src_t"][bass.ds(i, 1), k * P:(k + 1) * P, c * XC:(c + 1) * XC]
                                 .rearrange("b p s -> (b p) s")).then_inc(x_full[n % 2], 16)

            for n, (w, k) in enumerate(w_chunks):
                if n >= 2:
                    sp.wait_ge(stage_free, n - 1)
                if w < 6:
                    src = io[("wq", "wk", "wv")[w // 2]][k * P:(k + 1) * P, (w % 2) * CH:(w % 2 + 1) * CH]
                else:
                    src = io["wo"][k * P:(k + 1) * P, :]
                sp.dma_start(w_stage[:, n % 2, :], src).then_inc(stage_full[n % 2], 16)
            sp.wait_ge(setup, 3)
            with sp.Fori(0, B) as i:
                sp.wait_ge(stored, 1 + i * 16)
                alone(sp)
                sp.dma_start(y[:, :, :], io["res"][bass.ds(i, 1), :, :].rearrange("b (t p) d -> p (b t) d", p=P))\
                  .then_inc(res_in, 16)
                load_x(i)
                sp.wait_ge(y_ready, i * TT + TT)
                alone(sp)
                sp.dma_start(io["out"][bass.ds(i, 1), :, :].rearrange("b (t p) d -> p (b t) d", p=P), y[:, :, :])\
                  .then_inc(stored, 16)
            sp.wait_ge(stored, 1 + B * 16)

        @block.gpsimd
        def _(pool):
            for count in (*work_free, x_over, x_free, stored):
                pool.sem_inc(count, 1)
            pool.drain().then_inc(setup, 1)
            pool.wait_ge(setup, 3)
            with pool.Fori(0, B) as i:
                pool.wait_ge(x_over, 1 + i)
                alone(pool)
                for n in range(NX):
                    k, c = n // (S // XC), n % (S // XC)
                    pool.wait_ge(x_full[n % 2], (i * (NX // 2) + n // 2 + 1) * 16)
                    alone(pool)
                    hi, lo = (x[:, part, k, c * XC:(c + 1) * XC] for part in range(2))
                    pool.tensor_scalar(hi, stage[:, n % 2, :], 1.0, 0.0, ALU.mult, ALU.add)
                    pool.drain()
                    pool.tensor_tensor(lo, stage[:, n % 2, :], hi.bitcast(F32), ALU.subtract).then_inc(x_free, 1)
                pool.drain().then_inc(x_ready, 1)

        @block.tensor
        def _(pe):
            pe.wait_ge(setup, 3)
            pe.wait_ge(norm_sem, 1)
            for k in range(KT):
                last = pe.matmul(bank_of[0][:, 0:E], ones[:, :], sim_sq[:, k, :], start=(k == 0), stop=(k == KT - 1))
            last.then_inc(norm_sem, 1)
            pe.wait_ge(norm_sem, 5)
            with pe.Fori(0, B) as i:
                def parts(out, hi_l, lo_l, hi_r, lo_r, tiles=KT):
                    for k in range(tiles):
                        for n, (a, b) in enumerate(((hi_l, hi_r), (hi_l, lo_r), (lo_l, hi_r))):
                            last = pe.matmul(out, a(k), b(k), start=(k == 0 and n == 0),
                                             stop=(k == tiles - 1 and n == 2))
                    return last

                for n, step in enumerate(steps):
                    kind = step[0]
                    bank = bank_of[n % RING]
                    pe.wait_ge(work_free[n % RING], 1 + i * PER + n // RING)
                    if kind == "LG":
                        pe.wait_ge(x_ready, i + 1)
                        for t in range(TT):
                            last = parts(bank[:, t * E:(t + 1) * E], lambda k: x[:, 0, k, t * P:(t + 1) * P],
                                         lambda k: x[:, 1, k, t * P:(t + 1) * P],
                                         lambda k: sim[:, 0, k, :], lambda k: sim[:, 1, k, :])
                    elif kind == "proj":
                        _, w, t = step
                        if t == 0:
                            pe.wait_ge(w_ready, (w + 1) * KT)
                        last = parts(bank[:, :], lambda k: x[:, 0, k, t * P:(t + 1) * P],
                                     lambda k: x[:, 1, k, t * P:(t + 1) * P],
                                     lambda k: w_in[:, w, 0, k, :], lambda k: w_in[:, w, 1, k, :])
                    elif kind == "turn":
                        if step[1] == 0:
                            pe.wait_ge(qkv_ready, i + 1)
                        alone(pe)
                        for j in range(2):
                            for part_ in range(2):
                                at = (2 * part_ + j) * P
                                last = pe.transpose(bank[0:HD, at:at + P], qkv[:, part_, 2 * step[1] + j, :], eye[:, :])
                    elif kind == "score":
                        _, qt, c = step
                        if qt == 0:
                            pe.wait_ge(turned_in, i + 1)
                        last = pe.matmul(bank[:, 0:keys(qt, c)], q_t[:, qt * P:(qt + 1) * P],
                                         k_t[:, c * CH:c * CH + keys(qt, c)], start=True, stop=True)
                    elif kind == "prob_t":
                        _, qt, c = step
                        pe.wait_ge(prob_ready, i * SC + scored(qt) - len(halves(qt)) + c + 1)
                        for j in range(keys(qt, c) // P):
                            last = pe.transpose(bank[:, j * P:(j + 1) * P],
                                                prob[:, qt % 2, c * CH + j * P:c * CH + (j + 1) * P], eye[:, :])
                    elif kind == "pv":
                        qt = step[1]
                        pe.wait_ge(prob_t_ready, i * TT + qt + 1)
                        for kt in range(qt + 1):
                            last = pe.matmul(bank[:, 0:HD], prob_t[:, kt, :], qkv[:, 2, kt, :],
                                             start=(kt == 0), stop=(kt == qt))
                    elif kind == "mixed_t":
                        _, qt, g = step
                        pe.wait_ge(mixed_ready, i * TT + qt + 1)
                        for j in range(FK // 2):
                            at = (g * FK // 2 + j) * P
                            last = pe.transpose(bank[:, j * P:(j + 1) * P],
                                                mixed[:, :, :].rearrange("p e d -> p (e d)")[:, at:at + P], eye[:, :])
                    elif kind == "out":
                        qt = step[1]
                        pe.wait_ge(lo_ready, (i * TT + qt + 1) * 2)
                        if qt == 0:
                            pe.wait_ge(w_ready, NW)
                        last = parts(bank[:, :], lambda k: mixed_t[:, 0, k, :], lambda k: mixed_t[:, 1, k, :],
                                     lambda k: w_out[:, 0, k, :], lambda k: w_out[:, 1, k, :], FK)
                    elif kind == "pad":
                        last = pe.matmul(bank[:, 0:P], ones[:, :], eye[:, :], start=True, stop=True)
                    last.then_inc(work_full[n % RING], 1)
                    if step == ("out", TT - 1):
                        pe.drain().then_inc(x_over, 1)

        @block.scalar
        def _(act):
            act.wait_ge(norm_sem, 3)
            act.activation(norm[:, 1, :], norm[:, 0, :], ACT.Sqrt)
            act.drain()
            act.activation(norm[:, 2, :], gates[:, :], ACT.Exp, scale=-1.0)
            act.drain().then_inc(norm_sem, 1)
            act.wait_ge(setup, 3)
            for n, (w, k) in enumerate(w_chunks):
                act.wait_ge(stage_full[n % 2], 16 * (n // 2 + 1))
                hi = w_in[:, w, 0, k, :] if w < 6 else w_out[:, 0, k, :]
                act.activation(hi, w_stage[:, n % 2, :], ACT.Copy).then_inc(w_hi, 1)
            with act.Fori(0, B) as i:
                for step in steps:
                    kind = step[0]
                    if kind == "LG":
                        act.wait_ge(res_in, i * 16 + 16)
                        for t in range(TT):
                            act.activation(square[:, :], y[:, t, :], ACT.Square, accum_out=small[:, 0, t:t + 1])
                            act.drain()
                        act.activation(small[:, 1, :], small[:, 0, :], ACT.Sqrt)
                        act.drain().then_inc(roots, 1)
                        act.wait_ge(lg_ready, i + 1)
                        act.activation(pick[:, :, :], pick[:, :, :], ACT.Exp)
                        act.drain().then_inc(exp_ready, 1)
                    elif kind == "turn":
                        n = step[1]
                        bank, free = wait_full(act, i, step)
                        act.activation(q_t[:, 2 * n * P:(2 * n + 2) * P], bank[0:HD, 0:2 * P], ACT.Copy)
                        act.activation(k_t[:, 2 * n * P:(2 * n + 2) * P], bank[0:HD, 2 * P:4 * P], ACT.Copy)\
                           .then_inc(free, 1)
                        if n == TT // 2 - 1:
                            act.drain().then_inc(turned_in, 1)
                    elif kind == "score":
                        _, qt, c = step
                        act.wait_ge(masked_in, i * TT + qt + 1)
                        bank, free = wait_full(act, i, step)
                        act.activation(prob[:, qt % 2, c * CH:c * CH + keys(qt, c)], bank[:, 0:keys(qt, c)], ACT.Exp,
                                       scale=INV, bias=nmax[:, qt, 0:1], accum_out=total[:, qt, c:c + 1])\
                           .then_inc(free, 1)
                        act.drain().then_inc(prob_ready, 1)
                    elif kind == "prob_t":
                        _, qt, c = step
                        bank, free = wait_full(act, i, step)
                        act.activation(prob_t[:, c * 4:c * 4 + keys(qt, c) // P, :].rearrange("p k n -> p (k n)"),
                                       bank[:, 0:keys(qt, c)], ACT.Copy).then_inc(free, 1)
                        if c == halves(qt)[-1]:
                            act.drain().then_inc(prob_t_ready, 1)
                    elif kind == "mixed_t":
                        _, qt, g = step
                        n = use_no[step]
                        act.wait_ge(work_full[n % RING], i * PER + n // RING + 1)
                        act.activation(mixed_t[:, 0, g * 4:g * 4 + 4, :].rearrange("p k n -> p (k n)"),
                                       bank_of[n % RING][:, :], ACT.Copy)
                        act.drain().then_inc(hi_ready, 1)
                    elif kind == "pad":
                        bank, free = wait_full(act, i, step)
                        alone(act)
                        act.drain().then_inc(free, 1)
                    if step == ("out", TT - 1):
                        act.wait_ge(var_ready, i + 1)
                        act.activation(sd[:, :], tmp[:, :], ACT.Sqrt).then_inc(sd_ready, 1)

        @block.vector
        def _(dve):
            dve.memset(ones[:, :], 1.0)
            dve.wait_ge(const_in, 16 * 5)
            dve.tensor_tensor(sim_sq[:, :, :], sim_raw[:, :, :], sim_raw[:, :, :], ALU.mult)
            dve.drain().then_inc(setup, 1)
            dve.engine_nop().then_inc(setup, 1)
            dve.engine_nop().then_inc(norm_sem, 1)
            dve.wait_ge(norm_sem, 2)
            dve.tensor_copy(norm[:, 0, :], bank_of[0][:, 0:E])
            dve.tensor_scalar(gates[:, :], gates[:, :], -87.0, None, ALU.max)
            dve.drain().then_inc(norm_sem, 1)
            dve.wait_ge(norm_sem, 4)

            def better_root(out, sq, root, hold):
                dve.tensor_scalar(root, root, 1e-12, None, ALU.max)
                dve.drain()
                dve.reciprocal(hold, root)
                dve.drain()
                dve.tensor_tensor(hold, hold, sq, ALU.mult)
                dve.drain()
                dve.tensor_tensor(hold, hold, root, ALU.add)
                dve.drain()
                dve.tensor_scalar(out, hold, 0.5, 1e-12, ALU.mult, ALU.max)
                dve.drain()

            better_root(norm[:, 1, :], norm[:, 0, :], norm[:, 1, :], norm[:, 3, :])
            dve.reciprocal(norm[:, 1, :], norm[:, 1, :])
            dve.drain()
            dve.tensor_tensor(sim_sq[:, :, :], sim_raw[:, :, :], norm[:, 1, :].unsqueeze(1).to_broadcast([P, KT, E]),
                              ALU.mult)
            dve.tensor_scalar(norm[:, 2, :], norm[:, 2, :], 1.0, None, ALU.add)
            dve.drain()
            dve.reciprocal(gates[:, :], norm[:, 2, :])
            dve.tensor_copy(sim[:, 0, :, :], sim_sq[:, :, :])
            dve.drain()
            dve.tensor_tensor(sim[:, 1, :, :], sim_sq[:, :, :], sim[:, 0, :, :].bitcast(F32), ALU.subtract)
            dve.drain().then_inc(norm_sem, 1)
            for n, (w, k) in enumerate(w_chunks):
                dve.wait_ge(w_hi, n + 1)
                hi, lo = (w_in[:, w, part_, k, :] if w < 6 else w_out[:, part_, k, :] for part_ in range(2))
                dve.tensor_tensor(lo, w_stage[:, n % 2, :], hi.bitcast(F32), ALU.subtract).then_inc(stage_free, 1)
                dve.drain().then_inc(w_ready, 1)
            with dve.Fori(0, B) as i:
                for step in steps:
                    kind = step[0]
                    if kind == "LG":
                        bank, free = wait_full(dve, i, step)
                        dve.wait_ge(roots, i + 1)
                        alone(dve)
                        better_root(small[:, 1, :], small[:, 0, :], small[:, 1, :], small[:, 2, :])
                        dve.reciprocal(small[:, 1, :], small[:, 1, :])
                        dve.drain()
                        dve.tensor_tensor(lg[:, :, :], bank[:, 0:TT * E].rearrange("p (t e) -> p t e", t=TT),
                                          small[:, 1, :].unsqueeze(2).to_broadcast([P, TT, E]), ALU.mult)\
                           .then_inc(free, 1)
                        dve.drain()
                        dve.tensor_tensor(lg[:, :, :], lg[:, :, :], gates[:, :].unsqueeze(1).to_broadcast([P, TT, E]),
                                          ALU.subtract)
                        dve.drain()
                        for t in range(TT):
                            me = lg[:, t, :].unsqueeze(2).to_broadcast([P, E, E])
                            other = lg[:, t, :].unsqueeze(1).to_broadcast([P, E, E])
                            dve.tensor_tensor(beats[:, t, :, :], other, me, ALU.is_equal)
                        dve.drain()
                        for t in range(TT):
                            dve.tensor_tensor(beats[:, t, :, :], beats[:, t, :, :], lower[:, :, :], ALU.mult)
                        dve.drain()
                        dve.tensor_reduce(rw[:, :, :], beats[:, :, :, :], AX.X, ALU.add)
                        dve.drain()
                        for t in range(TT):
                            me = lg[:, t, :].unsqueeze(2).to_broadcast([P, E, E])
                            other = lg[:, t, :].unsqueeze(1).to_broadcast([P, E, E])
                            dve.tensor_tensor(beats[:, t, :, :], other, me, ALU.is_gt)
                        dve.drain()
                        dve.tensor_reduce(pick[:, :, :], beats[:, :, :, :], AX.X, ALU.add)
                        dve.drain()
                        dve.tensor_tensor(rw[:, :, :], rw[:, :, :], pick[:, :, :], ALU.add)
                        dve.drain()
                        dve.tensor_scalar(rw[:, :, :], rw[:, :, :], 2.0, None, ALU.is_lt)
                        dve.tensor_scalar(lg[:, :, :], lg[:, :, :], 0.0, None, ALU.max)
                        dve.drain()
                        dve.tensor_reduce(small[:, 3, :], lg[:, :, :], AX.X, ALU.max)
                        dve.drain()
                        dve.tensor_scalar(small[:, 4, :], small[:, 3, :], 0.0, None, ALU.is_le)
                        dve.drain()
                        top = small[:, 3, :].unsqueeze(2).to_broadcast([P, TT, E])
                        dve.tensor_tensor(rw[:, :, :], rw[:, :, :],
                                          small[:, 4, :].unsqueeze(2).to_broadcast([P, TT, E]), ALU.mult)
                        dve.tensor_tensor(pick[:, :, :], lg[:, :, :], top, ALU.subtract)
                        dve.drain().then_inc(lg_ready, 1)
                        dve.tensor_scalar(lg[:, :, :], lg[:, :, :], 0.0, None, ALU.is_gt)
                        dve.drain()
                        dve.tensor_tensor(rw[:, :, :], rw[:, :, :], lg[:, :, :], ALU.add)
                        dve.drain()
                        dve.wait_ge(exp_ready, i + 1)
                        dve.tensor_tensor(rw[:, :, :], rw[:, :, :], pick[:, :, :], ALU.mult)
                        dve.drain()
                        dve.tensor_reduce(small[:, 5, :], rw[:, :, :], AX.X, ALU.add)
                        dve.drain()
                        dve.reciprocal(small[:, 6, :], small[:, 5, :])
                        dve.drain()
                        dve.tensor_tensor(rw[:, :, :], rw[:, :, :],
                                          small[:, 6, :].unsqueeze(2).to_broadcast([P, TT, E]), ALU.mult)
                        dve.drain()
                    elif kind == "proj":
                        _, w, t = step
                        bank, free = wait_full(dve, i, step)
                        prod = weighted[:, t % 2, :]
                        dve.tensor_tensor(prod.rearrange("p (e d) -> p e d", d=HD),
                                          bank[:, :].rearrange("p (e d) -> p e d", d=HD),
                                          rw[:, t, (w % 2) * 8:(w % 2) * 8 + 8].unsqueeze(2)
                                          .to_broadcast([P, 8, HD]), ALU.mult).then_inc(free, 1)
                        dve.drain()
                        target = qkv[:, w // 2, t, :] if w % 2 == 0 else part[:, :]
                        dve.tensor_reduce(target, prod.rearrange("p (e d) -> p d e", d=HD), AX.X, ALU.add)
                        if w % 2:
                            dve.drain()
                            dve.tensor_tensor(qkv[:, w // 2, t, :], qkv[:, w // 2, t, :], part[:, :], ALU.add)
                            if (w, t) == (5, TT - 1):
                                dve.drain().then_inc(qkv_ready, 1)
                            else:
                                dve.drain()
                    elif kind == "score":
                        _, qt, c = step
                        bank, free = wait_full(dve, i, step)
                        last_half = c == halves(qt)[-1]
                        width = keys(qt, c)
                        if last_half:
                            dve.tensor_tensor(bank[:, width - P:width], bank[:, width - P:width], causal[:, :], ALU.add)
                            dve.drain()
                        dve.tensor_reduce(nmax[:, qt, c:c + 1], bank[:, 0:width], AX.X, ALU.max)
                        if last_half:
                            dve.drain()
                            if c:
                                dve.tensor_tensor(nmax[:, qt, 0:1], nmax[:, qt, 0:1], nmax[:, qt, 1:2], ALU.max)
                                dve.drain()
                            dve.tensor_scalar(nmax[:, qt, 0:1], nmax[:, qt, 0:1], -INV, None, ALU.mult)
                            dve.drain().then_inc(masked_in, 1)
                    elif kind == "pv":
                        qt = step[1]
                        bank, free = wait_full(dve, i, step)
                        dve.wait_ge(prob_ready, i * SC + scored(qt))
                        if len(halves(qt)) == 2:
                            alone(dve)
                            dve.tensor_tensor(rtot[:, qt:qt + 1], total[:, qt, 0:1], total[:, qt, 1:2], ALU.add)
                            dve.drain()
                            dve.reciprocal(rtot[:, qt:qt + 1], rtot[:, qt:qt + 1])
                        else:
                            dve.reciprocal(rtot[:, qt:qt + 1], total[:, qt, 0:1])
                        dve.drain()
                        dve.tensor_scalar(attn[:, :], bank[:, 0:HD], rtot[:, qt:qt + 1], None, ALU.mult)\
                           .then_inc(free, 1)
                        dve.drain()
                        dve.tensor_tensor(mixed[:, :, :], attn[:, :].unsqueeze(1).to_broadcast([P, E, HD]),
                                          rw[:, qt, :].unsqueeze(2).to_broadcast([P, E, HD]), ALU.mult)
                        dve.drain().then_inc(mixed_ready, 1)
                    elif kind == "mixed_t":
                        _, qt, g = step
                        n = use_no[step]
                        dve.wait_ge(hi_ready, (i * TT + qt) * 2 + g + 1)
                        dst = lambda part_: mixed_t[:, part_, g * 4:g * 4 + 4, :].rearrange("p k n -> p (k n)")
                        dve.tensor_tensor(dst(1), bank_of[n % RING][:, :], dst(0).bitcast(F32), ALU.subtract)\
                           .then_inc(work_free[n % RING], 1)
                        dve.drain().then_inc(lo_ready, 1)
                    elif kind == "out":
                        t = step[1]
                        bank, free = wait_full(dve, i, step)
                        dve.tensor_tensor(y[:, t, :], bank[:, :], y[:, t, :], ALU.add).then_inc(free, 1)
                        dve.drain()
                        dve.bn_stats(stats[:, :], y[:, t, :])
                        dve.drain()
                        dve.bn_aggr(mv[:, t, :], stats[:, :])
                        if t == TT - 1:
                            dve.drain()
                            dve.tensor_scalar(tmp[:, :], mv[:, :, 1], EPS, None, ALU.add).then_inc(var_ready, 1)
                            dve.wait_ge(sd_ready, i + 1)
                            dve.reciprocal(rstd[:, :], sd[:, :])
                            dve.drain()
                            dve.tensor_tensor(sd[:, :], rstd[:, :], rstd[:, :], ALU.mult)
                            dve.drain()
                            dve.tensor_tensor(sd[:, :], sd[:, :], tmp[:, :], ALU.mult)
                            dve.drain()
                            dve.tensor_scalar(sd[:, :], sd[:, :], -0.5, 1.5, ALU.mult, ALU.add)
                            dve.drain()
                            dve.tensor_tensor(rstd[:, :], rstd[:, :], sd[:, :], ALU.mult)
                            dve.drain()
                            for q in range(TT):
                                dve.tensor_scalar(y[:, q, :], y[:, q, :], mv[:, q, 0:1], rstd[:, q:q + 1],
                                                  ALU.subtract, ALU.mult).then_inc(y_ready, 1)


def constants():
    import numpy as np

    eye = np.eye(P, dtype=np.float32)
    sel = {}
    for masked in (False, True):
        m = np.zeros((P, 2), np.float32)
        for h in range(2):
            m[64 * h + DH, h] = 1.0
            m[64 * h + DH + (2 if masked else 1), h] = 1.0
        sel[masked] = m
    sign = np.where(np.arange(P) % DH < DH // 2, 1.0, -1.0).astype(np.float32).reshape(P, 1)
    ap = np.zeros((2 * H + 1, PAIRS, P), np.float32)
    for p in range(PAIRS):
        for h in range(2):
            ap[2 * p + h, p, 64 * h:64 * h + DH + 1] = 1.0
            ap[2 * H, p, 64 * h + DH + 1] = 1.0
    return {"eye": eye, "neg_eye": -eye, "sel_den1": sel[False], "sel_den2": sel[True], "sel_ap": ap, "sign": sign,
            "causal": np.where(np.arange(P)[None, :] > np.arange(P)[:, None], np.float32(-1e30), np.float32(0)),
            "lower": np.tril(np.ones((E, E), np.float32), -1)}


def turned(a, axes):
    import numpy as np

    return np.ascontiguousarray(np.transpose(a, axes))



def program(nc, ins, out):
    scratch = lambda name, shape: nc.dram_tensor(name, shape, F32).ap()
    x1, x1_t = scratch("x1", [B, S, D]), scratch("x1_t", [B, D, S])
    x2, x2_t = scratch("x2", [B, S, D]), scratch("x2_t", [B, D, S])
    attention(nc, False, dict(
        q_src=ins["x_t"], kv_src=ins["x_t"], res=ins["x"], wq=ins["L0_attn_Wi"], wk=ins["L0_attn_Wo"],
        wv=ins["L0_attn_Wv"], wo=ins["L0_attn_Wout"], wo_swapped=ins["Wout_swapped"],
        wo_turned=scratch("wo_turned", [D, D]), wa=ins["L0_attn_Wa"], we=ins["L0_attn_We"], ba=ins["L0_attn_ba"],
        be=ins["L0_attn_be"], beta=ins["L0_attn_beta_p"], iv=ins["L0_attn_iv_p"], ov=ins["L0_attn_ov_p"],
        chi=ins["L0_attn_chi"], out=x1, out_t=x1_t, eye=ins["eye"], neg_eye=ins["neg_eye"],
        sel_den=ins["sel_den1"], sel_ap=ins["sel_ap"], sign=ins["sign"]))
    attention(nc, True, dict(
        q_src=x1_t, kv_src=ins["ctx_t"], res=x1, wq=ins["Wq_t"], wk=ins["Wk_t"], wv=ins["Wv_t"], wo=ins["Wo_t"],
        bq=ins["L0_xattn_bq"], bk=ins["L0_xattn_bk"], bv=ins["L0_xattn_bv"], bo=ins["L0_xattn_bo"],
        mask_q=ins["mask"], mask_k=ins["mask_t"], out=x2, out_t=x2_t, eye=ins["eye"], neg_eye=ins["neg_eye"],
        sel_den=ins["sel_den2"]))
    expert_layer(nc, dict(
        src_t=x2_t, res=x2, sim=ins["L0_ffn_sim_matrix"], gates=ins["L0_ffn_gates"], wq=ins["q_proj_t"],
        wk=ins["k_proj_t"], wv=ins["v_proj_t"], wo=ins["o_proj"], out=out, eye=ins["eye"],
        causal=ins["causal"], lower=ins["lower"]))


def kernel(**inputs):
    import numpy as np
    import concourse.bacc as bacc
    from concourse.bass_utils import run_bass_kernel_spmd

    arrays = {name: np.ascontiguousarray(inputs[name]) for name in (
        "x", "L0_attn_Wa", "L0_attn_ba", "L0_attn_We", "L0_attn_be", "L0_attn_Wi", "L0_attn_Wo", "L0_attn_Wv",
        "L0_attn_Wout", "L0_attn_chi", "L0_attn_beta_p", "L0_attn_iv_p", "L0_attn_ov_p", "L0_xattn_bq",
        "L0_xattn_bk", "L0_xattn_bv", "L0_xattn_bo", "L0_ffn_sim_matrix", "L0_ffn_gates")}
    arrays["x_t"] = turned(inputs["x"], (0, 2, 1))
    arrays["ctx_t"] = turned(inputs["ctx_1024"], (0, 2, 1))
    arrays["mask"] = np.ascontiguousarray(inputs["mask_BxSxS2_ik1"])
    arrays["mask_t"] = turned(inputs["mask_BxSxS2_ik1"], (0, 2, 1))
    for name in ("Wq", "Wk", "Wv", "Wo"):
        arrays[f"{name}_t"] = turned(inputs[f"L0_xattn_{name}"], (1, 0))
    arrays["Wout_swapped"] = np.ascontiguousarray(
        np.asarray(inputs["L0_attn_Wout"]).reshape(H, 2, DH // 2, D)[:, ::-1].reshape(D, D))
    for name in ("q_proj", "k_proj", "v_proj"):
        arrays[f"{name}_t"] = turned(inputs[f"L0_ffn_{name}"], (1, 0, 2)).reshape(D, WIDE)
    arrays["o_proj"] = np.ascontiguousarray(inputs["L0_ffn_o_proj"]).reshape(WIDE, D)
    arrays.update(constants())
    nc = bacc.Bacc("TRN2", target_bir_lowering=False, num_devices=1)
    ins = {name: nc.dram_tensor(name, a.shape, mybir.dt.from_np(a.dtype), kind="ExternalInput").ap()
           for name, a in arrays.items()}
    out = nc.dram_tensor("out", (B, S, D), F32, kind="ExternalOutput").ap()
    program(nc, ins, out)
    result = run_bass_kernel_spmd(nc, [arrays], core_ids=[0])
    return result.results[0]["out"]
```

```python
import math
from contextlib import ExitStack

import concourse.bass as bass
from concourse import mybir

P = 128
B, S, D, H = 4, 1024, 512, 16
DH = D // H
KT = D // P
TT = S // P
CH = 512
NC_ = S // CH
HALF = TT // NC_
PAIRS = H // 2
VW = DH + 2
EPS = 1e-5
SCALE = DH ** -0.5
MASKED = -57344.0 * 16384.0
ABSENT = -1e8
STACK_DMAS = 6
SLOTS = 3
PRING = 4

ALU = mybir.AluOpType
ACT = mybir.ActivationFunctionType
AX = mybir.AxisListType
F32 = mybir.dt.float32
F32R = mybir.dt.float32r
BF16 = mybir.dt.bfloat16
FP8 = mybir.dt.float8e5
I32 = mybir.dt.int32


def attention_steps(masked):
    smax = lambda p: [("smax", p, h, t, c) for h in range(2) for t in range(TT) for c in range(NC_)]
    steps = [("Q", g, c) for g in range(KT) for c in range(NC_)]
    steps += [("K", 0, c) for c in range(NC_)]
    rest = [] if masked else [("EX", c) for c in range(NC_)]
    rest += [("K", g, c) for g in range(1, KT) for c in range(NC_)]
    rest += [] if masked else [("AP",)]
    rest += [("V", t) for t in range(TT)]
    first = [("smax0", h, t) for h in range(2) for t in range(TT)]
    lead = 6
    every = -(-len(first) // (len(rest) - lead - 2))
    for n, step in enumerate(rest):
        if n == len(rest) - 1:
            steps.append(("mneg", 0))
        steps.append(step)
        if n >= lead:
            steps += first[:every]
            first = first[every:]
    if masked:
        steps.append(("CS",))

    GAPS = 4
    ahead = [m for p in range(1, PAIRS) for m in smax(p)]
    left = 0
    due = []
    for p in range(PAIRS):
        extra = {}
        if p > 0:
            extra[6] = [("den", p - 1, 0)]
            extra[8] = [("den", p - 1, 1)]
            extra[11] = [("bc", p - 1, 0)]
            extra[13] = [("bc", p - 1, 1)]
        if masked and p == 2:
            extra[15] = [("RZ",)]
        for kt in range(TT):
            before = (p, kt - 1) if kt else (p - 1, TT - 1)
            work = [("st", p, kt, h) for h in range(2)] + [("pv", *before, c) for c in range(NC_)]
            for g in range(GAPS):
                if work[g][1] >= 0:
                    steps.append(work[g])
                n = GAPS * kt + g
                steps += extra.get(n, [])
                if due:
                    left += 1
                    if left >= 3:
                        steps.append(due.pop(0))
                        left = 0
                rate = (0 if n < GAPS else 2 if n % 2 else 1) if p == 0 else 1
                for _ in range(rate):
                    if ahead:
                        m = ahead.pop(0)
                        steps.append(m)
                        if m[2:] == (1, TT - 1, NC_ - 1):
                            due.append(("mneg", m[1]))
                            left = 0
    assert not ahead and not due
    steps += [("pv", PAIRS - 1, TT - 1, c) for c in range(NC_)]
    steps += [(kind, PAIRS - 1, c) for kind in ("den", "bc") for c in range(NC_)]
    steps += [("out", t) for t in range(TT)]
    steps += [("xt", t) for t in range(TT)]
    if sum(s[0] not in ("st", "pv", "smax0") for s in steps) % 2:
        steps.append(("pad",))
    return steps


def attention(nc, masked, io):
    steps = attention_steps(masked)
    uses = [s for s in steps if s[0] not in ("st", "pv", "smax0")]
    PER = len(uses) // 2
    use_no = {s: n for n, s in enumerate(uses)}
    pair_slots = [[p for p in range(PAIRS) if p % SLOTS == s] for s in range(SLOTS)]

    ctx = ExitStack()
    with ctx:
        used = [0]
        base = nc.sbuf_base
        size = nc.sbuf_bytes_remaining // 64 * 64
        ctx.enter_context(nc.sbuf_tensor(f"arena{int(masked)}", [P, size], mybir.dt.uint8))
        start = -(-base // 64) * 64
        wide = {F32: 4, F32R: 4, BF16: 2, FP8: 1, I32: 4}

        def sb(name, shape, dt=F32, at=None):
            n = wide[dt]
            for k in shape[1:]:
                n *= k
            if at is None:
                at = start + used[0]
                used[0] += -(-n // 64) * 64
                assert used[0] + 64 <= size, (name, used[0], size)
            t = nc.alloc_sbuf_tensor_at(f"{name}_{int(masked)}", shape, dt, offset=at)
            place[name] = at
            return t

        place = {}
        sem = lambda n: ctx.enter_context(nc.semaphore(f"{n}_{int(masked)}"))

        stack = sb("stack", [P, SLOTS, 4, S], F32R)
        x_hi = stack[:, 1, :, :]
        x_lo = stack[:, 2, :, :]
        q_raw = sb("q_raw", [P, KT, S])
        k_raw = sb("k_raw", [P, KT, S])
        y = k_raw[:, :, :].rearrange("p g (a d) -> p (g a) d", d=D)
        qk = sb("qk", [P, 4, S], F32R)
        v_ext = sb("v_ext", [P, TT, H, VW])
        w0 = sb("w0", [P, 2, KT, D], F32R)
        probs = sb("probs", [P, PRING, S])
        w1 = sb("w1", [P, 2, KT, D], F32R, at=place["probs"])
        stage = sb("stage", [P, 2, S])
        u = sb("u", [P, NC_, CH])
        r = sb("r", [P, TT, 2])
        r_wide = sb("r_wide", [P, TT, 2, DH])
        eye = sb("eye", [P, P])
        neg_eye = sb("neg_eye", [P, P])
        mx = sb("mx", [P, 2, 2 * TT * NC_])
        mm = sb("mm", [P, 2 * TT])
        mrow = sb("mrow", [2 * TT, P], F32R)
        stats = sb("stats", [P, 6])
        mv = sb("mv", [P, TT, 2])
        sd = sb("sd", [P, TT])
        rstd = sb("rstd", [P, TT])
        tmp = sb("tmp", [P, TT])
        xts = sb("xts", [P, KT, S], at=place["qk"])
        if masked:
            kv_raw = sb("kv_raw", [P, KT, S], at=place["qk"])
            mask_q = sb("mask_q", [P, TT, S], BF16)
            mask_k = sb("mask_k", [P, TT, S], FP8)
            mstage = sb("mstage", [P, 2, S], I32)
            eye8 = sb("eye8", [P, P], FP8)
            bq = sb("bq", [P, KT])
            bk = sb("bk", [P, KT])
            bv = sb("bv", [P, D])
            bo = sb("bo", [P, D])
            ones = sb("ones", [P, 1])
            none = sb("none", [P, TT])
            vmean = sb("vmean", [P, KT])
            vm = sb("vm", [P, 2, KT, P], F32R)
            rz = sb("rz", [P, D])
        else:
            wsm_raw = sb("wsm_raw", [P, KT, 2 * H])
            wsm = sb("wsm", [P, 2, KT, 2 * H], F32R)
            bsm = sb("bsm", [2 * H, 1])
            gate = sb("gate", [P, TT, 2 * H])
            gate_t = sb("gate_t", [2 * H, S])
            turn_in = sb("turn_in", [P, 4, KT])
            turn = sb("turn", [P, 8, KT])
            sign = sb("sign", [P, 1])
            half_pi = sb("half_pi", [P, 1])

        psum = lambda n, shape: ctx.enter_context(nc.psum_tensor(f"{n}_{int(masked)}", shape, F32))
        work = [psum(f"work{b}", [P, CH]) for b in range(2)]
        scores = [psum(f"scores{b}", [P, S]) for b in range(2)]
        acc = psum("acc", [P, NC_, CH])

        const_in = sem("const_in")
        turn_sem = sem("turn_sem")
        setup = sem("setup")
        apart = sem("apart")
        work_full = [sem(f"work_full{b}") for b in range(2)]
        work_free = [sem(f"work_free{b}") for b in range(2)]
        stage_full = [sem(f"stage_full{b}") for b in range(2)]
        stage_free = sem("stage_free")
        hi_split = sem("hi_split")
        chunk_ready = sem("chunk_ready")
        proj_done = sem("proj_done")
        group_split = sem("group_split")
        ones_set = sem("ones_set")
        stacked = [sem(f"stacked{s}") for s in range(SLOTS)]
        mrow_ready = sem("mrow_ready")
        mrow_in = [sem(f"mrow_in{s}") for s in range(SLOTS)]
        st_full = sem("st_full")
        p_full = sem("p_full")
        pv_done = sem("pv_done")
        smax0_full = sem("smax0_full")
        smax0_free = sem("smax0_free")
        u_ready = sem("u_ready")
        r_ready = sem("r_ready")
        ctx_done = sem("ctx_done")
        mm_ready = sem("mm_ready")
        res_in = sem("res_in")
        res_ready = sem("res_ready")
        ct_split = sem("ct_split")
        out_done = sem("out_done")
        y_done = sem("y_done")
        var_ready = sem("var_ready")
        sd_ready = sem("sd_ready")
        x_ready = sem("x_ready")
        stored = sem("stored")
        xt_ready = sem("xt_ready")
        xt_stored = sem("xt_stored")
        if masked:
            x2_raw = sem("x2_raw")
            x2_hi = sem("x2_hi")
            x2_ready = sem("x2_ready")
            mstage_full = [sem(f"mstage_full{b}") for b in range(2)]
            mstage_free = sem("mstage_free")
            maskq_ready = sem("maskq_ready")
            maskk_ready = sem("maskk_ready")
            vm_ready = sem("vm_ready")
            rz_ready = sem("rz_ready")
            bo_added = sem("bo_added")
        else:
            gate_sum = sem("gate_sum")
            gate_exp = sem("gate_exp")
            gate_ready = sem("gate_ready")

        chunks = [("x", k) for k in range(KT)] + [("wq", 0), ("wq", 1), ("wk", 0), ("wk", 1)]
        before_group0 = len(chunks)
        shared = ("wq",)
        chunks += [("wv", 0), ("wv", 1), ("wo", 0), ("wo", 1)]
        NCH = len(chunks)
        upto = lambda what: max(n for n, c in enumerate(chunks) if c[0] == what) + 1

        def chunk_parts(what, k):
            if what == "x":
                return x_hi[:, k, :], x_lo[:, k, :]
            w = w1 if what in ("wq", "wv") else w0
            half = lambda part: w[:, part, 2 * k:2 * k + 2, :].rearrange("p k n -> p (k n)")
            return half(0), half(1)

        def wait_full(eng, i, step):
            n = use_no[step]
            eng.wait_ge(work_full[n % 2], i * PER + n // 2 + 1)
            return work[n % 2], work_free[n % 2]

        def alone(eng):
            eng.sem_inc(apart, 1)

        def chunks_of(what):
            return [n for n in range(NCH) if chunks[n][0] == what]

        SHARED = len([c for c in chunks if c[0] in shared])

        def nth_in_slot(n):
            return len([m for m in range(n + 1) if m % 2 == n % 2])

        def wait_place(eng, i, what):
            eng.wait_ge(pv_done, 1 + i * PAIRS * TT)
            eng.wait_ge(chunk_ready, i * NCH + chunks_of(what)[0])

        mask_steps = [step for step in steps if step[0] in ("Q", "K", "V")]

        def mask_pieces(step):
            m = mask_steps.index(step)
            return (m // 3 * 2 + m % 3,) if m % 3 < 2 else ()

        block = ctx.enter_context(nc.Block(f"layer{int(masked)}"))

        @block.sync
        def _(sp):
            consts = [(eye, io["eye"]), (neg_eye, io["neg_eye"])]
            for t, src in consts:
                sp.dma_start(t[:, :], src).then_inc(const_in, 16)
            if masked:
                sp.dma_start(bq[:, :], io["bq"].rearrange("(g p) -> p g", p=P),
                             allow_slow_non_contiguous=True).then_inc(const_in, 16)
                sp.dma_start(bk[:, :], io["bk"].rearrange("(g p) -> p g", p=P),
                             allow_slow_non_contiguous=True).then_inc(const_in, 16)
                sp.dma_start(bv[:, :], io["bv"].partition_broadcast(P)).then_inc(const_in, 16)
                sp.dma_start(bo[:, :], io["bo"].partition_broadcast(P)).then_inc(const_in, 16)
            else:
                sp.dma_start(wsm_raw[:, :, 0:H], io["wa"].rearrange("(k p) h -> p k h", p=P)).then_inc(const_in, 16)
                sp.dma_start(wsm_raw[:, :, H:2 * H], io["we"].rearrange("(k p) h -> p k h", p=P)).then_inc(const_in, 16)
                for n, name in enumerate(("ba", "be")):
                    sp.dma_start(bsm[n * H:(n + 1) * H, :], io[name].rearrange("(h a) -> h a", a=1),
                                 allow_slow_non_contiguous=True).then_inc(const_in, 16)
                for n, src in enumerate((io["wo"], io["wo_swapped"])):
                    sp.dma_start(q_raw[:, 2 * n:2 * n + 2, :].rearrange("p g (a d) -> p (g a) d", d=D),
                                 src.rearrange("(k p) d -> p k d", p=P)).then_inc(const_in, 16)
                for n, name in enumerate(("beta", "iv", "ov", "chi")):
                    for q in range(4):
                        sp.dma_start(turn_in[DH * q:DH * (q + 1), n, :],
                                     io[name].rearrange("(k q) -> q k", q=4)[q, :].partition_broadcast(DH),
                                     allow_slow_non_contiguous=True).then_inc(const_in, 16)
                sp.dma_start(sign[:, :], io["sign"]).then_inc(const_in, 16)
            sp.wait_ge(setup, 3)
            with sp.Fori(0, B) as i:
                def load_chunk(n):
                    what, k = chunks[n]
                    sp.wait_ge(stage_free, 1 + i * NCH + max(n - 1, 0))
                    alone(sp)
                    if what == "x":
                        src = io["q_src"][bass.ds(i, 1), k * P:(k + 1) * P, :].rearrange("b p s -> (b p) s")
                        dst = stage[:, n % 2, :]
                    else:
                        if what == "wo" and not masked:
                            sp.wait_ge(turn_sem, 21)
                        name = "wo_turned" if what == "wo" and not masked else what
                        src = io[name][2 * k * P:(2 * k + 2) * P, :].rearrange("(k p) n -> p k n", p=P)
                        dst = stage[:, n % 2, :].rearrange("p (k n) -> p k n", k=2)
                    sp.dma_start(dst, src).then_inc(stage_full[n % 2], 16)

                def stack_pair(p):
                    s = p % SLOTS
                    sp.wait_ge(group_split, i * KT + p // 2 + 1)
                    alone(sp)
                    if p >= SLOTS:
                        sp.wait_ge(st_full, 1 + i * H * TT + 2 * TT * (p - SLOTS + 1))
                    elif p > 0:
                        sp.wait_ge(proj_done, 1 + i * 4 + 3)
                    alone(sp)
                    for h in range(2):
                        a = DH * ((2 * p + h) % 4)
                        for j, (first, step) in enumerate(((0, 2), (1, 1), (0, 3))):
                            sp.dma_start(stack[DH * j:DH * (j + 1), s, h:h + 3:2, :].bitcast(F32),
                                         qk[a:a + DH, first:first + step + 1:step, :].bitcast(F32))\
                              .then_inc(stacked[s], 16)

                def max_row(p):
                    sp.wait_ge(mrow_ready, i * PAIRS + p + 1)
                    alone(sp)
                    sp.dma_start(stack[3 * DH:3 * DH + 1, p % SLOTS, 0:2, :].bitcast(F32),
                                 mrow[:, :].bitcast(F32)).then_inc(mrow_in[p % SLOTS], 16)

                for n in range(chunks.index(("wk", 0))):
                    load_chunk(n)
                if masked:
                    sp.wait_ge(out_done, 1 + i * TT)
                    sp.wait_ge(xt_stored, 1 + i * NC_ * 16)
                    alone(sp)
                    sp.dma_start(kv_raw[:, :, :], io["kv_src"][bass.ds(i, 1), :, :]
                                 .rearrange("b (k p) s -> p (b k) s", p=P)).then_inc(x2_raw, 16)
                for n in range(chunks.index(("wk", 0)), NCH - 2):
                    load_chunk(n)
                stack_pair(0)
                max_row(0)
                stack_pair(1)
                for n in range(NCH - 2, NCH):
                    load_chunk(n)
                stack_pair(2)
                max_row(1)
                for p in range(1, PAIRS):
                    if p + 2 < PAIRS and p > 0:
                        stack_pair(p + 2)
                    if p + 1 < PAIRS and p > 0:
                        max_row(p + 1)
                    if p == 5:
                        sp.wait_ge(group_split, i * KT + KT)
                        alone(sp)
                        sp.dma_start(y, io["res"][bass.ds(i, 1), :, :].rearrange("b (t p) d -> p (b t) d", p=P))\
                          .then_inc(res_in, 16)

        @block.gpsimd
        def _(pool):
            def split(raw, hi, lo):
                pool.tensor_scalar(hi, raw, 1.0, 0.0, ALU.mult, ALU.add)
                pool.drain()
                return pool.tensor_tensor(lo, raw, hi.bitcast(F32), ALU.subtract)

            pool.memset(stack[3 * DH:3 * DH + 1, 0, 2:4, :].bitcast(F32), 1.0)
            pool.drain()
            if not masked:
                pool.wait_ge(const_in, 16 * 25)
                split(wsm_raw[:, :, :], wsm[:, 0, :, :], wsm[:, 1, :, :])
                pool.drain()
            for count in (*work_free, stage_free, ct_split, stored, proj_done, pv_done, st_full, smax0_free, out_done, u_ready,
                          xt_stored, *([mstage_free] if masked else [])):
                pool.sem_inc(count, 1)
            pool.drain().then_inc(setup, 1)
            with pool.Fori(0, B) as i:
                def split_chunk(n):
                    what, k = chunks[n]
                    if what in shared:
                        return
                    hi, lo = chunk_parts(what, k)
                    if what == "x" and k == 0:
                        pool.wait_ge(st_full, 1 + i * H * TT)
                    if what == "wk" and k == 0:
                        pool.wait_ge(proj_done, 1 + i * 4)
                        pool.wait_ge(chunk_ready, i * NCH + upto("wq"))
                    if what == "wv" and k == 0:
                        pool.wait_ge(proj_done, 1 + i * 4 + 1)
                    if what == "wo" and k == 0:
                        pool.wait_ge(proj_done, 1 + i * 4 + 2)
                    pool.wait_ge(stage_full[n % 2], (i * (NCH // 2) + nth_in_slot(n)) * 16)
                    alone(pool)
                    split(stage[:, n % 2, :], hi, lo).then_inc(stage_free, 1)
                    pool.drain()
                    pool.engine_nop().then_inc(chunk_ready, 1)

                def split_group(g):
                    if g > 0:
                        for p in (2 * g - 2, 2 * g - 1):
                            s = p % SLOTS
                            pool.wait_ge(stacked[s], (i * len(pair_slots[s]) + pair_slots[s].index(p) + 1) * STACK_DMAS * 16)
                    else:
                        for step in [("Q", 0, c) for c in range(NC_)] + [("K", 0, c) for c in range(NC_)]:
                            n = use_no[step]
                            pool.wait_ge(work_free[n % 2], 1 + i * PER + n // 2 + 1)
                    if g == 1:
                        for c in range(NC_):
                            n = use_no[("K", KT - 1, c)]
                            pool.wait_ge(work_free[n % 2], 1 + i * PER + n // 2 + 1)
                    if g == 0:
                        pool.wait_ge(out_done, 1 + i * TT)
                        pool.wait_ge(xt_stored, 1 + i * NC_ * 16)
                    alone(pool)
                    split(q_raw[:, g, :], qk[:, 0, :], qk[:, 1, :])
                    pool.drain()
                    split(k_raw[:, g, :], qk[:, 2, :], qk[:, 3, :])
                    pool.drain()
                    pool.engine_nop().then_inc(group_split, 1)

                for n in range(before_group0):
                    split_chunk(n)
                split_group(0)
                for n in range(before_group0, NCH - 2):
                    split_chunk(n)
                pool.wait_ge(proj_done, 1 + i * 4 + 3)
                alone(pool)
                for s in range(1, SLOTS):
                    pool.memset(stack[3 * DH:3 * DH + 1, s, 2:4, :].bitcast(F32), 1.0)
                    pool.drain()
                pool.engine_nop().then_inc(ones_set, 1)
                split_group(1)
                for n in range(NCH - 2, NCH):
                    split_chunk(n)
                for g in range(2, KT):
                    split_group(g)
                if masked:
                    pool.wait_ge(const_in, 16 * 6)
                    pool.wait_ge(res_in, i * 16 + 16)
                    for t in range(TT):
                        pool.tensor_tensor(y[:, t, :], y[:, t, :], bo[:, :], ALU.add)
                        pool.drain()
                    pool.engine_nop().then_inc(bo_added, 1)
                for t in range(TT):
                    if t == 0:
                        for s in range(SLOTS):
                            pool.wait_ge(stacked[s], (i + 1) * len(pair_slots[s]) * STACK_DMAS * 16)
                    if t % (TT // NC_) == 0:
                        pool.wait_ge(ctx_done, i * NC_ + t // (TT // NC_) + 1)
                    if t >= 4:
                        pool.wait_ge(out_done, 1 + i * TT + t - 3)
                    alone(pool)
                    part = lambda k: qk[:, t % 4, k * D:(k + 1) * D].rearrange("p (g n) -> p g n", g=KT)
                    split(q_raw[:, :, t * P:(t + 1) * P], part(0), part(1)).then_inc(ct_split, 1)
                    pool.drain()

        @block.tensor
        def _(pe):
            pe.wait_ge(setup, 3)
            pe.wait_ge(const_in, 16 * (6 if masked else 25))
            with pe.Fori(0, B) as i:
                def parts(out, hi_l, lo_l, hi_r, lo_r, ready=None):
                    for k in range(KT):
                        if ready:
                            ready(k)
                        for n, (a, b) in enumerate(((hi_l, hi_r), (hi_l, lo_r), (lo_l, hi_r))):
                            last = pe.matmul(out, a(k), b(k), start=(k == 0 and n == 0),
                                             stop=(k == KT - 1 and n == 2))
                    return last

                def smax_ready(p):
                    s = p % SLOTS
                    pe.wait_ge(stacked[s], (i * len(pair_slots[s]) + pair_slots[s].index(p) + 1) * STACK_DMAS * 16)

                for step in steps:
                    kind = step[0]
                    if kind == "smax0":
                        _, h, t = step
                        n = h * TT + t
                        if n == 0:
                            smax_ready(0)
                        pe.wait_ge(smax0_free, 1 + i * 2 * TT + max(n - 1, 0))
                        for c in range(NC_):
                            last = pe.matmul(scores[n % 2][:, c * CH:(c + 1) * CH],
                                             stack[0:3 * DH, 0, h, t * P:(t + 1) * P],
                                             stack[0:3 * DH, 0, 2 + h, c * CH:(c + 1) * CH], start=True, stop=True)
                        last.then_inc(smax0_full, 1)
                        continue
                    if kind == "st":
                        _, p, kt, h = step
                        s = p % SLOTS
                        if kt == 0 and h == 0:
                            if p == 0:
                                pe.wait_ge(smax0_free, 1 + (i + 1) * 2 * TT)
                            pe.wait_ge(mrow_in[s], (i * len(pair_slots[s]) + pair_slots[s].index(p) + 1) * 16)
                            if p == 1:
                                pe.wait_ge(ones_set, i + 1)
                            if p == 0 and masked:
                                pe.wait_ge(maskk_ready, i + 1)
                        n = 2 * (p * TT + kt) + h
                        if n >= 2:
                            pe.wait_ge(p_full, i * H * TT + n - 1)
                        for c in range(NC_):
                            last = pe.matmul(scores[n % 2][:, c * CH:(c + 1) * CH],
                                             stack[0:3 * DH + 1, s, 2 + h, kt * P:(kt + 1) * P],
                                             stack[0:3 * DH + 1, s, h, c * CH:(c + 1) * CH],
                                             start=True, stop=not masked)
                            if masked:
                                last = pe.matmul(scores[n % 2][:, c * CH:(c + 1) * CH], eye8[:, :],
                                                 mask_k[:, kt, c * CH:(c + 1) * CH], start=False, stop=True)
                        last.then_inc(st_full, 1)
                        continue
                    if step in (("CS",), ("pv", 0, 0, 0)):
                        for t in (TT - 2, TT - 1):
                            n = use_no[("V", t)]
                            pe.wait_ge(work_free[n % 2], 1 + i * PER + n // 2 + 1)
                    if kind == "pv":
                        _, p, kt, c = step
                        if c == 0:
                            pe.wait_ge(p_full, i * H * TT + 2 * (p * TT + kt) + 2)
                            if kt == 0:
                                pe.wait_ge(u_ready, 1 + (i * PAIRS + p) * NC_)
                        for h in range(2):
                            n = 2 * (p * TT + kt) + h
                            last = pe.matmul(acc[64 * h:64 * h + VW, c, :], v_ext[:, kt, 2 * p + h, :],
                                             probs[:, n % PRING, c * CH:(c + 1) * CH],
                                             start=(kt == 0), stop=(kt == TT - 1), skip_group_check=True)
                        if c == NC_ - 1:
                            last.then_inc(pv_done, 1)
                        continue
                    n = use_no[step]
                    bank = work[n % 2]
                    pe.wait_ge(work_free[n % 2], 1 + i * PER + n // 2)
                    if kind in ("Q", "K"):
                        _, g, c = step
                        w = w1 if kind == "Q" else w0
                        ready = None
                        if step == ("Q", 0, 0):
                            ready = lambda k: pe.wait_ge(chunk_ready, i * NCH + upto("x") + k // 2 + 1)
                        if step == ("K", 0, 0):
                            pe.wait_ge(chunk_ready, i * NCH + before_group0)
                            if masked:
                                ready = lambda k: pe.wait_ge(x2_ready, i * KT + k + 1)
                        last = parts(bank[:, :], lambda k: w[:, 0, k, g * P:(g + 1) * P],
                                     lambda k: w[:, 1, k, g * P:(g + 1) * P],
                                     lambda k: x_hi[:, k, c * CH:(c + 1) * CH],
                                     lambda k: x_lo[:, k, c * CH:(c + 1) * CH], ready)
                    elif kind == "V":
                        t = step[1]
                        if t == 0:
                            pe.wait_ge(chunk_ready, i * NCH + upto("wv"))
                        last = parts(bank[:, :], lambda k: x_hi[:, k, t * P:(t + 1) * P],
                                     lambda k: x_lo[:, k, t * P:(t + 1) * P],
                                     lambda k: w1[:, 0, k, :], lambda k: w1[:, 1, k, :])
                    elif kind == "EX":
                        c = step[1]
                        last = parts(bank[0:2 * H, :], lambda k: wsm[:, 0, k, :], lambda k: wsm[:, 1, k, :],
                                     lambda k: x_hi[:, k, c * CH:(c + 1) * CH],
                                     lambda k: x_lo[:, k, c * CH:(c + 1) * CH])
                    elif kind == "AP":
                        pe.wait_ge(gate_ready, (i + 1) * NC_)
                        alone(pe)
                        for t in range(TT):
                            last = pe.transpose(bank[:, t * 2 * H:(t + 1) * 2 * H], gate_t[:, t * P:(t + 1) * P],
                                                eye[0:2 * H, 0:2 * H])
                    elif kind == "smax":
                        _, p, h, t, c = step
                        if h == 0 and t == 0 and c == 0:
                            smax_ready(p)
                        s = p % SLOTS
                        last = pe.matmul(bank[:, :], stack[0:3 * DH, s, h, t * P:(t + 1) * P],
                                         stack[0:3 * DH, s, 2 + h, c * CH:(c + 1) * CH], start=True, stop=True)
                    elif kind == "mneg":
                        pe.wait_ge(mm_ready, i * PAIRS + step[1] + 1)
                        last = pe.matmul(bank[0:2 * TT, 0:P], mm[:, :], neg_eye[:, :], start=True, stop=True)
                    elif kind == "den":
                        _, p, c = step
                        pe.wait_ge(u_ready, 1 + (i * PAIRS + p) * NC_ + c + 1)
                        for t in range(HALF):
                            last = pe.transpose(bank[:, t * P:(t + 1) * P], u[:, c, t * P:(t + 1) * P], eye[:, :])
                    elif kind == "bc":
                        _, p, c = step
                        pe.wait_ge(r_ready, (i * PAIRS + p) * NC_ + c + 1)
                        alone(pe)
                        for t in range(TT // NC_):
                            last = pe.transpose(bank[0:2 * DH, t * P:(t + 1) * P],
                                                r_wide[:, c * HALF + t, :, :].rearrange("p h d -> p (h d)"), eye[:, :])
                    elif kind == "CS":
                        for h in range(H):
                            a = DH * (h % 4)
                            for t in range(TT):
                                last = pe.matmul(bank[a:a + DH, h // 4:h // 4 + 1], v_ext[:, t, h, 0:DH],
                                                 ones[:, :], start=(t == 0), stop=(t == TT - 1))
                    elif kind == "RZ":
                        pe.wait_ge(vm_ready, i + 1)
                        pe.wait_ge(chunk_ready, i * NCH + upto("wo"))
                        last = parts(bank[:, :], lambda k: vm[:, 0, k, :], lambda k: vm[:, 1, k, :],
                                     lambda k: w0[:, 0, k, :], lambda k: w0[:, 1, k, :])
                    elif kind == "out":
                        t = step[1]
                        if t == 0:
                            pe.wait_ge(chunk_ready, i * NCH + upto("wo"))
                        pe.wait_ge(ct_split, 1 + i * TT + t + 1)
                        last = parts(bank[:, :], lambda k: qk[:, t % 4, k * P:(k + 1) * P],
                                     lambda k: qk[:, t % 4, D + k * P:D + (k + 1) * P],
                                     lambda k: w0[:, 0, k, :], lambda k: w0[:, 1, k, :])
                    elif kind == "xt":
                        t = step[1]
                        if t % HALF == 0:
                            pe.wait_ge(x_ready, i * TT + t + HALF)
                        for k in range(KT):
                            last = pe.transpose(bank[:, k * P:(k + 1) * P], y[:, t, k * P:(k + 1) * P], eye[:, :])
                    elif kind == "pad":
                        last = pe.matmul(bank[0:2 * TT, 0:P], mm[:, :], neg_eye[:, :], start=True, stop=True)
                    last.then_inc(work_full[n % 2], 1)
                    if step in (("Q", KT - 1, NC_ - 1), ("K", KT - 1, NC_ - 1), ("V", TT - 1), ("out", TT - 1)):
                        pe.drain().then_inc(proj_done, 1)
                    if kind == "out":
                        pe.drain().then_inc(out_done, 1)

        @block.scalar
        def _(act):
            act.wait_ge(const_in, 16 * (6 if masked else 25))
            if not masked:
                act.wait_ge(turn_sem, 1)
                act.activation(turn[:, 0:3, :], turn_in[:, 0:3, :], ACT.Exp, scale=-1.0)
                act.activation(turn[:, 3, :], turn_in[:, 3, :], ACT.Tanh)
                act.drain().then_inc(turn_sem, 1)
                act.wait_ge(turn_sem, 3)
                act.activation(turn[:, 4, :], turn[:, 0, :], ACT.Sin, scale=math.pi)
                act.activation(turn[:, 5, :], turn[:, 0, :], ACT.Sin, scale=-math.pi, bias=half_pi[:, 0:1])
                act.drain().then_inc(turn_sem, 1)
                act.wait_ge(turn_sem, 5)
                act.dma_start(io["wo_turned"].rearrange("(k p) d -> p k d", p=P), y[:, 0:KT, :])\
                   .then_inc(turn_sem, 16)
            with act.Fori(0, B) as i:
                def split_hi(what):
                    wait_place(act, i, what)
                    alone(act)
                    for n in chunks_of(what):
                        act.wait_ge(stage_full[n % 2], (i * (NCH // 2) + nth_in_slot(n)) * 16)
                        act.activation(chunk_parts(*chunks[n])[0], stage[:, n % 2, :], ACT.Copy).then_inc(hi_split, 1)

                def load_next_pieces(step):
                    m = mask_steps.index(step) + 1
                    for n in mask_pieces(mask_steps[m]) if m < len(mask_steps) else ():
                        load_piece(n)

                def load_piece(n):
                    src = io["mask_q"] if n < TT else io["mask_k"]
                    t = n % TT
                    act.wait_ge(mstage_free, 1 + i * 2 * TT + max(n - 1, 0))
                    alone(act)
                    act.dma_start(mstage[:, n % 2, :],
                                  src[bass.ds(i, 1), t * P:(t + 1) * P, :].rearrange("b p s -> (b p) s"))\
                       .then_inc(mstage_full[n % 2], 16)

                for step in steps:
                    kind = step[0]
                    if step == ("Q", 0, 0):
                        if masked:
                            load_piece(0)
                        split_hi("wq")
                    if step == ("K", 0, 0) and masked:
                        act.wait_ge(proj_done, 1 + i * 4 + 1)
                        act.wait_ge(x2_raw, (i + 1) * 16)
                        alone(act)
                        for k in range(KT):
                            act.activation(x_hi[:, k, :], kv_raw[:, k, :], ACT.Copy).then_inc(x2_hi, 1)
                    if kind in ("Q", "K"):
                        _, g, c = step
                        bank, free = wait_full(act, i, step)
                        if g == 0 and c == 0:
                            if kind == "Q":
                                act.wait_ge(ct_split, 1 + i * TT)
                            else:
                                if not masked:
                                    act.wait_ge(turn_sem, 21)
                                act.wait_ge(stored, 1 + i * 16)
                        dst = (q_raw if kind == "Q" else k_raw)[:, g, c * CH:(c + 1) * CH]
                        if masked:
                            bias = (bq if kind == "Q" else bk)[:, g:g + 1]
                            act.activation(dst, bank[:, :], ACT.Identity, bias=bias).then_inc(free, 1)
                            load_next_pieces(step)
                        else:
                            act.activation(dst, bank[:, :], ACT.Copy).then_inc(free, 1)
                    elif kind == "V" and masked:
                        load_next_pieces(step)
                    elif kind == "EX":
                        c = step[1]
                        act.wait_ge(gate_sum, i * NC_ + c + 1)
                        z = gate_t[:, c * CH:(c + 1) * CH]
                        act.activation(z, z, ACT.Exp, scale=-1.0).then_inc(gate_exp, 1)
                    elif kind == "mneg":
                        bank, free = wait_full(act, i, step)
                        p = step[1]
                        if p > 0:
                            s = (p - 1) % SLOTS
                            act.wait_ge(mrow_in[s], (i * len(pair_slots[s]) + pair_slots[s].index(p - 1) + 1) * 16)
                        act.activation(mrow[:, :], bank[0:2 * TT, 0:P], ACT.Copy).then_inc(free, 1)
                        act.drain().then_inc(mrow_ready, 1)
                    elif kind == "RZ":
                        bank, free = wait_full(act, i, step)
                        act.activation(rz[:, :], bank[:, :], ACT.Copy).then_inc(free, 1)
                        act.drain().then_inc(rz_ready, 1)
                    elif kind == "pad":
                        bank, free = wait_full(act, i, step)
                        alone(act)
                        act.drain().then_inc(free, 1)
                    elif kind == "st":
                        _, p, kt, h = step
                        n = 2 * (p * TT + kt) + h
                        act.wait_ge(st_full, 1 + i * H * TT + n + 1)
                        if n >= PRING:
                            act.wait_ge(pv_done, 1 + i * PAIRS * TT + p * TT + kt - PRING // 2 + 1)
                        act.activation(probs[:, n % PRING, :], scores[n % 2][:, :], ACT.Exp,
                                       scale=SCALE).then_inc(p_full, 1)
                    elif kind == "xt":
                        t = step[1]
                        if t == 0:
                            for c in range(NC_):
                                half = slice(c * HALF, (c + 1) * HALF)
                                act.wait_ge(var_ready, i * NC_ + c + 1)
                                act.activation(sd[:, half], tmp[:, half], ACT.Sqrt).then_inc(sd_ready, 1)
                        if t == TT - 1:
                            act.wait_ge(x_ready, i * TT + TT)
                            alone(act)
                            act.dma_start(io["out"][bass.ds(i, 1), :, :].rearrange("b (t p) d -> p (b t) d", p=P), y)\
                               .then_inc(stored, 16)
                        bank, free = wait_full(act, i, step)
                        act.activation(xts[:, :, t * P:(t + 1) * P], bank[:, :].rearrange("p (k n) -> p k n", k=KT),
                                       ACT.Copy).then_inc(free, 1)
                        if t % HALF == HALF - 1:
                            c = t // HALF
                            act.drain().then_inc(xt_ready, 1)
                            act.wait_ge(xt_ready, i * NC_ + c + 1)
                            act.dma_start(io["out_t"][bass.ds(i, 1), :, c * CH:(c + 1) * CH]
                                          .rearrange("b (k p) s -> p (b k) s", p=P), xts[:, :, c * CH:(c + 1) * CH])\
                               .then_inc(xt_stored, 16)
            act.wait_ge(stored, 1 + B * 16)
            act.wait_ge(xt_stored, 1 + B * NC_ * 16)

        @block.vector
        def _(dve):
            dve.memset(acc[:, :, :], 1e-30 if masked else 0.0).then_inc(setup, 1)
            dve.wait_ge(const_in, 16 * (6 if masked else 25))
            if masked:
                dve.memset(ones[:, :], 1.0)
                dve.memset(v_ext[:, :, :, DH:VW], 1.0)
                dve.tensor_scalar(eye8[:, :], eye[:, :], 16384.0, None, ALU.mult, saturate=False)
            else:
                dve.memset(v_ext[:, :, :, DH + 1:VW], 1.0)
                dve.memset(half_pi[:, :], math.pi / 2)
                dve.drain().then_inc(setup, 1)
                dve.tensor_scalar(turn_in[:, 0:3, :], turn_in[:, 0:3, :], -87.0, None, ALU.max)
                dve.drain().then_inc(turn_sem, 1)
                dve.wait_ge(turn_sem, 2)
                dve.tensor_scalar(turn[:, 0:3, :], turn[:, 0:3, :], 1.0, None, ALU.add)
                dve.drain()
                dve.reciprocal(turn[:, 0:3, :], turn[:, 0:3, :])
                dve.drain().then_inc(turn_sem, 1)
                dve.wait_ge(turn_sem, 4)
                dve.tensor_tensor(turn[:, 6, :], turn[:, 1, :], turn[:, 2, :], ALU.mult)
                dve.drain()
                dve.tensor_tensor(turn[:, 6, :], turn[:, 6, :], turn[:, 3, :], ALU.mult)
                dve.drain()
                dve.tensor_tensor(turn[:, 5, :], turn[:, 5, :], turn[:, 6, :], ALU.mult)
                dve.tensor_tensor(turn[:, 7, :], turn[:, 4, :], turn[:, 6, :], ALU.mult)
                dve.drain()
                dve.tensor_scalar(turn[:, 7, :], turn[:, 7, :], sign[:, 0:1], None, ALU.mult)
                dve.drain()
                wo_as_is = q_raw[:, 0:2, :].rearrange("p g (a d) -> p (g a) d", d=D)
                wo_swapped = q_raw[:, 2:4, :].rearrange("p g (a d) -> p (g a) d", d=D)
                for k in range(KT):
                    dve.tensor_scalar(y[:, k, :], wo_as_is[:, k, :], turn[:, 5, k:k + 1], None, ALU.mult)
                dve.drain()
                for k in range(KT):
                    dve.scalar_tensor_tensor(out=y[:, k, :], in0=wo_swapped[:, k, :], scalar=turn[:, 7, k:k + 1],
                                             in1=y[:, k, :], op0=ALU.mult, op1=ALU.add)
                dve.drain().then_inc(turn_sem, 1)
            if masked:
                dve.drain().then_inc(setup, 1)
            with dve.Fori(0, B) as i:
                def take_sums(p):
                    alone(dve)
                    dve.drain()
                    dve.wait_ge(pv_done, 1 + i * PAIRS * TT + (p + 1) * TT)
                    for c in range(NC_):
                        dve.tensor_copy(u[:, c, :], acc[:, c, :]).then_inc(u_ready, 1)

                def split_lo(what):
                    wait_place(dve, i, what)
                    alone(dve)
                    for j, n in enumerate(chunks_of(what)):
                        hi, lo = chunk_parts(*chunks[n])
                        dve.wait_ge(hi_split, i * SHARED + j + 1)
                        alone(dve)
                        dve.tensor_tensor(lo, stage[:, n % 2, :], hi.bitcast(F32), ALU.subtract)\
                           .then_inc(stage_free, 1)
                        dve.drain().then_inc(chunk_ready, 1)

                def maxima(p):
                    if p > 0:
                        n = use_no[("mneg", p - 1)]
                        dve.wait_ge(work_full[n % 2], i * PER + n // 2 + 1)
                    alone(dve)
                    dve.drain()
                    m = mx[:, p % 2, :].rearrange("p (n c) -> p n c", c=NC_)
                    if p == 0:
                        m = mx[:, 0, 0:2 * TT].unsqueeze(2).to_broadcast([P, 2 * TT, 2])
                    if masked:
                        dve.tensor_tensor(mm[:, :], m[:, :, 0], m[:, :, 1], ALU.max)
                        dve.drain()
                        if p == 0:
                            dve.tensor_scalar(none[:, :], mm[:, 0:TT], ABSENT, None, ALU.is_lt)
                            dve.drain()
                        dve.tensor_scalar(mm[:, :], mm[:, :], ABSENT, None, ALU.max).then_inc(mm_ready, 1)
                    else:
                        dve.tensor_tensor(mm[:, :], m[:, :, 0], m[:, :, 1], ALU.max).then_inc(mm_ready, 1)

                def convert_mask_pieces(pieces):
                    for n in pieces:
                        t = n % TT
                        dve.wait_ge(mstage_full[n % 2], (i * TT + n // 2 + 1) * 16)
                        alone(dve)
                        mask, fill = (mask_q, MASKED) if n < TT else (mask_k, MASKED / 16384.0)
                        dve.tensor_scalar(mask[:, t, :], mstage[:, n % 2, :], 0, fill,
                                          ALU.is_equal, ALU.mult, saturate=False).then_inc(mstage_free, 1)

                for step in steps:
                    kind = step[0]
                    if step == ("Q", 0, 0):
                        split_lo("wq")
                    if step == ("K", 0, 0) and masked:
                        dve.wait_ge(proj_done, 1 + i * 4 + 1)
                        alone(dve)
                        for k in range(KT):
                            dve.wait_ge(x2_hi, i * KT + k + 1)
                            dve.tensor_tensor(x_lo[:, k, :], kv_raw[:, k, :], x_hi[:, k, :].bitcast(F32),
                                              ALU.subtract)
                            dve.drain().then_inc(x2_ready, 1)
                        dve.wait_ge(st_full, 1 + i * H * TT)
                        alone(dve)
                    if kind == "V":
                        t = step[1]
                        bank, free = wait_full(dve, i, step)
                        val = bank[:, :].rearrange("p (h d) -> p h d", h=H)
                        if masked:
                            dve.tensor_tensor(v_ext[:, t, :, 0:DH], val,
                                              bv[:, :].rearrange("p (h d) -> p h d", h=H), ALU.add).then_inc(free, 1)
                            convert_mask_pieces(mask_pieces(step))
                            if t == TT - 1:
                                dve.drain().then_inc(maskk_ready, 1)
                        else:
                            dve.tensor_tensor(v_ext[:, t, :, 0:DH], val,
                                              gate[:, t, H:2 * H].unsqueeze(2).to_broadcast([P, H, DH]),
                                              ALU.mult).then_inc(free, 1)
                    elif kind in ("Q", "K") and masked:
                        convert_mask_pieces(mask_pieces(step))
                    elif kind == "EX":
                        bank, free = wait_full(dve, i, step)
                        c = step[1]
                        z = gate_t[:, c * CH:(c + 1) * CH]
                        dve.tensor_scalar(z, bank[0:2 * H, :], bsm[:, 0:1], -87.0, ALU.add, ALU.max).then_inc(free, 1)
                        dve.drain().then_inc(gate_sum, 1)
                        dve.wait_ge(gate_exp, i * NC_ + c + 1)
                        alone(dve)
                        dve.tensor_scalar(z, z, 1.0, None, ALU.add)
                        dve.drain()
                        dve.reciprocal(z, z)
                        dve.drain().then_inc(gate_ready, 1)
                    elif kind == "AP":
                        bank, free = wait_full(dve, i, step)
                        dve.tensor_copy(gate[:, :, :], bank[:, 0:TT * 2 * H].rearrange("p (t h) -> p t h", t=TT))\
                           .then_inc(free, 1)
                        dve.drain()
                        dve.tensor_copy(v_ext[:, :, :, DH:DH + 1], gate[:, :, H:2 * H].unsqueeze(3))
                    elif kind == "smax0":
                        _, h, t = step
                        n = h * TT + t
                        dve.wait_ge(smax0_full, i * 2 * TT + n + 1)
                        alone(dve)
                        if masked:
                            dve.tensor_tensor_reduce(scores[n % 2][:, :], scores[n % 2][:, :], mask_q[:, t, :],
                                                     1.0, -3e38, ALU.add, ALU.max,
                                                     mx[:, 0, n:n + 1]).then_inc(smax0_free, 1)
                        else:
                            dve.tensor_reduce(mx[:, 0, n:n + 1], scores[n % 2][:, :], AX.X,
                                              ALU.max).then_inc(smax0_free, 1)
                        if n == 2 * TT - 1:
                            maxima(0)
                    elif kind == "smax":
                        _, p, h, t, c = step
                        bank, free = wait_full(dve, i, step)
                        j = (h * TT + t) * NC_ + c
                        if masked:
                            alone(dve)
                            dve.tensor_tensor_reduce(bank[:, :], bank[:, :], mask_q[:, t, c * CH:(c + 1) * CH],
                                                     1.0, -3e38, ALU.add, ALU.max,
                                                     mx[:, p % 2, j:j + 1]).then_inc(free, 1)
                        else:
                            dve.tensor_reduce(mx[:, p % 2, j:j + 1], bank[:, :], AX.X, ALU.max).then_inc(free, 1)
                        if (h, t, c) == (1, TT - 1, NC_ - 1):
                            maxima(p)
                    elif kind == "CS":
                        bank, free = wait_full(dve, i, step)
                        dve.tensor_scalar(vmean[:, :], bank[:, 0:KT], 1.0 / S, None, ALU.mult).then_inc(free, 1)
                        dve.drain()
                        wide_mean = vmean[:, :].unsqueeze(2).to_broadcast([P, KT, P])
                        dve.tensor_copy(vm[:, 0, :, :], wide_mean)
                        dve.drain()
                        dve.tensor_tensor(vm[:, 1, :, :], wide_mean, vm[:, 0, :, :].bitcast(F32), ALU.subtract)
                        dve.drain().then_inc(vm_ready, 1)
                    elif kind == "st":
                        if step == ("st", PAIRS - 1, 4, 0) and masked:
                            dve.wait_ge(bo_added, i + 1)
                            dve.wait_ge(rz_ready, i + 1)
                            for t in range(TT):
                                dve.scalar_tensor_tensor(out=y[:, t, :], in0=rz[:, :], scalar=none[:, t:t + 1],
                                                         in1=y[:, t, :], op0=ALU.mult, op1=ALU.add)
                    elif kind == "pv":
                        if step[2:] == (TT - 1, NC_ - 1):
                            take_sums(step[1])
                    elif kind == "den":
                        bank, free = wait_full(dve, i, step)
                        c = step[2]
                        half = r[:, c * HALF:(c + 1) * HALF, :]
                        sums = bank[:, :].rearrange("p (t h d) -> p t h d", t=HALF, h=2)
                        if masked:
                            dve.tensor_copy(half, sums[:, :, :, DH])
                            dve.drain()
                            dve.tensor_tensor(half, half, sums[:, :, :, DH + 2], ALU.add).then_inc(free, 1)
                            dve.drain()
                            dve.reciprocal(half, half)
                        else:
                            p = step[1]
                            aperture = gate[:, c * HALF:(c + 1) * HALF, 2 * p:2 * p + 2]
                            dve.tensor_tensor(half, sums[:, :, :, DH], aperture, ALU.mult)
                            dve.drain()
                            dve.scalar_tensor_tensor(out=half, in0=sums[:, :, :, DH + 1], scalar=1e-8, in1=half,
                                                     op0=ALU.mult, op1=ALU.add).then_inc(free, 1)
                            dve.drain()
                            dve.reciprocal(half, half)
                            dve.drain()
                            dve.tensor_tensor(half, half, aperture, ALU.mult)
                        dve.drain()
                        dve.tensor_copy(r_wide[:, c * HALF:(c + 1) * HALF, :, :],
                                        half.unsqueeze(3).to_broadcast([P, HALF, 2, DH]))
                        dve.drain().then_inc(r_ready, 1)
                    elif kind == "bc":
                        _, p, c = step
                        bank, free = wait_full(dve, i, step)
                        for h in range(2):
                            a = DH * ((2 * p + h) % 4)
                            last = dve.tensor_tensor(q_raw[a:a + DH, p // 2, c * CH:(c + 1) * CH],
                                                     u[64 * h:64 * h + DH, c, :], bank[DH * h:DH * (h + 1), :],
                                                     ALU.mult)
                        last.then_inc(free, 1)
                        if p == PAIRS - 1:
                            dve.drain().then_inc(ctx_done, 1)
                    elif kind == "out":
                        t = step[1]
                        bank, free = wait_full(dve, i, step)
                        if t == 0:
                            dve.wait_ge(res_in, i * 16 + 16)
                        dve.tensor_tensor(y[:, t, :], bank[:, :], y[:, t, :], ALU.add).then_inc(free, 1)
                        dve.drain()
                        dve.bn_stats(stats[:, :], y[:, t, :])
                        dve.drain()
                        dve.bn_aggr(mv[:, t, :], stats[:, :])
                        c = t // (TT - 1)
                        if t == HALF or t == TT - 1:
                            half = slice(c * HALF, (c + 1) * HALF)
                            dve.drain()
                            dve.tensor_scalar(tmp[:, half], mv[:, half, 1], EPS, None, ALU.add).then_inc(var_ready, 1)
                        if t in (HALF + 1, TT - 1):
                            dve.wait_ge(sd_ready, i * NC_ + c + 1)
                            half = slice(c * HALF, (c + 1) * HALF)
                            alone(dve)
                            dve.reciprocal(rstd[:, half], sd[:, half])
                            dve.drain()
                            dve.tensor_tensor(sd[:, half], rstd[:, half], rstd[:, half], ALU.mult)
                            dve.drain()
                            dve.tensor_tensor(sd[:, half], sd[:, half], tmp[:, half], ALU.mult)
                            dve.drain()
                            dve.tensor_scalar(sd[:, half], sd[:, half], -0.5, 1.5, ALU.mult, ALU.add)
                            dve.drain()
                            dve.tensor_tensor(rstd[:, half], rstd[:, half], sd[:, half], ALU.mult)
                            dve.drain()
                        if t > HALF:
                            ready = range((t - HALF - 1) * 2, (t - HALF) * 2) if t < TT - 1 else range(HALF, TT)
                            for q in ready:
                                dve.tensor_scalar(y[:, q, :], y[:, q, :], mv[:, q, 0:1], rstd[:, q:q + 1],
                                                  ALU.subtract, ALU.mult).then_inc(x_ready, 1)


SUM = 32
WS, WK = 4, 2
E = 16
HD = 64
WIDE = E * HD
FK = WIDE // P
RING = 8
INV = HD ** -0.5


def ffn_steps():
    steps = [("SQ", 0), ("SQ", 1), ("LT", 0), ("LT", 1), ("LG",)] + [("proj", w, t) for w in range(6) for t in range(TT)]
    steps += [("turn", n) for n in range(TT // 2)]
    halves = lambda qt: range(1 if qt < TT // 2 else 2)
    for n in range(TT + 2):
        if 2 <= n:
            steps += [("mixed_t", n - 2, g) for g in range(2)]
        if 1 <= n <= TT:
            steps += [("prob_t", n - 1, c) for c in halves(n - 1)]
        if n < TT:
            steps += [("score", n, c) for c in halves(n)]
        if 1 <= n <= TT:
            steps.append(("pv", n - 1))
        if 2 <= n:
            steps.append(("out", n - 2))
    while len(steps) % RING:
        steps.append(("pad", len(steps) % RING))
    return steps


def expert_layer(nc, io):
    steps = ffn_steps()
    PER = len(steps) // RING
    use_no = {s: n for n, s in enumerate(steps)}
    ctx = ExitStack()
    with ctx:
        used = [0]
        size = nc.sbuf_bytes_remaining // 64 * 64
        start = -(-nc.sbuf_base // 64) * 64
        ctx.enter_context(nc.sbuf_tensor("arena_e", [P, size], mybir.dt.uint8))

        def sb(name, shape, dt=F32, at=None):
            n = 4
            for k in shape[1:]:
                n *= k
            if at is None:
                at = start + used[0]
                used[0] += -(-n // 64) * 64
                assert used[0] + 64 <= size, (name, used[0], size)
            place[name] = at
            return nc.alloc_sbuf_tensor_at(f"{name}_e", shape, dt, offset=at)

        place = {}
        sem = lambda n: ctx.enter_context(nc.semaphore(f"{n}_e"))

        w_in = sb("w_in", [P, 6, 2, KT, CH], F32R)
        w_out = sb("w_out", [P, 2, FK, D], F32R)
        x = sb("x", [P, 2, KT, S], F32R)
        prob = sb("prob", [P, 2, S], at=place["x"])
        mixed_t = sb("mixed_t", [P, 2, FK, P], F32R, at=place["x"] + 8 * S)
        prob_t = sb("prob_t", [P, TT, P])
        y = sb("y", [P, TT, D])
        w_stage = sb("w_stage", [P, WS, WK, CH], at=place["y"])
        weighted = sb("weighted", [P, 2, CH])
        mixed = sb("mixed", [P, E, HD], at=place["weighted"])
        lg_t = sb("lg_t", [SUM + 1, S], at=place["weighted"])
        part = sb("part", [P, HD])
        qkv = sb("qkv", [P, 3, TT, HD])
        q_t = sb("q_t", [HD, S])
        k_t = sb("k_t", [HD, S])
        eye = sb("eye", [P, P])
        causal = sb("causal", [P, P])
        lower = sb("lower", [P, E, E])
        squares = sb("squares", [P, 2, S], at=place["q_t"])
        sim_raw = sb("sim_raw", [P, KT, E])
        sim_sq = sb("sim_sq", [P, KT, E])
        sim = sb("sim", [P, 2, KT, SUM], F32R)
        ones = sb("ones", [P, P])
        norm = sb("norm", [P, 4, E])
        gates = sb("gates", [P, E])
        lg = sb("lg", [P, TT, E])
        rw = sb("rw", [P, TT, E])
        pick = sb("pick", [P, TT, E])
        beats = sb("beats", [P, TT, E, E], at=place["q_t"])
        small = sb("small", [P, 10, TT])
        nmax = sb("nmax", [P, TT, 2])
        total = sb("total", [P, TT, 2])
        rtot = sb("rtot", [P, TT])
        attn = sb("attn", [P, HD])
        stats = sb("stats", [P, 6])
        mv = sb("mv", [P, TT, 2])
        sd = sb("sd", [P, TT])
        rstd = sb("rstd", [P, TT])
        tmp = sb("tmp", [P, TT])

        bank_of = [ctx.enter_context(nc.psum_tensor(f"work{b}_e", [P, CH], F32)) for b in range(RING)]

        const_in = sem("const_in")
        setup = sem("setup")
        apart = sem("apart")
        norm_sem = sem("norm_sem")
        work_full = [sem(f"work_full{b}") for b in range(RING)]
        work_free = [sem(f"work_free{b}") for b in range(RING)]
        stage_full = [sem(f"stage_full{b}") for b in range(WS)]
        stage_free = sem("stage_free")
        w_hi = sem("w_hi")
        w_ready = sem("w_ready")
        x_over = sem("x_over")
        x_raw = sem("x_raw")
        x_hi = sem("x_hi")
        squared = sem("squared")
        squares_used = sem("squares_used")
        scores_done = sem("scores_done")
        sums_in = sem("sums_in")
        lt_ready = sem("lt_ready")
        x_ready = sem("x_ready")
        proj_done = sem("proj_done")
        res_in = sem("res_in")
        roots = sem("roots")
        lg_ready = sem("lg_ready")
        exp_ready = sem("exp_ready")
        qkv_ready = sem("qkv_ready")
        turned_in = sem("turned_in")
        masked_in = sem("masked_in")
        prob_ready = sem("prob_ready")
        prob_t_ready = sem("prob_t_ready")
        mixed_ready = sem("mixed_ready")
        hi_ready = sem("hi_ready")
        lo_ready = sem("lo_ready")
        var_ready = sem("var_ready")
        sd_ready = sem("sd_ready")
        y_ready = sem("y_ready")
        stored = sem("stored")

        w_chunks = [w_in[:, w, :, k:k + WK, :] for w in range(6) for k in range(0, KT, WK)]
        w_chunks += [w_out[:, :, k:k + WK, :] for k in range(0, FK, WK)]
        NW = len(w_chunks)
        halves = lambda qt: range(1 if qt < TT // 2 else 2)
        keys = lambda qt, c: min(CH, (qt + 1) * P - c * CH)
        scored = lambda qt: sum(len(halves(q)) for q in range(qt + 1))
        SC = scored(TT - 1)

        def turned_logits(bank):
            return bank[:, 0:TT * (SUM + 1)].rearrange("p (t e) -> p t e", t=TT)

        def wait_full(eng, i, step):
            n = use_no[step]
            eng.wait_ge(work_full[n % RING], i * PER + n // RING + 1)
            return bank_of[n % RING], work_free[n % RING]

        def alone(eng):
            eng.sem_inc(apart, 1)

        block = ctx.enter_context(nc.Block("experts"))

        @block.sync
        def _(sp):
            for t, src in ((eye, io["eye"]), (causal, io["causal"])):
                sp.dma_start(t[:, :], src).then_inc(const_in, 16)
            sp.dma_start(lower[:, :, :], io["lower"].partition_broadcast(P)).then_inc(const_in, 16)
            sp.dma_start(gates[:, :], io["gates"].partition_broadcast(P)).then_inc(const_in, 16)
            sp.dma_start(sim_raw[:, :, :], io["sim"].rearrange("(k p) e -> p k e", p=P)).then_inc(const_in, 16)

            def load_x(i):
                sp.dma_start(x[:, 1, :, :].bitcast(F32), io["src_t"][bass.ds(i, 1), :, :]
                             .rearrange("b (k p) s -> p (b k) s", p=P)).then_inc(x_raw, 16)

            def load_res(i):
                sp.dma_start(y[:, :, :], io["res"][bass.ds(i, 1), :, :].rearrange("b (t p) d -> p (b t) d", p=P))\
                  .then_inc(res_in, 16)

            def store(i):
                sp.dma_start(io["out"][bass.ds(i, 1), :, :].rearrange("b (t p) d -> p (b t) d", p=P), y[:, :, :])\
                  .then_inc(stored, 16)

            for n in range(NW):
                if n == WS:
                    load_x(0)
                if n >= WS:
                    sp.wait_ge(stage_free, n - WS + 1)
                w, k = n // (KT // WK), n % (KT // WK) * WK
                if w < 6:
                    src = io[("wq", "wk", "wv")[w // 2]][k * P:(k + WK) * P, (w % 2) * CH:(w % 2 + 1) * CH]
                else:
                    k = (n - 6 * KT // WK) * WK
                    src = io["wo"][k * P:(k + WK) * P, :]
                sp.dma_start(w_stage[:, n % WS, :, :], src.rearrange("(k p) n -> p k n", p=P))\
                  .then_inc(stage_full[n % WS], 16)
            sp.wait_ge(stage_free, NW)
            load_res(0)
            sp.wait_ge(setup, 3)
            with sp.Fori(0, B - 1) as i:
                sp.wait_ge(proj_done, i + 1)
                alone(sp)
                load_x(i + 1)
                sp.wait_ge(y_ready, i * TT + TT)
                alone(sp)
                store(i)
                sp.wait_ge(stored, 1 + (i + 1) * 16)
                alone(sp)
                load_res(i + 1)
            sp.wait_ge(y_ready, B * TT)
            store(B - 1)
            sp.wait_ge(stored, 1 + B * 16)

        @block.gpsimd
        def _(pool):
            for count in (*work_free, x_over, squares_used, scores_done, stored):
                pool.sem_inc(count, 1)
            pool.drain().then_inc(setup, 1)
            pool.wait_ge(setup, 3)
            with pool.Fori(0, B) as i:
                pool.wait_ge(scores_done, 1 + i)
                pool.wait_ge(x_raw, i * 16 + 16)
                alone(pool)
                for k in range(KT):
                    if k >= 2:
                        pool.wait_ge(squares_used, 1 + i * KT + k - 1)
                        alone(pool)
                    raw = x[:, 1, k, :].bitcast(F32)
                    pool.tensor_tensor(squares[:, k % 2, :], raw, raw, ALU.mult).then_inc(squared, 1)

        @block.tensor
        def _(pe):
            pe.wait_ge(setup, 3)
            pe.wait_ge(norm_sem, 1)
            for k in range(KT):
                last = pe.matmul(bank_of[0][:, 0:E], ones[:, :], sim_sq[:, k, :], start=(k == 0), stop=(k == KT - 1))
            last.then_inc(norm_sem, 1)
            pe.wait_ge(norm_sem, 5)
            with pe.Fori(0, B) as i:
                def parts(out, hi_l, lo_l, hi_r, lo_r, tiles=KT, ready=None):
                    for k in range(tiles):
                        if ready:
                            ready(k)
                        for n, (a, b) in enumerate(((hi_l, hi_r), (hi_l, lo_r), (lo_l, hi_r))):
                            last = pe.matmul(out, a(k), b(k), start=(k == 0 and n == 0),
                                             stop=(k == tiles - 1 and n == 2))
                    return last

                for n, step in enumerate(steps):
                    kind = step[0]
                    bank = bank_of[n % RING]
                    pe.wait_ge(work_free[n % RING], 1 + i * PER + n // RING)
                    if step == ("SQ", 1):
                        for k in range(KT):
                            pe.wait_ge(squared, i * KT + k + 1)
                            alone(pe)
                            for c in range(NC_):
                                last = pe.matmul(bank_of[n - 1 + c][SUM:SUM + 32, :], ones[:, 0:32],
                                                 squares[:, k % 2, c * CH:(c + 1) * CH],
                                                 start=(k == 0), stop=(k == KT - 1), skip_group_check=True)
                            pe.drain().then_inc(squares_used, 1)
                        pe.drain().then_inc(work_full[n - 1], 1)
                    elif kind == "SQ":
                        continue
                    elif kind == "LT":
                        c = step[1]
                        last = parts(bank[0:SUM, :], lambda k: sim[:, 0, k, :], lambda k: sim[:, 1, k, :],
                                     lambda k: x[:, 0, k, c * CH:(c + 1) * CH],
                                     lambda k: x[:, 1, k, c * CH:(c + 1) * CH],
                                     ready=lambda k: pe.wait_ge(x_ready, i * KT + k + 1))
                    elif kind == "LG":
                        pe.wait_ge(lt_ready, i + 1)
                        alone(pe)
                        for t in range(TT):
                            last = pe.transpose(bank[:, t * (SUM + 1):(t + 1) * (SUM + 1)],
                                                lg_t[:, t * P:(t + 1) * P], eye[0:SUM + 1, 0:SUM + 1])
                    elif kind == "proj":
                        _, w, t = step
                        if t == 0:
                            pe.wait_ge(w_ready, (w + 1) * KT // WK)
                        last = parts(bank[:, :], lambda k: x[:, 0, k, t * P:(t + 1) * P],
                                     lambda k: x[:, 1, k, t * P:(t + 1) * P],
                                     lambda k: w_in[:, w, 0, k, :], lambda k: w_in[:, w, 1, k, :])
                    elif kind == "turn":
                        if step[1] == 0:
                            pe.wait_ge(qkv_ready, i + 1)
                        alone(pe)
                        for j in range(2):
                            for part_ in range(2):
                                at = (2 * part_ + j) * P
                                last = pe.transpose(bank[0:HD, at:at + P], qkv[:, part_, 2 * step[1] + j, :], eye[:, :])
                    elif kind == "score":
                        _, qt, c = step
                        if qt == 0:
                            pe.wait_ge(turned_in, i + 1)
                        last = pe.matmul(bank[:, 0:keys(qt, c)], q_t[:, qt * P:(qt + 1) * P],
                                         k_t[:, c * CH:c * CH + keys(qt, c)], start=True, stop=True)
                    elif kind == "prob_t":
                        _, qt, c = step
                        pe.wait_ge(prob_ready, i * SC + scored(qt) - len(halves(qt)) + c + 1)
                        for j in range(keys(qt, c) // P):
                            last = pe.transpose(bank[:, j * P:(j + 1) * P],
                                                prob[:, qt % 2, c * CH + j * P:c * CH + (j + 1) * P], eye[:, :])
                    elif kind == "pv":
                        qt = step[1]
                        pe.wait_ge(prob_t_ready, i * TT + qt + 1)
                        for kt in range(qt + 1):
                            last = pe.matmul(bank[:, 0:HD], prob_t[:, kt, :], qkv[:, 2, kt, :],
                                             start=(kt == 0), stop=(kt == qt))
                    elif kind == "mixed_t":
                        _, qt, g = step
                        pe.wait_ge(mixed_ready, i * TT + qt + 1)
                        for j in range(FK // 2):
                            at = (g * FK // 2 + j) * P
                            last = pe.transpose(bank[:, j * P:(j + 1) * P],
                                                mixed[:, :, :].rearrange("p e d -> p (e d)")[:, at:at + P], eye[:, :])
                    elif kind == "out":
                        qt = step[1]
                        pe.wait_ge(lo_ready, (i * TT + qt + 1) * 2)
                        if qt == 0:
                            pe.wait_ge(w_ready, NW)
                        last = parts(bank[:, :], lambda k: mixed_t[:, 0, k, :], lambda k: mixed_t[:, 1, k, :],
                                     lambda k: w_out[:, 0, k, :], lambda k: w_out[:, 1, k, :], FK)
                    elif kind == "pad":
                        last = pe.matmul(bank[:, 0:P], ones[:, :], eye[:, :], start=True, stop=True)
                    last.then_inc(work_full[n % RING], 1)
                    if step == ("proj", 5, TT - 1):
                        pe.drain().then_inc(proj_done, 1)
                    if step == ("score", TT - 1, 1):
                        pe.drain().then_inc(scores_done, 1)
                    if step == ("out", TT - 1):
                        pe.drain().then_inc(x_over, 1)

        @block.scalar
        def _(act):
            act.wait_ge(norm_sem, 3)
            act.activation(norm[:, 1, :], norm[:, 0, :], ACT.Sqrt)
            act.drain()
            act.activation(norm[:, 2, :], gates[:, :], ACT.Exp, scale=-1.0)
            act.drain().then_inc(norm_sem, 1)
            act.wait_ge(setup, 3)
            for n, w in enumerate(w_chunks):
                act.wait_ge(stage_full[n % WS], 16 * (n // WS + 1))
                act.activation(w[:, 0, :, :], w_stage[:, n % WS, :, :], ACT.Copy).then_inc(w_hi, 1)
            with act.Fori(0, B) as i:
                act.wait_ge(x_over, 1 + i)
                act.wait_ge(x_raw, i * 16 + 16)
                alone(act)
                for k in range(KT):
                    act.activation(x[:, 0, k, :], x[:, 1, k, :].bitcast(F32), ACT.Copy).then_inc(x_hi, 1)
                for step in steps:
                    kind = step[0]
                    if kind == "SQ":
                        bank, free = wait_full(act, i, step)
                        c = step[1]
                        act.activation(lg_t[SUM:SUM + 1, c * CH:(c + 1) * CH], bank[SUM:SUM + 1, :],
                                       ACT.Copy).then_inc(free, 1)
                    elif kind == "LT":
                        bank, free = wait_full(act, i, step)
                        c = step[1]
                        act.activation(lg_t[0:SUM, c * CH:(c + 1) * CH], bank[0:SUM, :], ACT.Copy).then_inc(free, 1)
                        if c == 1:
                            act.drain().then_inc(lt_ready, 1)
                    elif kind == "LG":
                        act.wait_ge(sums_in, i + 1)
                        act.activation(small[:, 1, :], small[:, 0, :], ACT.Sqrt)
                        act.drain().then_inc(roots, 1)
                        act.wait_ge(lg_ready, i + 1)
                        act.activation(pick[:, :, :], pick[:, :, :], ACT.Exp)
                        act.drain().then_inc(exp_ready, 1)
                    elif kind == "turn":
                        n = step[1]
                        bank, free = wait_full(act, i, step)
                        act.activation(q_t[:, 2 * n * P:(2 * n + 2) * P], bank[0:HD, 0:2 * P], ACT.Copy)
                        act.activation(k_t[:, 2 * n * P:(2 * n + 2) * P], bank[0:HD, 2 * P:4 * P], ACT.Copy)\
                           .then_inc(free, 1)
                        if n == TT // 2 - 1:
                            act.drain().then_inc(turned_in, 1)
                    elif kind == "score":
                        _, qt, c = step
                        act.wait_ge(masked_in, i * TT + qt + 1)
                        bank, free = wait_full(act, i, step)
                        act.activation(prob[:, qt % 2, c * CH:c * CH + keys(qt, c)], bank[:, 0:keys(qt, c)], ACT.Exp,
                                       scale=INV, bias=nmax[:, qt, 0:1], accum_out=total[:, qt, c:c + 1])\
                           .then_inc(free, 1)
                        act.drain().then_inc(prob_ready, 1)
                    elif kind == "prob_t":
                        _, qt, c = step
                        bank, free = wait_full(act, i, step)
                        act.activation(prob_t[:, c * 4:c * 4 + keys(qt, c) // P, :].rearrange("p k n -> p (k n)"),
                                       bank[:, 0:keys(qt, c)], ACT.Copy).then_inc(free, 1)
                        if c == halves(qt)[-1]:
                            act.drain().then_inc(prob_t_ready, 1)
                    elif kind == "mixed_t":
                        _, qt, g = step
                        n = use_no[step]
                        act.wait_ge(work_full[n % RING], i * PER + n // RING + 1)
                        act.activation(mixed_t[:, 0, g * 4:g * 4 + 4, :].rearrange("p k n -> p (k n)"),
                                       bank_of[n % RING][:, :], ACT.Copy)
                        act.drain().then_inc(hi_ready, 1)
                    elif kind == "pad":
                        bank, free = wait_full(act, i, step)
                        alone(act)
                        act.drain().then_inc(free, 1)
                    if step in (("out", HALF), ("out", TT - 1)):
                        c = step[1] // (TT - 1)
                        half = slice(c * HALF, (c + 1) * HALF)
                        act.wait_ge(var_ready, i * NC_ + c + 1)
                        act.activation(sd[:, half], tmp[:, half], ACT.Sqrt).then_inc(sd_ready, 1)

        @block.vector
        def _(dve):
            dve.memset(ones[:, :], 1.0)
            dve.memset(sim[:, :, :, :].bitcast(F32), 0.0)
            dve.wait_ge(const_in, 16 * 5)
            dve.tensor_tensor(sim_sq[:, :, :], sim_raw[:, :, :], sim_raw[:, :, :], ALU.mult)
            dve.drain().then_inc(setup, 1)
            dve.engine_nop().then_inc(setup, 1)
            dve.engine_nop().then_inc(norm_sem, 1)
            dve.wait_ge(norm_sem, 2)
            dve.tensor_copy(norm[:, 0, :], bank_of[0][:, 0:E])
            dve.tensor_scalar(gates[:, :], gates[:, :], -87.0, None, ALU.max)
            dve.drain().then_inc(norm_sem, 1)
            dve.wait_ge(norm_sem, 4)

            def better_root(out, sq, root, hold):
                dve.tensor_scalar(root, root, 1e-12, None, ALU.max)
                dve.drain()
                dve.reciprocal(hold, root)
                dve.drain()
                dve.tensor_tensor(hold, hold, sq, ALU.mult)
                dve.drain()
                dve.tensor_tensor(hold, hold, root, ALU.add)
                dve.drain()
                dve.tensor_scalar(out, hold, 0.5, 1e-12, ALU.mult, ALU.max)
                dve.drain()

            better_root(norm[:, 1, :], norm[:, 0, :], norm[:, 1, :], norm[:, 3, :])
            dve.reciprocal(norm[:, 1, :], norm[:, 1, :])
            dve.drain()
            dve.tensor_tensor(sim_sq[:, :, :], sim_raw[:, :, :], norm[:, 1, :].unsqueeze(1).to_broadcast([P, KT, E]),
                              ALU.mult)
            dve.tensor_scalar(norm[:, 2, :], norm[:, 2, :], 1.0, None, ALU.add)
            dve.drain()
            dve.reciprocal(gates[:, :], norm[:, 2, :])
            dve.tensor_copy(sim[:, 0, :, 0:E], sim_sq[:, :, :])
            dve.drain()
            dve.tensor_tensor(sim[:, 1, :, 0:E], sim_sq[:, :, :], sim[:, 0, :, 0:E].bitcast(F32), ALU.subtract)
            dve.drain().then_inc(norm_sem, 1)
            for n, w in enumerate(w_chunks):
                dve.wait_ge(w_hi, n + 1)
                dve.tensor_tensor(w[:, 1, :, :], w_stage[:, n % WS, :, :], w[:, 0, :, :].bitcast(F32), ALU.subtract)\
                   .then_inc(stage_free, 1)
                dve.drain().then_inc(w_ready, 1)
            with dve.Fori(0, B) as i:
                for k in range(KT):
                    dve.wait_ge(x_hi, i * KT + k + 1)
                    dve.wait_ge(squared, i * KT + k + 1)
                    alone(dve)
                    lo = x[:, 1, k, :]
                    dve.tensor_tensor(lo, lo.bitcast(F32), x[:, 0, k, :].bitcast(F32), ALU.subtract)
                    dve.drain().then_inc(x_ready, 1)
                for step in steps:
                    kind = step[0]
                    if kind == "LG":
                        bank, free = wait_full(dve, i, step)
                        dve.tensor_copy(small[:, 0, :], turned_logits(bank)[:, :, SUM])
                        dve.drain().then_inc(sums_in, 1)
                        dve.wait_ge(roots, i + 1)
                        alone(dve)
                        better_root(small[:, 1, :], small[:, 0, :], small[:, 1, :], small[:, 2, :])
                        dve.reciprocal(small[:, 1, :], small[:, 1, :])
                        dve.drain()
                        dve.tensor_tensor(lg[:, :, :], turned_logits(bank)[:, :, 0:E],
                                          small[:, 1, :].unsqueeze(2).to_broadcast([P, TT, E]), ALU.mult)\
                           .then_inc(free, 1)
                        dve.drain()
                        dve.tensor_tensor(lg[:, :, :], lg[:, :, :], gates[:, :].unsqueeze(1).to_broadcast([P, TT, E]),
                                          ALU.subtract)
                        dve.drain()
                        for t in range(TT):
                            me = lg[:, t, :].unsqueeze(2).to_broadcast([P, E, E])
                            other = lg[:, t, :].unsqueeze(1).to_broadcast([P, E, E])
                            dve.tensor_tensor(beats[:, t, :, :], other, me, ALU.is_equal)
                        dve.drain()
                        for t in range(TT):
                            dve.tensor_tensor(beats[:, t, :, :], beats[:, t, :, :], lower[:, :, :], ALU.mult)
                        dve.drain()
                        dve.tensor_reduce(rw[:, :, :], beats[:, :, :, :], AX.X, ALU.add)
                        dve.drain()
                        for t in range(TT):
                            me = lg[:, t, :].unsqueeze(2).to_broadcast([P, E, E])
                            other = lg[:, t, :].unsqueeze(1).to_broadcast([P, E, E])
                            dve.tensor_tensor(beats[:, t, :, :], other, me, ALU.is_gt)
                        dve.drain()
                        dve.tensor_reduce(pick[:, :, :], beats[:, :, :, :], AX.X, ALU.add)
                        dve.drain()
                        dve.tensor_tensor(rw[:, :, :], rw[:, :, :], pick[:, :, :], ALU.add)
                        dve.drain()
                        dve.tensor_scalar(rw[:, :, :], rw[:, :, :], 2.0, None, ALU.is_lt)
                        dve.tensor_scalar(lg[:, :, :], lg[:, :, :], 0.0, None, ALU.max)
                        dve.drain()
                        dve.tensor_reduce(small[:, 3, :], lg[:, :, :], AX.X, ALU.max)
                        dve.drain()
                        dve.tensor_scalar(small[:, 4, :], small[:, 3, :], 0.0, None, ALU.is_le)
                        dve.drain()
                        top = small[:, 3, :].unsqueeze(2).to_broadcast([P, TT, E])
                        dve.tensor_tensor(rw[:, :, :], rw[:, :, :],
                                          small[:, 4, :].unsqueeze(2).to_broadcast([P, TT, E]), ALU.mult)
                        dve.tensor_tensor(pick[:, :, :], lg[:, :, :], top, ALU.subtract)
                        dve.drain().then_inc(lg_ready, 1)
                        dve.tensor_scalar(lg[:, :, :], lg[:, :, :], 0.0, None, ALU.is_gt)
                        dve.drain()
                        dve.tensor_tensor(rw[:, :, :], rw[:, :, :], lg[:, :, :], ALU.add)
                        dve.drain()
                        dve.wait_ge(exp_ready, i + 1)
                        dve.tensor_tensor(rw[:, :, :], rw[:, :, :], pick[:, :, :], ALU.mult)
                        dve.drain()
                        dve.tensor_reduce(small[:, 5, :], rw[:, :, :], AX.X, ALU.add)
                        dve.drain()
                        dve.reciprocal(small[:, 6, :], small[:, 5, :])
                        dve.drain()
                        dve.tensor_tensor(rw[:, :, :], rw[:, :, :],
                                          small[:, 6, :].unsqueeze(2).to_broadcast([P, TT, E]), ALU.mult)
                        dve.drain()
                    elif kind == "proj":
                        _, w, t = step
                        bank, free = wait_full(dve, i, step)
                        prod = weighted[:, t % 2, :]
                        dve.tensor_tensor(prod.rearrange("p (e d) -> p e d", d=HD),
                                          bank[:, :].rearrange("p (e d) -> p e d", d=HD),
                                          rw[:, t, (w % 2) * 8:(w % 2) * 8 + 8].unsqueeze(2)
                                          .to_broadcast([P, 8, HD]), ALU.mult).then_inc(free, 1)
                        dve.drain()
                        target = qkv[:, w // 2, t, :] if w % 2 == 0 else part[:, :]
                        dve.tensor_reduce(target, prod.rearrange("p (e d) -> p d e", d=HD), AX.X, ALU.add)
                        if w % 2:
                            dve.drain()
                            dve.tensor_tensor(qkv[:, w // 2, t, :], qkv[:, w // 2, t, :], part[:, :], ALU.add)
                            if (w, t) == (5, TT - 1):
                                dve.drain().then_inc(qkv_ready, 1)
                            else:
                                dve.drain()
                    elif kind == "score":
                        _, qt, c = step
                        bank, free = wait_full(dve, i, step)
                        last_half = c == halves(qt)[-1]
                        width = keys(qt, c)
                        if last_half:
                            dve.tensor_tensor(bank[:, width - P:width], bank[:, width - P:width], causal[:, :], ALU.add)
                            dve.drain()
                        dve.tensor_reduce(nmax[:, qt, c:c + 1], bank[:, 0:width], AX.X, ALU.max)
                        if last_half:
                            dve.drain()
                            if c:
                                dve.tensor_tensor(nmax[:, qt, 0:1], nmax[:, qt, 0:1], nmax[:, qt, 1:2], ALU.max)
                                dve.drain()
                            dve.tensor_scalar(nmax[:, qt, 0:1], nmax[:, qt, 0:1], -INV, None, ALU.mult)
                            dve.drain().then_inc(masked_in, 1)
                    elif kind == "pv":
                        qt = step[1]
                        bank, free = wait_full(dve, i, step)
                        dve.wait_ge(prob_ready, i * SC + scored(qt))
                        if len(halves(qt)) == 2:
                            alone(dve)
                            dve.tensor_tensor(rtot[:, qt:qt + 1], total[:, qt, 0:1], total[:, qt, 1:2], ALU.add)
                            dve.drain()
                            dve.reciprocal(rtot[:, qt:qt + 1], rtot[:, qt:qt + 1])
                        else:
                            dve.reciprocal(rtot[:, qt:qt + 1], total[:, qt, 0:1])
                        dve.drain()
                        dve.tensor_scalar(attn[:, :], bank[:, 0:HD], rtot[:, qt:qt + 1], None, ALU.mult)\
                           .then_inc(free, 1)
                        dve.drain()
                        dve.tensor_tensor(mixed[:, :, :], attn[:, :].unsqueeze(1).to_broadcast([P, E, HD]),
                                          rw[:, qt, :].unsqueeze(2).to_broadcast([P, E, HD]), ALU.mult)
                        dve.drain().then_inc(mixed_ready, 1)
                    elif kind == "mixed_t":
                        _, qt, g = step
                        n = use_no[step]
                        dve.wait_ge(hi_ready, (i * TT + qt) * 2 + g + 1)
                        dst = lambda part_: mixed_t[:, part_, g * 4:g * 4 + 4, :].rearrange("p k n -> p (k n)")
                        dve.tensor_tensor(dst(1), bank_of[n % RING][:, :], dst(0).bitcast(F32), ALU.subtract)\
                           .then_inc(work_free[n % RING], 1)
                        dve.drain().then_inc(lo_ready, 1)
                    elif kind == "out":
                        t = step[1]
                        bank, free = wait_full(dve, i, step)
                        if t == 0:
                            dve.wait_ge(res_in, i * 16 + 16)
                            alone(dve)
                        dve.tensor_tensor(y[:, t, :], bank[:, :], y[:, t, :], ALU.add).then_inc(free, 1)
                        dve.drain()
                        dve.bn_stats(stats[:, :], y[:, t, :])
                        dve.drain()
                        dve.bn_aggr(mv[:, t, :], stats[:, :])
                        c = t // (TT - 1)
                        if t == HALF or t == TT - 1:
                            half = slice(c * HALF, (c + 1) * HALF)
                            dve.drain()
                            dve.tensor_scalar(tmp[:, half], mv[:, half, 1], EPS, None, ALU.add).then_inc(var_ready, 1)
                        if t in (HALF + 1, TT - 1):
                            dve.wait_ge(sd_ready, i * NC_ + c + 1)
                            half = slice(c * HALF, (c + 1) * HALF)
                            alone(dve)
                            dve.reciprocal(rstd[:, half], sd[:, half])
                            dve.drain()
                            dve.tensor_tensor(sd[:, half], rstd[:, half], rstd[:, half], ALU.mult)
                            dve.drain()
                            dve.tensor_tensor(sd[:, half], sd[:, half], tmp[:, half], ALU.mult)
                            dve.drain()
                            dve.tensor_scalar(sd[:, half], sd[:, half], -0.5, 1.5, ALU.mult, ALU.add)
                            dve.drain()
                            dve.tensor_tensor(rstd[:, half], rstd[:, half], sd[:, half], ALU.mult)
                            dve.drain()
                        if t > HALF:
                            ready = range((t - HALF - 1) * 2, (t - HALF) * 2) if t < TT - 1 else range(HALF, TT)
                            for q in ready:
                                dve.tensor_scalar(y[:, q, :], y[:, q, :], mv[:, q, 0:1], rstd[:, q:q + 1],
                                                  ALU.subtract, ALU.mult).then_inc(y_ready, 1)


def constants():
    import numpy as np

    eye = np.eye(P, dtype=np.float32)
    sign = np.where(np.arange(P) % DH < DH // 2, 1.0, -1.0).astype(np.float32).reshape(P, 1)
    return {"eye": eye, "neg_eye": -eye, "sign": sign,
            "causal": np.where(np.arange(P)[None, :] > np.arange(P)[:, None], np.float32(-1e30), np.float32(0)),
            "lower": np.tril(np.ones((E, E), np.float32), -1)}


def turned(a, axes):
    import numpy as np

    return np.ascontiguousarray(np.transpose(a, axes))



def program(nc, ins, out):
    scratch = lambda name, shape: nc.dram_tensor(name, shape, F32).ap()
    x1, x1_t = scratch("x1", [B, S, D]), scratch("x1_t", [B, D, S])
    x2, x2_t = scratch("x2", [B, S, D]), scratch("x2_t", [B, D, S])
    attention(nc, False, dict(
        q_src=ins["x_t"], kv_src=ins["x_t"], res=ins["x"], wq=ins["L0_attn_Wi"], wk=ins["L0_attn_Wo"],
        wv=ins["L0_attn_Wv"], wo=ins["L0_attn_Wout"], wo_swapped=ins["Wout_swapped"],
        wo_turned=scratch("wo_turned", [D, D]), wa=ins["L0_attn_Wa"], we=ins["L0_attn_We"], ba=ins["L0_attn_ba"],
        be=ins["L0_attn_be"], beta=ins["L0_attn_beta_p"], iv=ins["L0_attn_iv_p"], ov=ins["L0_attn_ov_p"],
        chi=ins["L0_attn_chi"], out=x1, out_t=x1_t, eye=ins["eye"], neg_eye=ins["neg_eye"],
        sign=ins["sign"]))
    attention(nc, True, dict(
        q_src=x1_t, kv_src=ins["ctx_t"], res=x1, wq=ins["Wq_t"], wk=ins["Wk_t"], wv=ins["Wv_t"], wo=ins["Wo_t"],
        bq=ins["L0_xattn_bq"], bk=ins["L0_xattn_bk"], bv=ins["L0_xattn_bv"], bo=ins["L0_xattn_bo"],
        mask_q=ins["mask"], mask_k=ins["mask_t"], out=x2, out_t=x2_t, eye=ins["eye"], neg_eye=ins["neg_eye"]))
    expert_layer(nc, dict(
        src_t=x2_t, res=x2, sim=ins["L0_ffn_sim_matrix"], gates=ins["L0_ffn_gates"], wq=ins["q_proj_t"],
        wk=ins["k_proj_t"], wv=ins["v_proj_t"], wo=ins["o_proj"], out=out, eye=ins["eye"],
        causal=ins["causal"], lower=ins["lower"]))


def kernel(**inputs):
    import numpy as np
    import concourse.bacc as bacc
    from concourse.bass_utils import run_bass_kernel_spmd

    arrays = {name: np.ascontiguousarray(inputs[name]) for name in (
        "x", "L0_attn_Wa", "L0_attn_ba", "L0_attn_We", "L0_attn_be", "L0_attn_Wi", "L0_attn_Wo", "L0_attn_Wv",
        "L0_attn_Wout", "L0_attn_chi", "L0_attn_beta_p", "L0_attn_iv_p", "L0_attn_ov_p", "L0_xattn_bq",
        "L0_xattn_bk", "L0_xattn_bv", "L0_xattn_bo", "L0_ffn_sim_matrix", "L0_ffn_gates")}
    arrays["x_t"] = turned(inputs["x"], (0, 2, 1))
    arrays["ctx_t"] = turned(inputs["ctx_1024"], (0, 2, 1))
    arrays["mask"] = np.ascontiguousarray(inputs["mask_BxSxS2_ik1"])
    arrays["mask_t"] = turned(inputs["mask_BxSxS2_ik1"], (0, 2, 1))
    for name in ("Wq", "Wk", "Wv", "Wo"):
        arrays[f"{name}_t"] = turned(inputs[f"L0_xattn_{name}"], (1, 0))
    arrays["Wout_swapped"] = np.ascontiguousarray(
        np.asarray(inputs["L0_attn_Wout"]).reshape(H, 2, DH // 2, D)[:, ::-1].reshape(D, D))
    for name in ("q_proj", "k_proj", "v_proj"):
        arrays[f"{name}_t"] = turned(inputs[f"L0_ffn_{name}"], (1, 0, 2)).reshape(D, WIDE)
    arrays["o_proj"] = np.ascontiguousarray(inputs["L0_ffn_o_proj"]).reshape(WIDE, D)
    arrays.update(constants())
    nc = bacc.Bacc("TRN2", target_bir_lowering=False, num_devices=1)
    ins = {name: nc.dram_tensor(name, a.shape, mybir.dt.from_np(a.dtype), kind="ExternalInput").ap()
           for name, a in arrays.items()}
    out = nc.dram_tensor("out", (B, S, D), F32, kind="ExternalOutput").ap()
    program(nc, ins, out)
    result = run_bass_kernel_spmd(nc, [arrays], core_ids=[0])
    return result.results[0]["out"]
```
